# Optimizing a Trainium2 kernel written in Bass

```python
import numpy as np
import jax
import jax.numpy as jnp

def _softmax(x, axis=-1):
    return jax.nn.softmax(x, axis=axis)

def _gelu(x):
    return jax.nn.gelu(x, approximate=True)

def _silu(x):
    return jax.nn.silu(x)

def _sigmoid(x):
    return jax.nn.sigmoid(x)

def _layernorm(x, axis=-1, eps=1e-05):
    m = jnp.mean(x, axis=axis, keepdims=True)
    v = jnp.var(x, axis=axis, keepdims=True)
    return (x - m) / jnp.sqrt(v + eps)

def _scatter_add(tgt, idx, src, axis=0):
    return tgt.at[idx].add(src)

def _segment_sum(src, seg, n):
    return jax.ops.segment_sum(src, seg, n)
kernel_name = 'mk_seq_postln_d2_jaxref_r8_d08b66'

def setup_inputs(seed: int=0):
    np.random.seed(seed)
    _w = jnp.asarray

    def _L0_attn_setup():
        import jax, jax.numpy as jnp
        import numpy as np
        EPS = 1e-15
        HEAD_DIM = 32
        PAD_VAL = 1.0
        key = jax.random.key(seed)
        k1, k2, k3, k4 = jax.random.split(key, 4)
        B, N, C = (2, 512, 256)
        s = 1.0 / np.sqrt(C).astype(np.float32)
        x = jax.random.normal(k1, (B, N, C), jnp.float32)
        w_qkv = jax.random.normal(k2, (3 * C, C), jnp.float32) * s
        w_proj = jax.random.normal(k3, (C, C), jnp.float32) * s
        b_proj = jax.random.normal(k4, (C,), jnp.float32) * 0.01
        return {'x': x, 'w_qkv': w_qkv, 'w_proj': w_proj, 'b_proj': b_proj}
    _L0_attn_in = _L0_attn_setup()

    def _L0_ffn_setup():
        import jax, jax.numpy as jnp
        import numpy as np
        TOP_K = 4
        NUM_EXPERTS = 16
        key = jax.random.key(seed)
        ks = jax.random.split(key, 6)
        B, S, H, I, E = (2, 128, 256, 224, NUM_EXPERTS)
        return {'x': jax.random.normal(ks[0], (B, S, H), dtype=jnp.float32), 'router_w': jax.random.normal(ks[1], (E, H), dtype=jnp.float32) * 0.02, 'expert_bias': jnp.zeros((E,), dtype=jnp.float32), 'gate_proj': jax.random.normal(ks[2], (E, H, I), dtype=jnp.float32) * 0.02, 'up_proj': jax.random.normal(ks[3], (E, H, I), dtype=jnp.float32) * 0.02, 'down_proj': jax.random.normal(ks[4], (E, I, H), dtype=jnp.float32) * 0.02}
    _L0_ffn_in = _L0_ffn_setup()

    def _L1_attn_setup():
        import jax, jax.numpy as jnp
        import numpy as np
        B, S, E, H = (2, 256, 256, 16)
        NOPE, ROPE, VD = (128, 64, 128)
        QH = NOPE + ROPE
        LORA = 64
        ROPE_THETA = 10000.0
        EPS = 1e-06

        def _rope(xp, cos, sin):
            d2 = xp.shape[-1] // 2
            x1, x2 = (xp[..., :d2], xp[..., d2:])
            return jnp.concatenate([x1 * cos - x2 * sin, x2 * cos + x1 * sin], axis=-1)
        key = jax.random.key(seed)
        ks = jax.random.split(key, 5)
        sd = lambda n: 1.0 / np.sqrt(n)
        return {'x': jax.random.normal(ks[0], (B, S, E), jnp.float32), 'wq': jax.random.normal(ks[1], (E, H * QH), jnp.float32) * sd(E), 'wkv_a': jax.random.normal(ks[2], (E, LORA + ROPE), jnp.float32) * sd(E), 'wkv_b': jax.random.normal(ks[3], (LORA, H * (NOPE + VD)), jnp.float32) * sd(LORA), 'wo': jax.random.normal(ks[4], (H * VD, E), jnp.float32) * sd(H * VD), 'kv_norm_scale': jnp.ones((LORA,), jnp.float32)}
    _L1_attn_in = _L1_attn_setup()

    def _L1_ffn_setup():
        import jax, jax.numpy as jnp
        import numpy as np
        DIM = 256
        HID = 704
        ZERO_POINT = 128.0

        def _qlinear(x, wq, scale):
            W = (wq.astype(jnp.float32) - ZERO_POINT) * scale[:, None]
            return jnp.einsum('bsd,hd->bsh', x, W)
        key = jax.random.key(seed)
        ks = jax.random.split(key, 7)
        B, S = (4, 256)
        sg = jax.random.uniform(ks[1], (HID,)) * (0.02 / np.sqrt(DIM)) + 0.0001
        su = jax.random.uniform(ks[3], (HID,)) * (0.02 / np.sqrt(DIM)) + 0.0001
        sd = jax.random.uniform(ks[5], (DIM,)) * (0.02 / np.sqrt(HID)) + 0.0001
        return {'x': jax.random.normal(ks[0], (B, S, DIM), dtype=jnp.float32), 'wq_gate': jax.random.randint(ks[2], (HID, DIM), 0, 32, dtype=jnp.int32), 's_gate': sg, 'wq_up': jax.random.randint(ks[4], (HID, DIM), 0, 32, dtype=jnp.int32), 's_up': su, 'wq_down': jax.random.randint(ks[6], (DIM, HID), 0, 32, dtype=jnp.int32), 's_down': sd}
    _L1_ffn_in = _L1_ffn_setup()
    _d = {'L0_attn_x': _L0_attn_in['x'], 'L0_attn_w_qkv': _L0_attn_in['w_qkv'], 'L0_attn_w_proj': _L0_attn_in['w_proj'], 'L0_attn_b_proj': _L0_attn_in['b_proj'], 'L0_ffn_router_w': _L0_ffn_in['router_w'], 'L0_ffn_expert_bias': _L0_ffn_in['expert_bias'], 'L0_ffn_gate_proj': _L0_ffn_in['gate_proj'], 'L0_ffn_up_proj': _L0_ffn_in['up_proj'], 'L0_ffn_down_proj': _L0_ffn_in['down_proj'], 'L1_attn_wq': _L1_attn_in['wq'], 'L1_attn_wkv_a': _L1_attn_in['wkv_a'], 'L1_attn_wkv_b': _L1_attn_in['wkv_b'], 'L1_attn_wo': _L1_attn_in['wo'], 'L1_attn_kv_norm_scale': _L1_attn_in['kv_norm_scale'], 'L1_ffn_wq_gate': _L1_ffn_in['wq_gate'], 'L1_ffn_s_gate': _L1_ffn_in['s_gate'], 'L1_ffn_wq_up': _L1_ffn_in['wq_up'], 'L1_ffn_s_up': _L1_ffn_in['s_up'], 'L1_ffn_wq_down': _L1_ffn_in['wq_down'], 'L1_ffn_s_down': _L1_ffn_in['s_down']}
    _x0 = _d['L0_attn_x']
    _d['L0_attn_x'] = jax.random.normal(jax.random.fold_in(jax.random.key(seed), 1), (2, 1024, 256), dtype=_x0.dtype)
    del _x0
    return _d

def reference(L0_attn_x, L0_attn_w_qkv, L0_attn_w_proj, L0_attn_b_proj, L0_ffn_router_w, L0_ffn_expert_bias, L0_ffn_gate_proj, L0_ffn_up_proj, L0_ffn_down_proj, L1_attn_wq, L1_attn_wkv_a, L1_attn_wkv_b, L1_attn_wo, L1_attn_kv_norm_scale, L1_ffn_wq_gate, L1_ffn_s_gate, L1_ffn_wq_up, L1_ffn_s_up, L1_ffn_wq_down, L1_ffn_s_down):

    def _L0_attn_ref(x, w_qkv, w_proj, b_proj):
        import jax, jax.numpy as jnp
        import numpy as np
        EPS = 1e-15
        HEAD_DIM = 32
        PAD_VAL = 1.0
        B, N, C = x.shape
        d = HEAD_DIM
        h = C // d
        qkv = (x @ w_qkv.T).reshape(B, N, 3, C)
        q, k, v = (qkv[:, :, 0], qkv[:, :, 1], qkv[:, :, 2])

        def to_heads(t):
            return t.reshape(B, N, h, d).transpose(0, 2, 3, 1)
        q = jax.nn.relu(to_heads(q))
        k = jax.nn.relu(to_heads(k))
        v = to_heads(v)
        v_pad = jnp.pad(v, ((0, 0), (0, 0), (0, 1), (0, 0)), constant_values=PAD_VAL)
        vk = jnp.einsum('bhen,bhdn->bhed', v_pad, k)
        out = jnp.einsum('bhed,bhdn->bhen', vk, q)
        out = out[:, :, :-1] / (out[:, :, -1:] + EPS)
        out = out.reshape(B, C, N).transpose(0, 2, 1)
        return out @ w_proj.T + b_proj

    def _L0_ffn_ref(x, router_w, expert_bias, gate_proj, up_proj, down_proj):
        import jax, jax.numpy as jnp
        import numpy as np
        TOP_K = 4
        NUM_EXPERTS = 16
        logits = jnp.einsum('bsh,eh->bse', x, router_w) + expert_bias
        scores = jax.nn.softmax(logits, axis=-1)
        top_w, top_idx = jax.lax.top_k(scores, TOP_K)
        top_w = top_w / jnp.sum(top_w, axis=-1, keepdims=True)
        g = jnp.einsum('bsh,khe->bske', x, gate_proj)
        u = jnp.einsum('bsh,khe->bske', x, up_proj)
        act = jax.nn.silu(g) * u
        out = jnp.einsum('bske,keh->bskh', act, down_proj)
        sel = jnp.take_along_axis(out, top_idx[..., None], axis=2)
        return jnp.sum(sel * top_w[..., None], axis=2)

    def _L1_attn_ref(x, wq, wkv_a, wkv_b, wo, kv_norm_scale):
        import jax, jax.numpy as jnp
        import numpy as np
        B, S, E, H = (2, 256, 256, 16)
        NOPE, ROPE, VD = (128, 64, 128)
        QH = NOPE + ROPE
        LORA = 64
        ROPE_THETA = 10000.0
        EPS = 1e-06

        def _rope(xp, cos, sin):
            d2 = xp.shape[-1] // 2
            x1, x2 = (xp[..., :d2], xp[..., d2:])
            return jnp.concatenate([x1 * cos - x2 * sin, x2 * cos + x1 * sin], axis=-1)
        b, s, _ = x.shape
        q = (x @ wq).reshape(b, s, H, QH).transpose(0, 2, 1, 3)
        q_nope, q_pe = (q[..., :NOPE], q[..., NOPE:])
        kva = x @ wkv_a
        ckv, k_pe = (kva[..., :LORA], kva[..., LORA:])
        ckv = ckv * jax.lax.rsqrt(jnp.mean(ckv * ckv, axis=-1, keepdims=True) + EPS)
        ckv = ckv * kv_norm_scale
        kv = (ckv @ wkv_b).reshape(b, s, H, NOPE + VD).transpose(0, 2, 1, 3)
        k_nope, v = (kv[..., :NOPE], kv[..., NOPE:])
        pos = jnp.arange(s, dtype=jnp.float32)
        inv = 1.0 / ROPE_THETA ** (jnp.arange(0, ROPE, 2, dtype=jnp.float32) / ROPE)
        ang = pos[:, None] * inv
        cos, sin = (jnp.cos(ang), jnp.sin(ang))
        q_pe = _rope(q_pe, cos, sin)
        k_pe = _rope(k_pe[:, None, :, :], cos, sin)
        qs = jnp.concatenate([q_nope, q_pe], axis=-1)
        ks_ = jnp.concatenate([k_nope, jnp.broadcast_to(k_pe, (b, H, s, ROPE))], axis=-1)
        scale = QH ** (-0.5)
        scores = jnp.einsum('bhqd,bhkd->bhqk', qs, ks_) * scale
        causal = jnp.tril(jnp.ones((s, s), dtype=bool))
        scores = jnp.where(causal, scores, jnp.finfo(scores.dtype).min)
        attn = jax.nn.softmax(scores, axis=-1)
        out = jnp.einsum('bhqk,bhkd->bhqd', attn, v)
        out = out.transpose(0, 2, 1, 3).reshape(b, s, H * VD)
        return out @ wo

    def _L1_ffn_ref(x, wq_gate, s_gate, wq_up, s_up, wq_down, s_down):
        import jax, jax.numpy as jnp
        import numpy as np
        DIM = 256
        HID = 704
        ZERO_POINT = 128.0

        def _qlinear(x, wq, scale):
            W = (wq.astype(jnp.float32) - ZERO_POINT) * scale[:, None]
            return jnp.einsum('bsd,hd->bsh', x, W)
        gate = _qlinear(x, wq_gate, s_gate)
        gate = jax.nn.silu(gate)
        up = _qlinear(x, wq_up, s_up)
        return _qlinear(gate * up, wq_down, s_down)
    x = L0_attn_x
    x = _layernorm(x + _L0_attn_ref(x, L0_attn_w_qkv, L0_attn_w_proj, L0_attn_b_proj), axis=-1)
    x = _layernorm(x + _L0_ffn_ref(x, L0_ffn_router_w, L0_ffn_expert_bias, L0_ffn_gate_proj, L0_ffn_up_proj, L0_ffn_down_proj), axis=-1)
    x = _layernorm(x + _L1_attn_ref(x, L1_attn_wq, L1_attn_wkv_a, L1_attn_wkv_b, L1_attn_wo, L1_attn_kv_norm_scale), axis=-1)
    x = _layernorm(x + _L1_ffn_ref(x, L1_ffn_wq_gate, L1_ffn_s_gate, L1_ffn_wq_up, L1_ffn_s_up, L1_ffn_wq_down, L1_ffn_s_down), axis=-1)
    return x

_drawn_inputs = setup_inputs


def setup_inputs(seed=0):
    import zlib

    import numpy as np

    out = dict(_drawn_inputs(seed))
    spreads = {'L0_ffn_expert_bias': (0.0, 0.8), 'L1_attn_kv_norm_scale': (1.0, 0.2)}
    factors = {'L0_attn_b_proj': 4.906,
     'L0_ffn_router_w': 8.0,
     'L0_ffn_gate_proj': 7.002,
     'L0_ffn_up_proj': 6.913,
     'L0_ffn_down_proj': 6.912,
     'L1_ffn_s_gate': 8.0,
     'L1_ffn_s_up': 8.0,
     'L1_ffn_s_down': 8.0}
    for name, (base, spread) in spreads.items():
        noise = np.random.default_rng([zlib.crc32(name.encode()), seed]).standard_normal(out[name].shape)
        drawn = base * np.exp(spread * noise) if base else spread * noise
        out[name] = jnp.asarray(drawn.astype(out[name].dtype))
    for name, factor in factors.items():
        out[name] = (out[name] * factor).astype(out[name].dtype)
    return out
```

```python
from contextlib import ExitStack

import numpy as np

import concourse.bass as bass
from concourse import mybir

F32 = mybir.dt.float32
BF16 = mybir.dt.bfloat16
I32 = mybir.dt.int32
U32 = mybir.dt.uint32
ALU = mybir.AluOpType
ACT = mybir.ActivationFunctionType
AX_X = mybir.AxisListType.X

P = 128
B, S, C = 2, 1024, 256
T = B * S
NT = T // P
KC = C // P
WIDE = 512
NCH = T // WIDE
EPS_LN = 1e-5

EPS_DEN = 1e-15
HD = 32

E, TOPK, I = 16, 4, 224
IH = I // 2
SLOT_TILES = T * TOPK // P + E
FAR = 2048

H, NOPE, ROPE, VD, LORA = 16, 128, 64, 128, 64
QH = NOPE + ROPE
SCALE = QH ** -0.5
EPS_RMS = 1e-6
QT = S // P
GH = 8
MASKED = -1e30

HID = 704
ZERO_POINT = 128.0
HT = [(n * P, min(P, HID - n * P)) for n in range((HID + P - 1) // P)]


def const_columns():
    at, n = {}, 0
    for name, width in (("ident", P), ("before", P), ("iota", P), ("headmask", P), ("late_q", P), ("late_k", P),
                        ("row", 1), ("eps_ln", 1), ("cos", QT * ROPE), ("sin", QT * ROPE)):
        at[name] = (n, n + width)
        n += width
    return at, n


def const_table():
    at, n = const_columns()
    t = np.zeros((P, n), np.float32)
    p, f = np.arange(P)[:, None], np.arange(P)[None, :]

    def put(name, v):
        t[:, at[name][0]:at[name][1]] = v

    put("ident", p == f)
    put("before", p < f)
    put("iota", np.broadcast_to(f, (P, P)))
    put("headmask", p // HD == f // HD)
    put("late_q", np.where(p > f, MASKED, 0.0))
    put("late_k", np.where(f > p, MASKED, 0.0))
    put("row", p)
    put("eps_ln", EPS_LN)
    half = ROPE // 2
    inv = (np.float32(1.0) / np.float32(10000.0) ** (np.arange(0, ROPE, 2, dtype=np.float32) / np.float32(ROPE)))
    ang = np.arange(S, dtype=np.float32)[:, None] * inv.astype(np.float32)
    cos, sin = np.cos(ang), np.sin(ang)
    lay = lambda a: a.reshape(QT, P, ROPE).transpose(1, 0, 2).reshape(P, QT * ROPE)
    put("cos", lay(np.concatenate([cos, cos], 1)))
    put("sin", lay(np.concatenate([-sin, sin], 1)))
    return t


class Memory:

    def __init__(self, nc, name):
        self.nc, self.name, self.stack, self.sems = nc, name, ExitStack(), []

    def __enter__(self):
        return self

    def __exit__(self, *a):
        if self.sems and a[0] is None:
            self.nc.clear_and_free_semaphores(self.sems)
            self.nc.all_engine_barrier(sem_only=True)
        return self.stack.__exit__(*a)

    def sb(self, name, shape, dt=F32):
        return self.stack.enter_context(self.nc.sbuf_tensor(f"{self.name}_{name}", shape, dt))

    def ps(self, name, shape, dt=F32):
        return self.stack.enter_context(self.nc.psum_tensor(f"{self.name}_{name}", shape, dt))

    def sem(self, name):
        self.sems.append(self.nc.alloc_semaphore(f"{self.name}_{name}"))
        return self.sems[-1]


class Count:

    def __init__(self, sem, engine):
        self.sem, self.engine, self.n = sem, engine, 0

    def up(self, ins):
        ins.then_inc(self.sem, 1)
        self.n += 1

    def settle(self):
        self.engine.wait_ge(self.sem, self.n)


def phase_linear_attention(nc, bank, cst, x_tok, xT, z, x_in, xT_in, wqkvT_in, wprojT_in, bproj_in):
    with Memory(nc, "lin") as m:
        wqkvT = m.sb("wqkvT", [P, KC, 3 * C])
        wprojT = m.sb("wprojT", [P, KC, C])
        bproj = m.sb("bproj", [P, C])
        kmat = m.sb("kmat", [P, NT, C])
        vones = m.sb("vones", [P, NT, KC, P + 1])
        qT = m.sb("qT0", [P, KC, T])
        aT = m.sb("aT", [P, KC, T])
        vk_num = m.sb("vk_num", [P, B * KC, P])
        vk_den = m.sb("vk_den", [P, B * KC, P])
        den = m.sb("den", [P, 2, WIDE])
        rec = m.sb("rec", [P, 2, WIDE])
        loaded, loaded_x = m.sem("loaded"), m.sem("loaded_x")
        kv_mm, k_sb, v_sb, q_mm, q_sb = (m.sem(n) for n in ("kv_mm", "k_sb", "v_sb", "q_mm", "q_sb"))
        vk_mm, vk_sb, nd_mm, den_sb, rec_sb, a_sb = (m.sem(n) for n in ("vk_mm", "vk_sb", "nd_mm", "den_sb", "rec_sb", "a_sb"))
        y_mm, z_sb, xb_sb, ones_sb = (m.sem(n) for n in ("y_mm", "z_sb", "xb_sb", "ones_sb"))
        kv_ps = [bank[:, n, :] for n in (0, 1)]
        q_ps = [bank[:, n, :] for n in (2, 3)]
        vk_ps = [bank[:, n, :] for n in (4, 5)]
        num_ps = [bank[:, n, :] for n in (0, 1)]
        den_ps = [bank[:, n, :] for n in (2, 3)]
        y_ps = [bank[:, n, :] for n in (6, 7)]
        cols = [(b, g, ch) for b in range(B) for g in range(KC) for ch in range(S // WIDE)]

        with nc.Block() as block:
            @block.sync
            def _(sp):
                sp.dma_start(wqkvT[:], wqkvT_in.rearrange("(k p) n -> p k n", p=P)).then_inc(loaded, 16)
                for k in range(KC):
                    sp.dma_start(xT[:, k, :], xT_in[k * P:(k + 1) * P, :]).then_inc(loaded, 16)
                sp.dma_start(wprojT[:], wprojT_in.rearrange("(k p) n -> p k n", p=P)).then_inc(loaded, 16)
                sp.dma_start(x_tok[:], x_in.rearrange("(t p) c -> p t c", p=P)).then_inc(loaded_x, 16)
                sp.dma_start(bproj[:], bproj_in.partition_broadcast(P)).then_inc(loaded_x, 16)

            @block.gpsimd
            def _(pool):
                nc.gpsimd.memset(vones[:, :, :, P:P + 1], 1.0).then_inc(ones_sb, 1)
                pool.wait_ge(loaded_x, 32)
                nc.gpsimd.tensor_tensor(x_tok[:], x_tok[:], bproj[:].unsqueeze(1).to_broadcast([P, NT, C]),
                                        ALU.add).then_inc(xb_sb, 1)

            @block.tensor
            def _(pe):
                pe.wait_ge(loaded, 16 * (KC + 2))
                for t in range(NT):
                    if t >= 2:
                        pe.wait_ge(k_sb, t - 1)
                        pe.wait_ge(v_sb, t - 1)
                    for k in range(KC):
                        mm = nc.tensor.matmul(kv_ps[t % 2], xT[:, k, t * P:(t + 1) * P], wqkvT[:, k, C:3 * C],
                                              start=k == 0, stop=k == KC - 1)
                    mm.then_inc(kv_mm, 1)
                for n in range(KC * NCH):
                    g, ch = divmod(n, NCH)
                    if n >= 2:
                        pe.wait_ge(q_sb, n - 1)
                    for k in range(KC):
                        mm = nc.tensor.matmul(q_ps[n % 2], wqkvT[:, k, g * P:(g + 1) * P],
                                              xT[:, k, ch * WIDE:(ch + 1) * WIDE], start=k == 0, stop=k == KC - 1)
                    mm.then_inc(q_mm, 1)
                pe.wait_ge(k_sb, NT)
                pe.wait_ge(v_sb, NT)
                pe.wait_ge(ones_sb, 1)
                for n in range(B * KC):
                    b, g = divmod(n, KC)
                    if n >= 2:
                        pe.wait_ge(vk_sb, 2 * (n - 1))
                    for i in range(QT):
                        t = b * QT + i
                        mm = nc.tensor.matmul(vk_ps[n % 2][:, 0:P + 1], kmat[:, t, g * P:(g + 1) * P],
                                              vones[:, t, g, :], start=i == 0, stop=i == QT - 1)
                    mm.then_inc(vk_mm, 1)
                pe.wait_ge(q_sb, KC * NCH)
                for n, (b, g, ch) in enumerate(cols):
                    pe.wait_ge(vk_sb, 2 * (b * KC + g + 1))
                    if n >= 2:
                        pe.wait_ge(a_sb, n - 1)
                    rhs = qT[:, g, b * S + ch * WIDE:b * S + (ch + 1) * WIDE]
                    nc.tensor.matmul(num_ps[n % 2], vk_num[:, b * KC + g, :], rhs, start=True, stop=True)
                    nc.tensor.matmul(den_ps[n % 2], vk_den[:, b * KC + g, :], rhs, start=True, stop=True).then_inc(nd_mm, 1)
                for t in range(NT):
                    if t % QT == 0:
                        pe.wait_ge(a_sb, len(cols) // B * (t // QT + 1))
                    if t >= 2:
                        pe.wait_ge(z_sb, t - 1)
                    for k in range(KC):
                        mm = nc.tensor.matmul(y_ps[t % 2][:, 0:C], aT[:, k, t * P:(t + 1) * P], wprojT[:, k, :],
                                              start=k == 0, stop=k == KC - 1)
                    mm.then_inc(y_mm, 1)

            @block.scalar
            def _(act):
                for t in range(NT):
                    act.wait_ge(kv_mm, t + 1)
                    nc.scalar.activation(kmat[:, t, :], kv_ps[t % 2][:, 0:C], ACT.Relu).then_inc(k_sb, 1)
                for n in range(KC * NCH):
                    g, ch = divmod(n, NCH)
                    act.wait_ge(q_mm, n + 1)
                    nc.scalar.activation(qT[:, g, ch * WIDE:(ch + 1) * WIDE], q_ps[n % 2], ACT.Relu).then_inc(q_sb, 1)

            @block.vector
            def _(dve):
                for t in range(NT):
                    dve.wait_ge(kv_mm, t + 1)
                    dve.wait_ge(k_sb, t + 1)
                    nc.vector.tensor_copy(vones[:, t, :, 0:P],
                                          kv_ps[t % 2][:, C:2 * C].rearrange("p (g c) -> p g c", g=KC)).then_inc(v_sb, 1)
                for n in range(B * KC):
                    dve.wait_ge(vk_mm, n + 1)
                    mask = cst["headmask"]
                    nc.vector.tensor_tensor(vk_num[:, n, :], vk_ps[n % 2][:, 0:P], mask, ALU.mult).then_inc(vk_sb, 1)
                    nc.vector.tensor_scalar(vk_den[:, n, :], mask, vk_ps[n % 2][:, P:P + 1], None,
                                            ALU.mult).then_inc(vk_sb, 1)
                for n, (b, g, ch) in enumerate(cols):
                    dve.wait_ge(nd_mm, n + 1)
                    nc.vector.tensor_scalar(den[:, n % 2, :], den_ps[n % 2], EPS_DEN, None, ALU.add).then_inc(den_sb, 1)
                    dve.wait_ge(den_sb, n + 1)
                    nc.vector.reciprocal(rec[:, n % 2, :], den[:, n % 2, :]).then_inc(rec_sb, 1)
                    dve.wait_ge(rec_sb, n + 1)
                    nc.vector.tensor_tensor(aT[:, g, b * S + ch * WIDE:b * S + (ch + 1) * WIDE], num_ps[n % 2],
                                            rec[:, n % 2, :], ALU.mult).then_inc(a_sb, 1)
                dve.wait_ge(xb_sb, 1)
                for t in range(NT):
                    dve.wait_ge(y_mm, t + 1)
                    nc.vector.tensor_tensor(z[:, t, :], y_ps[t % 2][:, 0:C], x_tok[:, t, :], ALU.add).then_inc(z_sb, 1)


def phase_layernorm(nc, name, bank, cst, z, x_tok, xT, rows_out):
    with Memory(nc, name) as m:
        stats = m.sb("ln_stats", [P, NT, 6])
        meanvar = m.sb("ln_meanvar", [P, NT, 2])
        vareps = m.sb("ln_vareps", [P, NT])
        power = m.sb("ln_power", [P, NT])
        rstd = m.sb("ln_rstd", [P, NT])
        power_sb, stats_sb, mv_sb, ve_sb, rstd_sb = (m.sem(n) for n in ("power_sb", "stats_sb", "mv_sb", "ve_sb", "rstd_sb"))
        x_sb, xT_mm, xT_sb, stored = (m.sem(n) for n in ("x_sb", "xT_mm", "xT_sb", "stored"))
        GT = 4
        with nc.Block() as block:
            @block.gpsimd
            def _(pool):
                nc.gpsimd.memset(power[:], -0.5).then_inc(power_sb, 1)
                for g in range(NT // GT):
                    sl = slice(g * GT, (g + 1) * GT)
                    pool.wait_ge(mv_sb, (g + 1) * GT)
                    nc.gpsimd.tensor_scalar(vareps[:, sl], meanvar[:, sl, 1], EPS_LN, None, ALU.add).then_inc(ve_sb, 1)
                    pool.wait_ge(ve_sb, g + 1)
                    pool.wait_ge(power_sb, 1)
                    nc.gpsimd.tensor_tensor(rstd[:, sl], vareps[:, sl], power[:, sl], ALU.pow).then_inc(rstd_sb, 1)

            @block.vector
            def _(dve):
                for g in range(NT // GT + 1):
                    if g < NT // GT:
                        for t in range(g * GT, (g + 1) * GT):
                            nc.vector.bn_stats(stats[:, t, :], z[:, t, :]).then_inc(stats_sb, 1)
                        for t in range(g * GT, (g + 1) * GT):
                            dve.wait_ge(stats_sb, t + 1)
                            nc.vector.bn_aggr(meanvar[:, t, :], stats[:, t, :]).then_inc(mv_sb, 1)
                    if g:
                        dve.wait_ge(rstd_sb, g)
                        for t in range((g - 1) * GT, g * GT):
                            nc.vector.tensor_scalar(x_tok[:, t, :], z[:, t, :], meanvar[:, t, 0:1], rstd[:, t:t + 1],
                                                    ALU.subtract, ALU.mult).then_inc(x_sb, 1)

            @block.tensor
            def _(pe):
                if xT is None:
                    return
                for g in range(NT // GT):
                    for k in range(KC):
                        n = g * KC + k
                        if n >= 4:
                            pe.wait_ge(xT_sb, n - 3)
                        for i in range(GT):
                            t = g * GT + i
                            pe.wait_ge(x_sb, t + 1)
                            mm = nc.tensor.transpose(bank[:, n % 4, i * P:(i + 1) * P], x_tok[:, t, k * P:(k + 1) * P],
                                                     cst["ident"])
                        mm.then_inc(xT_mm, 1)

            @block.scalar
            def _(act):
                if xT is None:
                    return
                for n in range(NT // GT * KC):
                    g, k = divmod(n, KC)
                    act.wait_ge(xT_mm, n + 1)
                    nc.scalar.copy(xT[:, k, g * WIDE:(g + 1) * WIDE], bank[:, n % 4, :]).then_inc(xT_sb, 1)

            @block.sync
            def _(sp):
                for g in range(NT // GT):
                    sp.wait_ge(x_sb, (g + 1) * GT)
                    for r in rows_out:
                        sp.dma_start(r[0:T, :].rearrange("(t p) c -> p t c", p=P)[:, g * GT:(g + 1) * GT, :],
                                     x_tok[:, g * GT:(g + 1) * GT, :]).then_inc(stored, 16)
                if rows_out:
                    sp.wait_ge(stored, 16 * len(rows_out) * (NT // GT))


def phase_route(nc, bank, cst, xT, routerT_in, bias_in, slot_row, slot_far, slot_w, tile_expert):
    N = NT * E
    ST = SLOT_TILES
    with Memory(nc, "route") as m:
        routerT = m.sb("routerT", [P, KC, E])
        bias = m.sb("bias", [P, E])
        logit = m.sb("logit", [P, NT, E])
        top = m.sb("top", [P, NT, 8])
        shifted = m.sb("shifted", [P, NT, E])
        expo = m.sb("expo", [P, NT, E])
        above = m.sb("above", [P, NT, E])
        tie = m.sb("tie", [P, NT, E])
        n_above = m.sb("n_above", [P, NT])
        room = m.sb("room", [P, NT])
        ones = m.sb("ones", [P, N])
        ties_so_far = m.sb("ties_so_far", [P, 1 + N])
        tie_rank = m.sb("tie_rank", [P, NT, E])
        fits = m.sb("fits", [P, NT, E])
        chosen = m.sb("chosen", [P, NT, E])
        picked = m.sb("picked", [P, NT, E])
        total = m.sb("total", [P, NT])
        rtotal = m.sb("rtotal", [P, NT])
        weight = m.sb("weight", [P, NT, E])
        earlier = m.sb("earlier", [P, NT + 1, E])
        up = m.sb("up", [P, E], I32)
        tiles_i = m.sb("tiles_i", [P, E], I32)
        tiles = m.sb("tiles", [P, E])
        tiles_end = m.sb("tiles_end", [P, E])
        start = m.sb("start", [P, E])
        place_a = m.sb("place_a", [P, NT, E])
        place_b = m.sb("place_b", [P, NT, E])
        key = m.sb("key", [P, NT, E])
        key4 = m.sb("key4", [P, NT, 8])
        match = m.sb("match", [P, TOPK, NT, E])
        match_w = m.sb("match_w", [P, TOPK, NT, E])
        w4 = m.sb("w4", [P, NT, TOPK])
        place_i = m.sb("place_i", [P, NT, TOPK], I32)
        lo_i = m.sb("lo_i", [P, NT, TOPK], I32)
        hi_i = m.sb("hi_i", [P, NT, TOPK], I32)
        lo = m.sb("lo", [P, NT * TOPK])
        hi = m.sb("hi", [P, NT * TOPK])
        is_lo = m.sb("is_lo", [P, 4, P])
        is_hi = m.sb("is_hi", [P, 4, 2, ST])
        token1 = m.sb("token1", [P, NT])
        filled = m.sb("filled", [P, ST])
        far = m.sb("far", [P, 1])
        slot_f = m.sb("slot_f", [P, ST])
        slot_e = m.sb("slot_e", [P, ST])
        slot_g = m.sb("slot_g", [P, ST])
        ends = m.sb("ends", [1, ST, E])
        n_ends = m.sb("n_ends", [1, ST])
        loaded, logit_mm, scalar_sb, dve_sb, count_mm, hot_sb, token_sb, slot_mm = (
            m.sem(n) for n in ("loaded", "logit_mm", "scalar_sb", "dve_sb", "count_mm", "hot_sb", "token_sb", "slot_mm"))
        expo_sb, shifted_sb, chosen_sb, spread_sb = (m.sem(n) for n in ("expo_sb", "shifted_sb", "chosen_sb", "spread_sb"))
        logit_ps = bank[:, 0, 0:N]
        rank_ps = bank[:, 1, 0:N]
        tally_ps = bank[:, 2, 0:N]
        slot_ps = bank[:, 3, 0:2 * ST]
        by_e = lambda a: a.rearrange("p (t e) -> p t e", e=E)
        over_e = lambda a: a.unsqueeze(2).to_broadcast([P, NT, E])

        with nc.Block() as block:
            @block.sync
            def _(sp):
                sp.dma_start(routerT[:], routerT_in.rearrange("(k p) e -> p k e", p=P)).then_inc(loaded, 16)
                sp.dma_start(bias[:], bias_in.partition_broadcast(P)).then_inc(loaded, 16)

            @block.tensor
            def _(pe):
                pe.wait_ge(loaded, 32)
                for t in range(NT):
                    for k in range(KC):
                        mm = nc.tensor.matmul(logit_ps[:, t * E:(t + 1) * E], xT[:, k, t * P:(t + 1) * P], routerT[:, k, :],
                                              start=k == 0, stop=k == KC - 1)
                mm.then_inc(logit_mm, 1)
                pe.wait_ge(chosen_sb, 1)
                flat = chosen[:].rearrange("p t e -> p (t e)")
                nc.tensor.matmul(rank_ps, cst["before"], flat, start=True, stop=True)
                nc.tensor.matmul(tally_ps, ones[:, 0:P], flat, start=True, stop=True).then_inc(count_mm, 1)
                for n in range(NT * TOPK):
                    pe.wait_ge(hot_sb, n + 1)
                    pe.wait_ge(token_sb, 2 * (n + 1))
                    nc.tensor.matmul(slot_ps, is_lo[:, n % 4, :], is_hi[:, n % 4].rearrange("p a s -> p (a s)"),
                                     start=n == 0, stop=n == NT * TOPK - 1).then_inc(slot_mm, 1)

            @block.scalar
            def _(act):
                act.wait_ge(shifted_sb, 1)
                nc.scalar.activation(expo[:], shifted[:], ACT.Exp).then_inc(expo_sb, 1)

            @block.gpsimd
            def _(pool):
                token = Count(spread_sb, pool)
                token.up(nc.gpsimd.iota(slot_g[:, 0:NT], pattern=[[P, NT]], base=1, channel_multiplier=1,
                                        allow_small_or_imprecise_dtypes=True))
                token.settle()
                token.up(nc.gpsimd.tensor_copy(token1[:], slot_g[:, 0:NT]))

            @block.vector
            def _(dve):
                step = Count(dve_sb, dve)
                v = nc.vector
                step.up(v.memset(ones[:], 1.0))
                step.up(v.memset(ties_so_far[:, 0:1], 0.0))
                step.up(v.memset(earlier[:, 0, :], 0.0))
                dve.wait_ge(loaded, 32)
                dve.wait_ge(logit_mm, 1)
                step.up(v.tensor_tensor(logit[:], by_e(logit_ps), bias[:].unsqueeze(1).to_broadcast([P, NT, E]), ALU.add))
                step.settle()
                for t in range(NT):
                    step.up(v.max(top[:, t, :], logit[:, t, :]))
                step.settle()
                v.tensor_tensor(shifted[:], logit[:], over_e(top[:, :, 0]), ALU.subtract).then_inc(shifted_sb, 1)
                fourth = over_e(top[:, :, TOPK - 1])
                step.up(v.tensor_tensor(above[:], logit[:], fourth, ALU.is_gt))
                step.up(v.tensor_tensor(tie[:], logit[:], fourth, ALU.is_equal))
                step.settle()
                step.up(v.tensor_reduce(n_above[:], above[:], AX_X, ALU.add))
                step.up(v.tensor_tensor_scan(ties_so_far[:, 1:1 + N], ones[:], tie[:].rearrange("p t e -> p (t e)"), 0.0,
                                             ALU.mult, ALU.add))
                step.settle()
                step.up(v.tensor_scalar(room[:], n_above[:], -1.0, float(TOPK), ALU.mult, ALU.add))
                step.up(v.tensor_tensor(tie_rank[:], by_e(ties_so_far[:, 1:1 + N]), over_e(by_e(ties_so_far[:, 0:N])[:, :, 0]),
                                        ALU.subtract))
                step.settle()
                step.up(v.tensor_tensor(fits[:], tie_rank[:], over_e(room[:]), ALU.is_le))
                step.settle()
                step.up(v.tensor_tensor(picked[:], fits[:], tie[:], ALU.mult))
                step.settle()
                v.tensor_tensor(chosen[:], picked[:], above[:], ALU.add).then_inc(chosen_sb, 1)
                dve.wait_ge(chosen_sb, 1)
                dve.wait_ge(expo_sb, 1)
                step.up(v.tensor_tensor(fits[:], expo[:], chosen[:], ALU.mult))
                step.settle()
                step.up(v.tensor_reduce(total[:], fits[:], AX_X, ALU.add))
                step.settle()
                step.up(v.reciprocal(rtotal[:], total[:]))
                step.settle()
                step.up(v.tensor_tensor(weight[:], fits[:], over_e(rtotal[:]), ALU.mult))
                dve.wait_ge(count_mm, 1)
                for t in range(NT):
                    step.settle()
                    step.up(v.tensor_tensor(earlier[:, t + 1, :], tally_ps[:, t * E:(t + 1) * E], earlier[:, t, :], ALU.add))
                step.settle()
                step.up(v.tensor_scalar(up[:], earlier[:, NT, :], float(P - 1), None, ALU.add))
                step.settle()
                step.up(v.tensor_scalar(tiles_i[:], up[:], 7, None, ALU.arith_shift_right))
                step.settle()
                step.up(v.tensor_copy(tiles[:], tiles_i[:]))
                step.settle()
                step.up(v.tensor_tensor_scan(tiles_end[:], ones[:, 0:E], tiles[:], 0.0, ALU.mult, ALU.add))
                step.settle()
                step.up(v.tensor_tensor(start[:], tiles_end[:], tiles[:], ALU.subtract))
                step.settle()
                step.up(v.tensor_scalar(start[:], start[:], float(P), 1.0, ALU.mult, ALU.add))
                step.up(v.tensor_tensor(place_a[:], by_e(rank_ps), earlier[:, 0:NT, :], ALU.add))
                step.settle()
                step.up(v.tensor_tensor(place_b[:], place_a[:], start[:].unsqueeze(1).to_broadcast([P, NT, E]), ALU.add))
                step.settle()
                step.up(v.tensor_tensor(key[:], place_b[:], chosen[:], ALU.mult))
                step.settle()
                for t in range(NT):
                    step.up(v.max(key4[:, t, :], key[:, t, :]))
                step.settle()
                for k in range(TOPK):
                    step.up(v.tensor_tensor(match[:, k], key[:], over_e(key4[:, :, k]), ALU.is_equal))
                step.up(v.tensor_scalar(place_i[:], key4[:, :, 0:TOPK], -1.0, None, ALU.add))
                step.settle()
                step.up(v.tensor_scalar(lo_i[:], place_i[:], P - 1, None, ALU.bitwise_and))
                step.up(v.tensor_scalar(hi_i[:], place_i[:], 7, None, ALU.arith_shift_right))
                for k in range(TOPK):
                    step.up(v.tensor_tensor(match_w[:, k], match[:, k], weight[:], ALU.mult))
                step.settle()
                step.up(v.tensor_copy(lo[:], lo_i[:].rearrange("p t k -> p (t k)")))
                step.up(v.tensor_copy(hi[:], hi_i[:].rearrange("p t k -> p (t k)")))
                for k in range(TOPK):
                    step.up(v.tensor_reduce(w4[:, :, k], match_w[:, k], AX_X, ALU.add))
                step.up(v.tensor_tensor(ends[:], cst["iota"][0:1, 0:ST].unsqueeze(2).to_broadcast([1, ST, E]),
                                        tiles_end[0:1, :].unsqueeze(1).to_broadcast([1, ST, E]), ALU.is_ge))
                step.settle()
                step.up(v.tensor_reduce(n_ends[:], ends[:], AX_X, ALU.add))
                step.settle()
                step.up(v.tensor_scalar(tile_expert[:], n_ends[:], float(E - 1), None, ALU.min))
                dve.wait_ge(spread_sb, 2)
                for n in range(NT * TOPK):
                    t, k = divmod(n, TOPK)
                    if n >= 4:
                        dve.wait_ge(slot_mm, n - 3)
                    v.tensor_scalar(is_lo[:, n % 4, :], cst["iota"], lo[:, n:n + 1], None, ALU.is_equal).then_inc(hot_sb, 1)
                    v.tensor_scalar(is_hi[:, n % 4, 0, :], cst["iota"][:, 0:ST], hi[:, n:n + 1], token1[:, t:t + 1],
                                    ALU.is_equal, ALU.mult).then_inc(token_sb, 1)
                    v.tensor_scalar(is_hi[:, n % 4, 1, :], cst["iota"][:, 0:ST], hi[:, n:n + 1], w4[:, t, k:k + 1],
                                    ALU.is_equal, ALU.mult).then_inc(token_sb, 1)
                dve.wait_ge(slot_mm, NT * TOPK)
                step.up(v.tensor_copy(slot_w[:], slot_ps[:, ST:2 * ST]))
                step.up(v.tensor_scalar(slot_f[:], slot_ps[:, 0:ST], -1.0, None, ALU.add))
                step.up(v.tensor_scalar(filled[:], slot_ps[:, 0:ST], 0.5, None, ALU.is_lt))
                step.up(v.tensor_scalar(far[:], cst["row"], float(FAR + 1), None, ALU.add))
                step.settle()
                step.up(v.tensor_scalar(slot_row[:], slot_f[:], 0.0, None, ALU.max))
                step.up(v.tensor_scalar(slot_e[:], filled[:], far[:, 0:1], None, ALU.mult))
                step.settle()
                step.up(v.tensor_tensor(slot_far[:], slot_f[:], slot_e[:], ALU.add))


def phase_experts(nc, bank, cst, w_gu, w_down, weights_loaded, weights_need, x_rows, sums, slot_row, slot_far, slot_w,
                  tile_expert):
    with Memory(nc, "moe") as m:
        row_at = m.sb("row_at", [P, 2], I32)
        far_at = m.sb("far_at", [P, 2], I32)
        xg = m.sb("xg", [P, 2, C])
        xgT = m.sb("xgT", [P, 2, KC, P])
        gate = m.sb("gate", [P, 2, I])
        hid = m.sb("hid", [P, 2, I])
        hidT = m.sb("hidT", [IH, 2, 2, P])
        y = m.sb("y", [P, 2, C])
        names = ("row_sb", "xT_mm", "xT_sb", "gu_mm", "gate_sb", "hid_sb", "hidT_mm", "hidT_sb", "y_mm", "y_sb", "far_sb")
        row_sb, xT_mm, xT_sb, gu_mm, gate_sb, hid_sb, hidT_mm, hidT_sb, y_mm, y_sb, far_sb = (m.sem(n) for n in names)
        go = m.sem("go")
        gathered = [m.sem(f"gathered{s}") for s in range(2)]
        added = [m.sem(f"added{s}") for s in range(2)]
        xT_ps = [bank[:, s, 0:KC * P] for s in range(2)]
        gu_ps = [bank[:, 2 + s, 0:2 * I] for s in range(2)]
        hidT_ps = [bank[0:IH, 4 + s, 0:2 * P] for s in range(2)]
        y_ps = [bank[:, 6 + s, 0:C] for s in range(2)]
        ST = SLOT_TILES

        FIRST = 4

        def run(engine, step):
            for r in range(FIRST):
                step(0, r)
            with engine.Fori(0, (ST - FIRST - 2) // 2) as u:
                step(u, FIRST)
                step(u, FIRST + 1)
            step(0, ST - 2)
            step(0, ST - 1)

        def wait(engine, sem, u, r, more):
            if r + more > 0:
                engine.wait_ge(sem, u * 2 + (r + more))

        def wait_dma(engine, sems, u, r, more):
            if r // 2 + more > 0:
                engine.wait_ge(sems[r % 2], u * 16 + 16 * (r // 2 + more))

        with nc.Block() as block:
            @block.gpsimd
            def _(pool):
                last_row, last_far = pool.to_reg(T - 1), pool.to_reg(FAR + P - 1)

                def gather(u, r):
                    s = r % 2
                    wait(pool, xT_mm, u, r, -1)
                    nc.gpsimd.tensor_copy(row_at[:, s:s + 1], slot_row[:, bass.ds(u * 2 + r, 1)]).then_inc(row_sb, 1)
                    wait(pool, row_sb, u, r, 1)
                    pool.sem_inc(go, 1)
                    nc.gpsimd.indirect_dma_start(xg[:, s, :], None, x_rows,
                                                 bass.IndirectOffsetOnAxis(row_at[:, s:s + 1], 0),
                                                 bounds_check=last_row).then_inc(gathered[s], 16)

                def scatter(u, r):
                    s = r % 2
                    wait_dma(pool, added, u, r, 0)
                    nc.gpsimd.tensor_copy(far_at[:, s:s + 1], slot_far[:, bass.ds(u * 2 + r, 1)]).then_inc(far_sb, 1)
                    wait(pool, far_sb, u, r, 1)
                    wait(pool, y_sb, u, r, 1)
                    pool.sem_inc(go, 1)
                    nc.gpsimd.indirect_dma_start(sums[s], bass.IndirectOffsetOnAxis(far_at[:, s:s + 1], 0), y[:, s, :], None,
                                                 bounds_check=last_far, compute_op=ALU.add).then_inc(added[s], 16)

                def step(u, r):
                    if r + 2 < ST:
                        gather(u, r + 2)
                    if r >= 1:
                        scatter(u, r - 1)

                gather(0, 0)
                gather(0, 1)
                run(pool, step)
                scatter(0, ST - 1)
                for s in range(2):
                    pool.wait_ge(added[s], 16 * (ST // 2))

            @block.tensor
            def _(pe):
                def turn_x(u, r):
                    s = r % 2
                    wait_dma(pe, gathered, u, r, 1)
                    wait(pe, xT_sb, u, r, -1)
                    for k in range(KC):
                        mm = nc.tensor.transpose(xT_ps[s][:, k * P:(k + 1) * P], xg[:, s, k * P:(k + 1) * P], cst["ident"])
                    mm.then_inc(xT_mm, 1)

                def expert_of(u, r):
                    return pe.value_load(tile_expert[0:1, bass.ds(u * 2 + r, 1)], min_val=0, max_val=E - 1)

                def gate_up(u, r):
                    s = r % 2
                    e = expert_of(u, r)
                    wait(pe, xT_sb, u, r, 1)
                    wait(pe, hid_sb, u, r, -1)
                    for k in range(KC):
                        mm = nc.tensor.matmul(gu_ps[s], xgT[:, s, k, :], w_gu[:, bass.ds(e * (KC * 2 * I) + k * 2 * I, 2 * I)],
                                              start=k == 0, stop=k == KC - 1)
                    mm.then_inc(gu_mm, 1)

                def turn_hid(u, r):
                    s = r % 2
                    wait(pe, hid_sb, u, r, 1)
                    wait(pe, hidT_sb, u, r, -1)
                    for k in range(2):
                        mm = nc.tensor.transpose(hidT_ps[s][:, k * P:(k + 1) * P], hid[:, s, k * IH:(k + 1) * IH], cst["ident"])
                    mm.then_inc(hidT_mm, 1)

                def down(u, r):
                    s = r % 2
                    e = expert_of(u, r)
                    wait(pe, hidT_sb, u, r, 1)
                    wait(pe, y_sb, u, r, -1)
                    for k in range(2):
                        mm = nc.tensor.matmul(y_ps[s], hidT[:, s, k, :], w_down[:, bass.ds(e * 2 * C + k * C, C)],
                                              start=k == 0, stop=k == 1)
                    mm.then_inc(y_mm, 1)

                def step(u, r):
                    if r >= 1:
                        turn_hid(u, r - 1)
                    gate_up(u, r)
                    if r + 1 < ST:
                        turn_x(u, r + 1)
                    if r >= 1:
                        down(u, r - 1)

                pe.wait_ge(weights_loaded, weights_need)
                turn_x(0, 0)
                run(pe, step)
                turn_hid(0, ST - 1)
                down(0, ST - 1)

            @block.scalar
            def _(act):
                def copy_x(u, r):
                    s = r % 2
                    wait(act, xT_mm, u, r, 1)
                    wait(act, gu_mm, u, r, -1)
                    nc.scalar.copy(xgT[:, s].rearrange("p k m -> p (k m)"), xT_ps[s]).then_inc(xT_sb, 1)

                def silu(u, r):
                    s = r % 2
                    wait(act, gu_mm, u, r, 1)
                    wait(act, hid_sb, u, r, -1)
                    nc.scalar.activation(gate[:, s, :], gu_ps[s][:, 0:I], ACT.Silu).then_inc(gate_sb, 1)

                def copy_y(u, r):
                    s = r % 2
                    wait(act, y_mm, u, r, 1)
                    wait_dma(act, added, u, r, 0)
                    nc.scalar.copy(y[:, s, :], y_ps[s]).then_inc(y_sb, 1)

                def step(u, r):
                    silu(u, r)
                    if r + 1 < ST:
                        copy_x(u, r + 1)
                    if r >= 1:
                        copy_y(u, r - 1)

                copy_x(0, 0)
                run(act, step)
                copy_y(0, ST - 1)

            @block.vector
            def _(dve):
                def multiply(u, r):
                    s = r % 2
                    wait(dve, gate_sb, u, r, 1)
                    wait(dve, hidT_mm, u, r, -1)
                    nc.vector.scalar_tensor_tensor(hid[:, s, :], gu_ps[s][:, I:2 * I], slot_w[:, bass.ds(u * 2 + r, 1)],
                                                   gate[:, s, :], ALU.mult, ALU.mult).then_inc(hid_sb, 1)

                def copy_hid(u, r):
                    s = r % 2
                    wait(dve, hidT_mm, u, r, 1)
                    wait(dve, y_mm, u, r, -1)
                    nc.vector.tensor_copy(hidT[:, s].rearrange("p k m -> p (k m)"), hidT_ps[s]).then_inc(hidT_sb, 1)

                def step(u, r):
                    if r >= 1:
                        copy_hid(u, r - 1)
                    multiply(u, r)

                run(dve, step)
                copy_hid(0, ST - 1)


def phase_collect(nc, z, sums):
    with Memory(nc, "collect") as m:
        odd = m.sb("odd", [P, NT, C])
        loaded = m.sem("loaded")
        G = 4
        with nc.Block() as block:
            @block.sync
            def _(sp):
                for g in range(G):
                    for dst, src in ((z, sums[0]), (odd, sums[1])):
                        sp.dma_start(dst[:, g * NT // G:(g + 1) * NT // G, :],
                                     src[g * T // G:(g + 1) * T // G, :].rearrange("(t p) c -> p t c", p=P)).then_inc(loaded, 16)

            @block.vector
            def _(dve):
                dve.wait_ge(loaded, 16 * 2 * G)
                nc.vector.tensor_tensor(z[:], z[:], odd[:], ALU.add)


def phase_absorb(nc, bank, cst, wqk, vo, wqT_in, wq_in, wkvbT_in, wo_in):
    with Memory(nc, "absorb") as m:
        wqT = m.sb("wqT", [P, 2, 4, C])
        wkT = m.sb("wkT", [P, H, LORA])
        wvT = m.sb("wvT", [P, H, 2 * LORA])
        wo = m.sb("wo", [P, H, C])
        rope_loaded, wk_loaded, kv_loaded, zero_sb = (m.sem(n) for n in ("rope_loaded", "wk_loaded", "kv_loaded", "zero_sb"))
        wq_loaded = [m.sem(f"wq_loaded{s}") for s in range(2)]
        a_mm, a_sb, vo_mm, vo_sb = (m.sem(n) for n in ("a_mm", "a_sb", "vo_mm", "vo_sb"))
        HG = 4
        with nc.Block() as block:
            @block.gpsimd
            def _(pool):
                nc.gpsimd.memset(wvT[:], 0.0).then_inc(zero_sb, 1)

            @block.sync
            def _(sp):
                kvT = wkvbT_in.rearrange("(h x) l -> x h l", x=NOPE + VD)
                nopeT = wqT_in.rearrange("(h x) c -> x h c", x=QH)
                sp.dma_start(wkT[:], kvT[0:NOPE]).then_inc(wk_loaded, 16)
                for g in range(H // HG):
                    if g >= 2:
                        sp.wait_ge(a_mm, g - 1)
                    sp.dma_start(wqT[:, g % 2], nopeT[0:NOPE, g * HG:(g + 1) * HG]).then_inc(wq_loaded[g % 2], 16)
                for k in range(KC):
                    sp.dma_start(wqk[:, k].rearrange("p (h x) -> p h x", h=H)[:, :, LORA:2 * LORA],
                                 wq_in[k * P:(k + 1) * P, :].rearrange("p (h x) -> p h x", h=H)[:, :, NOPE:QH]
                                 ).then_inc(rope_loaded, 16)
                sp.wait_ge(zero_sb, 1)
                for odd in range(2):
                    sp.dma_start(wvT[:].rearrange("p (n two) x -> p two n x", two=2)[:, odd, :, odd * LORA:(odd + 1) * LORA],
                                 kvT.rearrange("x (n two) l -> x two n l", two=2)[NOPE:NOPE + VD, odd]).then_inc(kv_loaded, 16)
                sp.dma_start(wo[:], wo_in.rearrange("(h v) c -> v h c", v=VD)).then_inc(kv_loaded, 16)
                sp.wait_ge(rope_loaded, 16 * KC)

            @block.tensor
            def _(pe):
                pe.wait_ge(wk_loaded, 16)
                for g in range(H // HG):
                    pe.wait_ge(wq_loaded[g % 2], 16 * (g // 2 + 1))
                    if g >= 2:
                        pe.wait_ge(a_sb, g - 1)
                    for k in range(KC):
                        for i in range(HG):
                            mm = nc.tensor.matmul(bank[:, g % 2, (k * HG + i) * LORA:(k * HG + i + 1) * LORA],
                                                  wqT[:, g % 2, i, k * P:(k + 1) * P], wkT[:, g * HG + i, :],
                                                  start=True, stop=True)
                    mm.then_inc(a_mm, 1)
                pe.wait_ge(kv_loaded, 16 * 3)
                for n in range(H // 2):
                    if n >= 2:
                        pe.wait_ge(vo_sb, n - 1)
                    for odd in range(2):
                        mm = nc.tensor.matmul(bank[:, 2 + n % 2, 0:C], wvT[:, 2 * n + odd, :], wo[:, 2 * n + odd, :],
                                              start=odd == 0, stop=odd == 1)
                    mm.then_inc(vo_mm, 1)

            @block.vector
            def _(dve):
                for g in range(H // HG):
                    dve.wait_ge(a_mm, g + 1)
                    for k in range(KC):
                        ins = nc.vector.tensor_copy(
                            wqk[:, k].rearrange("p (h x) -> p h x", h=H)[:, g * HG:(g + 1) * HG, 0:LORA],
                            bank[:, g % 2, k * HG * LORA:(k + 1) * HG * LORA].rearrange("p (h x) -> p h x", h=HG))
                    ins.then_inc(a_sb, 1)

            @block.scalar
            def _(act):
                for n in range(H // 2):
                    act.wait_ge(vo_mm, n + 1)
                    nc.scalar.copy(vo[:, n, :], bank[:, 2 + n % 2, 0:C]).then_inc(vo_sb, 1)


def phase_latent(nc, bank, cst, xT, identb, power, kT, kTb, vmat, wkva_in, scale_in):
    with Memory(nc, "latent") as m:
        wkva = m.sb("wkva", [P, KC, P])
        scale = m.sb("scale", [P, LORA])
        raw = m.sb("raw", [P, NT, P])
        square = m.sb("square", [P, NT, LORA])
        meansq = m.sb("meansq", [P, NT])
        sumsq = m.sb("sumsq", [P, NT])
        rrms = m.sb("rrms", [P, NT])
        unit = m.sb("unit", [P, NT, LORA])
        rows = m.sb("rows", [P, NT, P])
        by_cos = m.sb("by_cos", [P, NT, ROPE])
        by_sin = m.sb("by_sin", [P, NT, ROPE])
        loaded, raw_mm, raw_sb, step_sb, meansq_sb, rrms_sb, rows_sb, turn_mm, kT_sb, ones_sb = (
            m.sem(n) for n in ("loaded", "raw_mm", "raw_sb", "step_sb", "meansq_sb", "rrms_sb", "rows_sb", "turn_mm",
                               "kT_sb", "ones_sb"))
        GT = 4
        half = ROPE // 2
        with nc.Block() as block:
            @block.sync
            def _(sp):
                sp.dma_start(wkva[:], wkva_in.rearrange("(k p) n -> p k n", p=P)).then_inc(loaded, 16)
                sp.dma_start(scale[:], scale_in.partition_broadcast(P)).then_inc(loaded, 16)

            @block.gpsimd
            def _(pool):
                nc.gpsimd.memset(vmat[:, :, 0, LORA:P], 1.0)
                nc.gpsimd.memset(vmat[:, :, 1, 0:LORA], 1.0).then_inc(ones_sb, 1)
                pool.wait_ge(meansq_sb, 1)
                nc.gpsimd.tensor_tensor(rrms[:], meansq[:], power[:, 0:NT], ALU.pow).then_inc(rrms_sb, 1)

            @block.tensor
            def _(pe):
                pe.wait_ge(loaded, 32)
                for t in range(NT):
                    if t >= 4 * GT:
                        pe.wait_ge(raw_sb, t // GT - 3)
                    for k in range(KC):
                        mm = nc.tensor.matmul(bank[:, t // GT % 4, t % GT * P:(t % GT + 1) * P], xT[:, k, t * P:(t + 1) * P],
                                              wkva[:, k, :], start=k == 0, stop=k == KC - 1)
                    if t % GT == GT - 1:
                        mm.then_inc(raw_mm, 1)
                pe.wait_ge(rows_sb, 2)
                for t in range(NT):
                    mm = nc.tensor.transpose(bank[:, 4 + t // GT, t % GT * P:(t % GT + 1) * P], rows[:, t, :], cst["ident"])
                    if t % GT == GT - 1:
                        mm.then_inc(turn_mm, 1)

            @block.scalar
            def _(act):
                for g in range(NT // GT):
                    act.wait_ge(turn_mm, g + 1)
                    nc.scalar.copy(kT[:, g * WIDE:(g + 1) * WIDE], bank[:, 4 + g, :]).then_inc(kT_sb, 1)

            @block.vector
            def _(dve):
                v, step = nc.vector, Count(step_sb, dve)
                for g in range(NT // GT):
                    dve.wait_ge(raw_mm, g + 1)
                    v.tensor_copy(raw[:, g * GT:(g + 1) * GT, :], bank[:, g, :].rearrange("p (t n) -> p t n", n=P)
                                  ).then_inc(raw_sb, 1)
                dve.wait_ge(raw_sb, NT // GT)
                step.up(v.tensor_tensor(square[:], raw[:, :, 0:LORA], raw[:, :, 0:LORA], ALU.mult))
                seq = lambda n: cst[n].rearrange("p (t x) -> p t x", x=ROPE)
                for b in range(B):
                    own = raw[:, b * QT:(b + 1) * QT, LORA:P]
                    step.up(v.tensor_tensor(by_cos[:, b * QT:(b + 1) * QT, :], own, seq("cos"), ALU.mult))
                    for h in range(2):
                        step.up(v.tensor_tensor(by_sin[:, b * QT:(b + 1) * QT, h * half:(h + 1) * half],
                                                own[:, :, (1 - h) * half:(2 - h) * half],
                                                seq("sin")[:, :, h * half:(h + 1) * half], ALU.mult))
                step.settle()
                step.up(v.tensor_reduce(sumsq[:], square[:], AX_X, ALU.add))
                step.up(v.tensor_tensor(rows[:, :, LORA:P], by_cos[:], by_sin[:], ALU.add))
                step.settle()
                v.tensor_scalar(meansq[:], sumsq[:], 1.0 / LORA, EPS_RMS, ALU.mult, ALU.add).then_inc(meansq_sb, 1)
                dve.wait_ge(rrms_sb, 1)
                dve.wait_ge(loaded, 32)
                step.up(v.tensor_tensor(unit[:], raw[:, :, 0:LORA], rrms[:].unsqueeze(2).to_broadcast([P, NT, LORA]), ALU.mult))
                step.settle()
                v.tensor_tensor(rows[:, :, 0:LORA], unit[:], scale[:].unsqueeze(1).to_broadcast([P, NT, LORA]),
                                ALU.mult).then_inc(rows_sb, 2)
                dve.wait_ge(rows_sb, 2)
                step.up(v.tensor_copy(vmat[:, :, 0, 0:LORA], rows[:, :, 0:LORA]))
                step.up(v.tensor_copy(vmat[:, :, 1, LORA:P], rows[:, :, 0:LORA]))
                dve.wait_ge(kT_sb, NT // GT)
                step.up(v.tensor_copy(kTb[:], kT[:]))


def phase_queries(nc, name, bank, cst, xT, wqk, qT, qTb, b, g):
    with Memory(nc, name) as m:
        CH = 4
        N = QT * (GH // CH)
        rows = m.sb("rows", [P, 2, CH, P])
        by_cos = m.sb("by_cos", [P, 2, CH, ROPE])
        by_sin = m.sb("by_sin", [P, 2, CH, ROPE])
        q_mm, plain_sb, rot_sb, step_sb, turn_mm, qT_sb, qTb_sb, spare_sb = (
            m.sem(n) for n in ("q_mm", "plain_sb", "rot_sb", "step_sb", "turn_mm", "qT_sb", "qTb_sb", "spare_sb"))
        half = ROPE // 2
        steps = [(t, c) for t in range(QT) for c in range(GH // CH)]
        with nc.Block() as block:
            @block.gpsimd
            def _(pool):
                nc.gpsimd.memset(qTb[:, GH, :], 0.0).then_inc(spare_sb, 1)
                for n in range(N):
                    pool.wait_ge(step_sb, 3 * (n + 1))
                    if n >= 2:
                        pool.wait_ge(turn_mm, n - 1)
                    nc.gpsimd.tensor_tensor(rows[:, n % 2, :, LORA:P], by_cos[:, n % 2], by_sin[:, n % 2],
                                            ALU.add).then_inc(rot_sb, 1)

            @block.tensor
            def _(pe):
                def turn(n):
                    pe.wait_ge(plain_sb, n + 1)
                    pe.wait_ge(rot_sb, n + 1)
                    if n >= 2:
                        pe.wait_ge(qTb_sb, n - 1)
                        pe.wait_ge(qT_sb, n - 1)
                    for i in range(CH):
                        mm = nc.tensor.transpose(bank[:, 2 + n % 2, i * P:(i + 1) * P], rows[:, n % 2, i, :], cst["ident"])
                    mm.then_inc(turn_mm, 1)

                for n, (t, c) in enumerate(steps):
                    if n >= 2:
                        pe.wait_ge(step_sb, 3 * (n - 1))
                        pe.wait_ge(plain_sb, n - 1)
                    for k in range(KC):
                        tok = b * S + t * P
                        h0 = g * GH + c * CH
                        mm = nc.tensor.matmul(bank[:, n % 2, :], xT[:, k, tok:tok + P], wqk[:, k, h0 * P:(h0 + CH) * P],
                                              start=k == 0, stop=k == KC - 1)
                    mm.then_inc(q_mm, 1)
                    if n >= 1:
                        turn(n - 1)
                turn(N - 1)

            @block.scalar
            def _(act):
                def out(n):
                    t, c = steps[n]
                    act.wait_ge(turn_mm, n + 1)
                    nc.scalar.copy(qT[:, c * CH:(c + 1) * CH, t * P:(t + 1) * P],
                                   bank[:, 2 + n % 2, :].rearrange("p (h m) -> p h m", m=P)).then_inc(qT_sb, 1)

                for n in range(N):
                    act.wait_ge(step_sb, 3 * (n + 1))
                    if n >= 2:
                        act.wait_ge(turn_mm, n - 1)
                    nc.scalar.copy(rows[:, n % 2, :, 0:LORA],
                                   bank[:, n % 2, :].rearrange("p (h m) -> p h m", m=P)[:, :, 0:LORA]).then_inc(plain_sb, 1)
                    if n >= 1:
                        out(n - 1)
                out(N - 1)

            @block.vector
            def _(dve):
                def out(n):
                    t, c = steps[n]
                    dve.wait_ge(qT_sb, n + 1)
                    nc.vector.tensor_copy(qTb[:, c * CH:(c + 1) * CH, t * P:(t + 1) * P],
                                          bank[:, 2 + n % 2, :].rearrange("p (h m) -> p h m", m=P)).then_inc(qTb_sb, 1)

                for n, (t, c) in enumerate(steps):
                    own = bank[:, n % 2, :].rearrange("p (h m) -> p h m", m=P)[:, :, LORA:P]
                    at = lambda name: cst[name][:, t * ROPE:(t + 1) * ROPE].unsqueeze(1)
                    dve.wait_ge(q_mm, n + 1)
                    if n >= 2:
                        dve.wait_ge(rot_sb, n - 1)
                    nc.vector.tensor_tensor(by_cos[:, n % 2], own, at("cos").to_broadcast([P, CH, ROPE]),
                                            ALU.mult).then_inc(step_sb, 1)
                    for h in range(2):
                        nc.vector.tensor_tensor(by_sin[:, n % 2, :, h * half:(h + 1) * half],
                                                own[:, :, (1 - h) * half:(2 - h) * half],
                                                at("sin")[:, :, h * half:(h + 1) * half].to_broadcast([P, CH, half]),
                                                ALU.mult).then_inc(step_sb, 1)
                    if n >= 1:
                        out(n - 1)
                out(N - 1)


def phase_attention(nc, name, bank, cst, bf, qT, qTb, kT, kTb, vmat, oT, b, g):
    with Memory(nc, name) as m:
        peak = m.sb("peak", [P, 2, 2, QT])
        whole = m.sb("whole", [P, 2, QT])
        minus = m.sb("minus", [P, 2, QT, P], BF16)
        prob = m.sb("prob", [P, 2, 2 * WIDE])
        rden = m.sb("rden", [P, 2, WIDE])
        max_mm, max_sb, whole_sb, minus_sb, s_mm, prob_sb, pv_mm, pair_mm, rden_sb, o_sb = (
            m.sem(n) for n in ("max_mm", "max_sb", "whole_sb", "minus_sb", "s_mm", "prob_sb", "pv_mm", "pair_mm",
                               "rden_sb", "o_sb"))
        pieces = [(i, k0, min(WIDE, (i + 1) * P - k0), k0 + WIDE >= (i + 1) * P)
                  for i in range(QT) for k0 in range(0, (i + 1) * P, WIDE)]
        groups = [(qc, [(j, max(j * P, qc * WIDE)) for j in (j0, j0 + 1)])
                  for qc in range(S // WIDE) for j0 in range(0, (qc + 1) * WIDE // P, 2)]
        NG, NP = len(groups), len(pieces)
        LOW = 4

        def span(group):
            qc, tiles = group
            end = (qc + 1) * WIDE
            a, z = WIDE - (end - tiles[0][1]), WIDE + end - tiles[1][1]
            return a, z, [(a, WIDE), (WIDE, z)]

        def wait(engine, sem, u, r, k, more):
            if r * k + more > 0:
                engine.wait_ge(sem, u * (2 * k) + (r * k + more))

        with nc.Block() as block:
            @block.tensor
            def _(pe):
                def max_piece(u, r, x):
                    i, k0, w, diagonal = pieces[x]
                    ps = bank[:, x % 2, 0:w]
                    wait(pe, max_sb, u, r, NP, x - 1)
                    mm = nc.tensor.matmul(ps, qTb[:, bass.ds(u * 2 + r, 1), i * P:(i + 1) * P].rearrange("p a m -> p (a m)"),
                                          kTb[:, b * S + k0:b * S + k0 + w], start=True, stop=not diagonal)
                    if diagonal:
                        mm = nc.tensor.matmul(ps[:, w - P:w], bf["late_q"], bf["ident"], start=False, stop=True)
                    mm.then_inc(max_mm, 1)

                def scores(u, r, x):
                    qc, tiles = groups[x]
                    if x >= 2:
                        wait(pe, prob_sb, u, r, NG, x - 1)
                    wait(pe, minus_sb, u, r, 2, 1 + qc)
                    for (j, q0), (a, z) in zip(tiles, span(groups[x])[2]):
                        ps = bank[:, 2 + 2 * (x % 2):4 + 2 * (x % 2), :].rearrange("p a n -> p (a n)")[:, a:z]
                        w = z - a
                        nc.tensor.matmul(ps, kT[:, b * S + j * P:b * S + (j + 1) * P],
                                         qT[:, bass.ds(u * 2 + r, 1), q0:q0 + w].rearrange("p a m -> p (a m)"),
                                         start=True, stop=False)
                        if q0 == j * P:
                            nc.tensor.matmul(ps[:, 0:P], bf["late_k"], bf["ident"], start=False, stop=False)
                        mm = nc.tensor.matmul(ps, bf["ones"], minus[:, r % 2].rearrange("p i m -> p (i m)")[:, q0:q0 + w],
                                              start=False, stop=True)
                    mm.then_inc(s_mm, 1)

                def values(u, r, x):
                    qc, tiles = groups[x]
                    wait(pe, prob_sb, u, r, NG, x + 1)
                    if tiles[0][0] == 0:
                        wait(pe, o_sb, u, r, 2, qc + 1)
                    for (j, q0), (a, z) in zip(tiles, span(groups[x])[2]):
                        last = j == (qc + 1) * WIDE // P - 1
                        mm = nc.tensor.matmul(bank[:, 6 + qc, q0 - qc * WIDE:WIDE], vmat[:, b * QT + j, r % 2, :],
                                              prob[:, x % 2, a:z], start=j == 0, stop=last)
                    mm.then_inc(pv_mm, 1)

                pe.sem_inc(s_mm, NG)
                for x in range(NP):
                    max_piece(0, 0, x)
                with pe.Fori(0, GH // 2) as u:
                    for r in range(2):
                        for x in range(NG):
                            scores(u, r, x)
                            max_piece(u, r + 1, 2 * x)
                            if x:
                                values(u, r, x - 1)
                            max_piece(u, r + 1, 2 * x + 1)
                        values(u, r, NG - 1)

            @block.scalar
            def _(act):
                with act.Fori(0, GH // 2) as u:
                    for r in range(2):
                        for x in range(NG):
                            a, z, _ = span(groups[x])
                            wait(act, s_mm, u, r, NG, NG + x + 1)
                            if x >= 2:
                                wait(act, pv_mm, u, r, NG, x - 1)
                            nc.scalar.activation(prob[:, x % 2, a:z],
                                                 bank[:, 2 + 2 * (x % 2):4 + 2 * (x % 2), :].rearrange("p a n -> p (a n)")[:, a:z],
                                                 ACT.Exp, scale=SCALE).then_inc(prob_sb, 1)

            @block.vector
            def _(dve):
                def peaks(u, r, x):
                    i, k0, w, _ = pieces[x]
                    wait(dve, max_mm, u, r, NP, x + 1)
                    nc.vector.tensor_reduce(peak[:, r % 2, k0 // WIDE, i:i + 1], bank[:, x % 2, 0:w], AX_X,
                                            ALU.max).then_inc(max_sb, 1)

                def spread(u, r, half):
                    n = [y for y in range(NP) if pieces[y][0] < LOW * (half + 1)][-1]
                    wait(dve, max_sb, u, r, NP, n + 1)
                    at = slice(half * LOW, (half + 1) * LOW)
                    if half:
                        nc.vector.tensor_tensor(whole[:, r % 2, at], peak[:, r % 2, 0, at], peak[:, r % 2, 1, at],
                                                ALU.max).then_inc(whole_sb, 1)
                    else:
                        nc.vector.tensor_copy(whole[:, r % 2, at], peak[:, r % 2, 0, at]).then_inc(whole_sb, 1)
                    wait(dve, whole_sb, u, r, 2, half + 1)
                    wait(dve, s_mm, u, r, NG, 0)
                    nc.vector.scalar_tensor_tensor(minus[:, r % 2, at, :],
                                                   bf["ident"].unsqueeze(1).to_broadcast([P, LOW, P]), -1.0,
                                                   whole[:, r % 2, at].unsqueeze(2).to_broadcast([P, LOW, P]),
                                                   ALU.mult, ALU.mult).then_inc(minus_sb, 1)

                def finish(u, r, qc):
                    n = [y for y in range(NG) if groups[y][0] == qc][-1]
                    lat, one = ((0, LORA), (LORA, P)) if r % 2 == 0 else ((LORA, P), (0, LORA))
                    wait(dve, pv_mm, u, r, NG, n + 1)
                    wait(dve, o_sb, u, r, 2, qc + 1)
                    nc.vector.reciprocal(rden[lat[0]:lat[1], qc, :], bank[one[0]:one[1], 6 + qc, :]).then_inc(rden_sb, 1)
                    wait(dve, rden_sb, u, r, 2, qc + 1)
                    nc.vector.tensor_tensor(
                        oT[lat[0]:lat[1], bass.ds(u + (g * GH + r) // 2, 1), qc * WIDE:(qc + 1) * WIDE].rearrange("p a m -> p (a m)"),
                        bank[lat[0]:lat[1], 6 + qc, :], rden[lat[0]:lat[1], qc, :], ALU.mult).then_inc(o_sb, 1)

                dve.sem_inc(o_sb, 2)
                for x in range(NP):
                    peaks(0, 0, x)
                    if x == LOW - 1:
                        spread(0, 0, 0)
                spread(0, 0, 1)
                with dve.Fori(0, GH // 2) as u:
                    for r in range(2):
                        for x in range(NG):
                            peaks(u, r + 1, 2 * x)
                            peaks(u, r + 1, 2 * x + 1)
                            if x == 1:
                                spread(u, r + 1, 0)
                            if x == 3:
                                finish(u, r, 0)
                        spread(u, r + 1, 1)
                        finish(u, r, 1)


def phase_output(nc, name, bank, z, x_tok, oT, vo, b):
    with Memory(nc, name) as m:
        y_mm, z_sb = m.sem("y_mm"), m.sem("z_sb")
        with nc.Block() as block:
            @block.tensor
            def _(pe):
                for t in range(QT):
                    if t >= 4:
                        pe.wait_ge(z_sb, t - 3)
                    for n in range(H // 2):
                        mm = nc.tensor.matmul(bank[:, t % 4, 0:C], oT[:, n, t * P:(t + 1) * P], vo[:, n, :],
                                              start=n == 0, stop=n == H // 2 - 1)
                    mm.then_inc(y_mm, 1)

            @block.vector
            def _(dve):
                for t in range(QT):
                    dve.wait_ge(y_mm, t + 1)
                    nc.vector.tensor_tensor(z[:, b * QT + t, :], bank[:, t % 4, 0:C], x_tok[:, b * QT + t, :],
                                            ALU.add).then_inc(z_sb, 1)


def phase_feed_forward(nc, bank, xT, x_tok, z, gateT_in, upT_in, downT_in, s_gate_in, s_up_in, s_down_in):
    NHT = len(HT)
    with Memory(nc, "ffn") as m:
        raw = m.sb("raw", [P, 2, HID], I32)
        down_raw = m.sb("down_raw", [P, 2, C], I32)
        w = {n: m.sb(n, [P, KC, HID]) for n in ("gate", "up")}
        down = m.sb("down", [P, NHT, C])
        down_off = m.sb("down_off", [P, 2, C])
        s_gate = m.sb("s_gate", [P, NHT])
        s_up = m.sb("s_up", [P, NHT])
        s_down = m.sb("s_down", [P, C])
        gate = m.sb("gated", [P, 2, WIDE])
        hid = m.sb("hid", [P, 2, NHT, WIDE])
        scales, raw_sb, off_sb, down_sb = (m.sem(n) for n in ("scales", "raw_sb", "off_sb", "down_sb"))
        raw_loaded = [m.sem(f"raw_loaded{s}") for s in range(2)]
        down_loaded = [m.sem(f"down_loaded{s}") for s in range(2)]
        gu_mm, gate_sb, hid_sb, y_mm, z_sb = (m.sem(n) for n in ("gu_mm", "gate_sb", "hid_sb", "y_mm", "z_sb"))
        order = [("gate", 0), ("gate", 1), ("up", 0), ("up", 1)]
        CT = WIDE // P
        with nc.Block() as block:
            @block.sync
            def _(sp):
                for vec, dst in ((s_gate_in, s_gate), (s_up_in, s_up)):
                    for n, (h0, hw) in enumerate(HT):
                        sp.dma_start(dst[0:hw, n:n + 1], vec[h0:h0 + hw].unsqueeze(1)).then_inc(scales, 16)
                sp.dma_start(s_down[:], s_down_in.partition_broadcast(P)).then_inc(scales, 16)
                for n, (name, k) in enumerate(order):
                    if n >= 2:
                        sp.wait_ge(raw_sb, n - 1)
                    sp.dma_start(raw[:, n % 2, :], (gateT_in if name == "gate" else upT_in)[k * P:(k + 1) * P, :]
                                 ).then_inc(raw_loaded[n % 2], 16)
                for n, (h0, hw) in enumerate(HT):
                    if n >= 2:
                        sp.wait_ge(off_sb, n - 1)
                    sp.dma_start(down_raw[0:hw, n % 2, :], downT_in[h0:h0 + hw, :]).then_inc(down_loaded[n % 2], 16)

            @block.gpsimd
            def _(pool):
                for n, (name, k) in enumerate(order):
                    pool.wait_ge(raw_loaded[n % 2], 16 * (n // 2 + 1))
                    nc.gpsimd.tensor_scalar(w[name][:, k, :], raw[:, n % 2, :], -ZERO_POINT, 1.0, ALU.add,
                                            ALU.mult).then_inc(raw_sb, 1)
                pool.wait_ge(scales, 16 * (2 * NHT + 1))
                for n, (h0, hw) in enumerate(HT):
                    pool.wait_ge(down_loaded[n % 2], 16 * (n // 2 + 1))
                    if n >= 2:
                        pool.wait_ge(down_sb, n - 1)
                    nc.gpsimd.tensor_scalar(down_off[0:hw, n % 2, :], down_raw[0:hw, n % 2, :], -ZERO_POINT, 1.0, ALU.add,
                                            ALU.mult).then_inc(off_sb, 1)
                    pool.wait_ge(off_sb, n + 1)
                    nc.gpsimd.tensor_tensor(down[0:hw, n, :], down_off[0:hw, n % 2, :], s_down[0:hw, :],
                                            ALU.mult).then_inc(down_sb, 1)

            @block.tensor
            def _(pe):
                def gate_up(ch):
                    for n, (h0, hw) in enumerate(HT):
                        x = ch * NHT + n
                        if x >= 2:
                            pe.wait_ge(hid_sb, x - 1)
                        for a, name in enumerate(("gate", "up")):
                            for k in range(KC):
                                mm = nc.tensor.matmul(bank[0:hw, 2 * (x % 2) + a, :], w[name][:, k, h0:h0 + hw],
                                                      xT[:, k, ch * WIDE:(ch + 1) * WIDE], start=k == 0, stop=k == KC - 1)
                        mm.then_inc(gu_mm, 1)

                def down_of(ch):
                    pe.wait_ge(hid_sb, (ch + 1) * NHT)
                    for i in range(CT):
                        t = ch * CT + i
                        if t >= 4:
                            pe.wait_ge(z_sb, t - 3)
                        for n, (h0, hw) in enumerate(HT):
                            mm = nc.tensor.matmul(bank[:, 4 + t % 4, 0:C], hid[0:hw, ch % 2, n, i * P:(i + 1) * P],
                                                  down[0:hw, n, :], start=n == 0, stop=n == NHT - 1)
                        mm.then_inc(y_mm, 1)

                pe.wait_ge(raw_sb, len(order))
                for ch in range(NCH):
                    gate_up(ch)
                    if ch == 1:
                        pe.wait_ge(down_sb, NHT)
                    if ch:
                        down_of(ch - 1)
                down_of(NCH - 1)

            @block.scalar
            def _(act):
                act.wait_ge(scales, 16 * (2 * NHT + 1))
                for x in range(NCH * NHT):
                    n = x % NHT
                    hw = HT[n][1]
                    act.wait_ge(gu_mm, x + 1)
                    if x >= 2:
                        act.wait_ge(hid_sb, x - 1)
                    nc.scalar.activation(gate[0:hw, x % 2, :], bank[0:hw, 2 * (x % 2), :], ACT.Silu,
                                         scale=s_gate[0:hw, n:n + 1]).then_inc(gate_sb, 1)

            @block.vector
            def _(dve):
                def sum_of(ch):
                    for t in range(ch * CT, (ch + 1) * CT):
                        dve.wait_ge(y_mm, t + 1)
                        nc.vector.tensor_tensor(z[:, t, :], bank[:, 4 + t % 4, 0:C], x_tok[:, t, :], ALU.add).then_inc(z_sb, 1)

                dve.wait_ge(scales, 16 * (2 * NHT + 1))
                for ch in range(NCH):
                    for n, (h0, hw) in enumerate(HT):
                        x = ch * NHT + n
                        dve.wait_ge(gate_sb, x + 1)
                        if n == 0 and ch >= 2:
                            dve.wait_ge(y_mm, (ch - 1) * CT)
                        nc.vector.scalar_tensor_tensor(hid[0:hw, ch % 2, n, :], bank[0:hw, 2 * (x % 2) + 1, :],
                                                       s_up[0:hw, n:n + 1], gate[0:hw, x % 2, :], ALU.mult,
                                                       ALU.mult).then_inc(hid_sb, 1)
                    if ch:
                        sum_of(ch - 1)
                sum_of(NCH - 1)


def phase_start(nc, cst_tile, cst, bf, ones_f, power, table_in, w_gu, w_down, weights_loaded, gate_in, up_in, down_in, zero, sums):
    with Memory(nc, "start") as m:
        loaded, zero_sb, made_sb = m.sem("loaded"), m.sem("zero_sb"), m.sem("made_sb")
        with nc.Block() as block:
            @block.sync
            def _(sp):
                sp.dma_start(cst_tile[:], table_in).then_inc(loaded, 16)
                sp.wait_ge(loaded, 16)

            @block.gpsimd
            def _(pool):
                nc.gpsimd.memset(power[:], -0.5).then_inc(made_sb, 1)
                nc.gpsimd.memset(bf["ones"], 1.0).then_inc(made_sb, 1)

            @block.vector
            def _(dve):
                nc.vector.memset(zero[:], 0.0).then_inc(zero_sb, 1)
                dve.wait_ge(loaded, 16)
                for name in ("ident", "late_q", "late_k"):
                    nc.vector.tensor_copy(bf[name], cst[name])


def program(nc, x, xT_in, wqkvT, wprojT, bproj, routerT, rbias, gate, up, down, wqT, wq, wkva, wkvbT, wo, kvscale,
            gateT, s_gate, upT, s_up, downT, s_down, table, out):
    x_rows = nc.dram_tensor("x_rows", (T, C), F32).ap()
    sums = [nc.dram_tensor(f"sums{s}", (FAR + P, C), F32).ap() for s in range(2)]
    with Memory(nc, "all") as m:
        bank = m.ps("bank", [P, 8, WIDE])
        at, width = const_columns()
        cst_tile = m.sb("cst", [P, width])
        cst = {n: cst_tile[:, a:z] for n, (a, z) in at.items()}
        bft = m.sb("bf", [P, 4, P], BF16)
        bf = {n: bft[:, i, :] for i, n in enumerate(("ident", "ones", "late_q", "late_k"))}
        power = m.sb("power", [P, NT])
        x_tok = m.sb("x_tok", [P, NT, C])
        xT = m.sb("xT", [P, KC, T])
        with Memory(nc, "early") as me:
            z = me.sb("z", [P, NT, C])
            weights_loaded = me.sem("weights_loaded")
            with Memory(nc, "zeros") as mz:
                zero = mz.sb("zero", [P, C])
                phase_start(nc, cst_tile, cst, bf, None, power, table, None, None, None, None, None, None, zero, sums)
                zeroed = mz.sem("zeroed")
                with nc.Block() as block:
                    @block.sync
                    def _(sp):
                        for n in range(FAR // P + 1):
                            sp.dma_start(sums[1][n * P:(n + 1) * P, :], zero[:]).then_inc(zeroed, 16)
                        sp.dma_start(sums[0][FAR:FAR + P, :], zero[:]).then_inc(zeroed, 16)
                        sp.wait_ge(zeroed, 16 * (FAR // P + 2))
            phase_linear_attention(nc, bank, cst, x_tok, xT, z, x, xT_in, wqkvT, wprojT, bproj)
            phase_layernorm(nc, "ln1", bank, cst, z, x_tok, xT, [x_rows, sums[0]])
            slot_row = me.sb("slot_row", [P, SLOT_TILES], I32)
            slot_far = me.sb("slot_far", [P, SLOT_TILES], I32)
            slot_w = me.sb("slot_w", [P, SLOT_TILES])
            tile_expert = me.sb("tile_expert", [1, SLOT_TILES], I32)
            phase_route(nc, bank, cst, xT, routerT, rbias, slot_row, slot_far, slot_w, tile_expert)
            w_gu = me.sb("w_gu", [P, E * KC * 2 * I])
            w_down = me.sb("w_down", [IH, E * 2 * C])
            with nc.Block() as block:
                @block.sync
                def _(sp):
                    gu = w_gu[:].rearrange("p (e k n) -> p e k n", e=E, k=KC)
                    for e in range(E):
                        sp.dma_start(gu[:, e, :, 0:I], gate[e].rearrange("(k p) n -> p k n", p=P)).then_inc(weights_loaded, 16)
                        sp.dma_start(gu[:, e, :, I:2 * I], up[e].rearrange("(k p) n -> p k n", p=P)).then_inc(weights_loaded, 16)
                    sp.dma_start(w_down[:].rearrange("p (e k n) -> p e k n", e=E, k=2),
                                 down.rearrange("e (k p) n -> p e k n", p=IH)).then_inc(weights_loaded, 16)
            phase_experts(nc, bank, cst, w_gu, w_down, weights_loaded, 16 * (2 * E + 1), x_rows, sums, slot_row, slot_far,
                          slot_w, tile_expert)
            phase_collect(nc, z, sums)
            phase_layernorm(nc, "ln2", bank, cst, z, x_tok, xT, [])
        with Memory(nc, "late") as ml:
            wqk = ml.sb("wqk", [P, KC, H * P])
            vo = ml.sb("vo", [P, H // 2, C])
            kT = ml.sb("kT", [P, T])
            kTb = ml.sb("kTb", [P, T], BF16)
            vmat = ml.sb("vmat", [P, NT, 2, P])
            phase_absorb(nc, bank, cst, wqk, vo, wqT, wq, wkvbT, wo)
            phase_latent(nc, bank, cst, xT, bf["ident"], power, kT, kTb, vmat, wkva, kvscale)
            with Memory(nc, "heads") as mh:
                qT = mh.sb("qT", [P, GH, S])
                qTb = mh.sb("qTb", [P, GH + 1, S], BF16)
                oT = mh.sb("oT", [P, H // 2, S])
                for b in range(B):
                    for g in range(H // GH):
                        phase_queries(nc, f"q{b}{g}", bank, cst, xT, wqk, qT, qTb, b, g)
                        phase_attention(nc, f"att{b}{g}", bank, cst, bf, qT, qTb, kT, kTb, vmat, oT, b, g)
                    phase_output(nc, f"out{b}", bank, x_tok, x_tok, oT, vo, b)
        with Memory(nc, "last") as ml:
            z = ml.sb("z", [P, NT, C])
            phase_layernorm(nc, "ln3", bank, cst, x_tok, z, xT, [])
            phase_feed_forward(nc, bank, xT, z, x_tok, gateT, upT, downT, s_gate, s_up, s_down)
            phase_layernorm(nc, "ln4", bank, cst, x_tok, z, None, [out])


def kernel(**a):
    import concourse.bacc as bacc
    from concourse.bass_utils import run_bass_kernel_spmd

    x = np.asarray(a["L0_attn_x"]).reshape(T, C)
    turned = lambda n: np.asarray(a[n]).T
    ins = {
        "x": x, "xT": x.T, "wqkvT": turned("L0_attn_w_qkv"), "wprojT": turned("L0_attn_w_proj"), "bproj": a["L0_attn_b_proj"],
        "routerT": turned("L0_ffn_router_w"), "rbias": a["L0_ffn_expert_bias"], "gate": a["L0_ffn_gate_proj"],
        "up": a["L0_ffn_up_proj"], "down": a["L0_ffn_down_proj"], "wqT": turned("L1_attn_wq"), "wq": a["L1_attn_wq"],
        "wkva": a["L1_attn_wkv_a"], "wkvbT": turned("L1_attn_wkv_b"), "wo": a["L1_attn_wo"],
        "kvscale": a["L1_attn_kv_norm_scale"], "gateT": turned("L1_ffn_wq_gate"), "s_gate": a["L1_ffn_s_gate"],
        "upT": turned("L1_ffn_wq_up"), "s_up": a["L1_ffn_s_up"], "downT": turned("L1_ffn_wq_down"),
        "s_down": a["L1_ffn_s_down"], "table": const_table(),
    }
    nc = bacc.Bacc("TRN2", target_bir_lowering=False, num_devices=1)
    arrays, aps = {}, []
    for name, v in ins.items():
        v = np.ascontiguousarray(v)
        arrays[f"in_{name}"] = v
        aps.append(nc.dram_tensor(f"in_{name}", v.shape, mybir.dt.from_np(v.dtype), kind="ExternalInput").ap())
    out = nc.dram_tensor("out_x", (T, C), F32, kind="ExternalOutput").ap()
    program(nc, *aps, out)
    r = run_bass_kernel_spmd(nc, [arrays], core_ids=[0])
    return r.results[0]["out_x"].reshape(B, S, C)
```

```python
from contextlib import ExitStack

import numpy as np

import concourse.bass as bass
from concourse import mybir

F32 = mybir.dt.float32
F32R = mybir.dt.float32r
BF16 = mybir.dt.bfloat16
I32 = mybir.dt.int32
U32 = mybir.dt.uint32
ALU = mybir.AluOpType
ACT = mybir.ActivationFunctionType
AX_X = mybir.AxisListType.X

P = 128
B, S, C = 2, 1024, 256
T = B * S
NT = T // P
KC = C // P
WIDE = 512
NCH = T // WIDE
EPS_LN = 1e-5

EPS_DEN = 1e-15
HD = 32

E, TOPK, I = 16, 4, 224
IH = I // 2
SLOT_TILES = T * TOPK // P + E
WIDTH_HOT = 86
FAR = 2048

H, NOPE, ROPE, VD, LORA = 16, 128, 64, 128, 64
QH = NOPE + ROPE
SCALE = QH ** -0.5
EPS_RMS = 1e-6
QT = S // P
PAIRS = H // 2
MASKED = -1e30

HID = 704
ZERO_POINT = 128.0
HT = [(n * P, min(P, HID - n * P)) for n in range((HID + P - 1) // P)]


def const_columns():
    at, n = {}, 0
    for name, width in (("ident", P), ("before", P), ("iota", P), ("headmask", P), ("late_q", P), ("late_k", P), ("late_cols", 2 * P),
                        ("row", 1), ("eps_ln", 1), ("cos", QT * ROPE), ("sin", QT * ROPE)):
        at[name] = (n, n + width)
        n += width
    return at, n


def const_table():
    at, n = const_columns()
    t = np.zeros((P, n), np.float32)
    p, f = np.arange(P)[:, None], np.arange(P)[None, :]

    def put(name, v):
        t[:, at[name][0]:at[name][1]] = v

    put("ident", p == f)
    put("before", p < f)
    put("iota", np.broadcast_to(f, (P, P)))
    put("headmask", p // HD == f // HD)
    put("late_q", np.where(p > f, MASKED, 0.0))
    put("late_k", np.where(f >= p, MASKED, 0.0))
    q = np.arange(2 * P)[None, :] - P
    put("late_cols", p == np.maximum(q + 1, 0))
    put("row", p)
    put("eps_ln", EPS_LN)
    half = ROPE // 2
    inv = (np.float32(1.0) / np.float32(10000.0) ** (np.arange(0, ROPE, 2, dtype=np.float32) / np.float32(ROPE)))
    ang = np.arange(S, dtype=np.float32)[:, None] * inv.astype(np.float32)
    cos, sin = np.cos(ang), np.sin(ang)
    lay = lambda a: a.reshape(QT, P, ROPE).transpose(1, 0, 2).reshape(P, QT * ROPE)
    put("cos", lay(np.concatenate([cos, cos], 1)))
    put("sin", lay(np.concatenate([-sin, sin], 1)))
    return t


class Memory:

    def __init__(self, nc, name):
        self.nc, self.name, self.stack, self.sems = nc, name, ExitStack(), []

    def __enter__(self):
        return self

    def __exit__(self, *a):
        if self.sems and a[0] is None:
            self.nc.clear_and_free_semaphores(self.sems)
            self.nc.all_engine_barrier(sem_only=True)
        return self.stack.__exit__(*a)

    def sb(self, name, shape, dt=F32):
        return self.stack.enter_context(self.nc.sbuf_tensor(f"{self.name}_{name}", shape, dt))

    def ps(self, name, shape, dt=F32):
        return self.stack.enter_context(self.nc.psum_tensor(f"{self.name}_{name}", shape, dt))

    def sem(self, name):
        self.sems.append(self.nc.alloc_semaphore(f"{self.name}_{name}"))
        return self.sems[-1]


class Count:

    def __init__(self, sem, engine):
        self.sem, self.engine, self.n = sem, engine, 0

    def up(self, ins):
        ins.then_inc(self.sem, 1)
        self.n += 1

    def settle(self):
        self.engine.wait_ge(self.sem, self.n)


def phase_linear_attention(nc, bank, cst, x_tok, xT, z, x_in, xT_in, wqkvT_in, wprojT_in, bproj_in, w_gu, weights_loaded,
                           gate_in, up_in):
    with Memory(nc, "lin") as m:
        wqkvT = m.sb("wqkvT", [P, KC, 3 * C])
        wprojT = m.sb("wprojT", [P, KC, C])
        bproj = m.sb("bproj", [P, C])
        kmat = m.sb("kmat", [P, NT, C])
        vones = m.sb("vones", [P, NT, KC, P + 1])
        qT = m.sb("qT0", [P, KC, T])
        aT = m.sb("aT", [P, KC, T])
        vk_num = m.sb("vk_num", [P, B * KC, P])
        vk_den = m.sb("vk_den", [P, B * KC, P])
        den = m.sb("den", [P, 2, WIDE])
        rec = m.sb("rec", [P, 2, WIDE])
        loaded, loaded_x = m.sem("loaded"), m.sem("loaded_x")
        kv_mm, k_sb, v_sb, q_mm, q_sb = (m.sem(n) for n in ("kv_mm", "k_sb", "v_sb", "q_mm", "q_sb"))
        vk_mm, vk_sb, nd_mm, den_sb, rec_sb, a_sb = (m.sem(n) for n in ("vk_mm", "vk_sb", "nd_mm", "den_sb", "rec_sb", "a_sb"))
        y_mm, z_sb, xb_sb, ones_sb = (m.sem(n) for n in ("y_mm", "z_sb", "xb_sb", "ones_sb"))
        kv_ps = [bank[:, n, :] for n in (0, 1)]
        q_ps = [bank[:, n, :] for n in (2, 3)]
        vk_ps = [bank[:, n, :] for n in (4, 5)]
        num_ps = [bank[:, n, :] for n in (0, 1)]
        den_ps = [bank[:, n, :] for n in (2, 3)]
        y_ps = [bank[:, n, :] for n in (6, 7)]
        cols = [(b, g, ch) for b in range(B) for g in range(KC) for ch in range(S // WIDE)]

        with nc.Block() as block:
            @block.sync
            def _(sp):
                sp.dma_start(wqkvT[:], wqkvT_in.rearrange("(k p) n -> p k n", p=P)).then_inc(loaded, 16)
                for k in range(KC):
                    sp.dma_start(xT[:, k, :], xT_in[k * P:(k + 1) * P, :]).then_inc(loaded, 16)
                sp.dma_start(wprojT[:], wprojT_in.rearrange("(k p) n -> p k n", p=P)).then_inc(loaded, 16)
                sp.dma_start(x_tok[:], x_in.rearrange("(t p) c -> p t c", p=P)).then_inc(loaded_x, 16)
                sp.dma_start(bproj[:], bproj_in.partition_broadcast(P)).then_inc(loaded_x, 16)
                gu = w_gu[:].rearrange("p (e k n) -> p e k n", e=E, k=KC)
                for e in range(E):
                    for a, src in enumerate((gate_in, up_in)):
                        sp.dma_start(gu[:, e, :, a * I:(a + 1) * I], src[e].rearrange("(k p) n -> p k n", p=P)
                                     ).then_inc(weights_loaded, 16)

            @block.gpsimd
            def _(pool):
                nc.gpsimd.memset(vones[:, :, :, P:P + 1], 1.0).then_inc(ones_sb, 1)
                pool.wait_ge(loaded_x, 32)
                nc.gpsimd.tensor_tensor(x_tok[:], x_tok[:], bproj[:].unsqueeze(1).to_broadcast([P, NT, C]),
                                        ALU.add).then_inc(xb_sb, 1)

            @block.tensor
            def _(pe):
                pe.wait_ge(loaded, 16 * (KC + 2))
                for t in range(NT):
                    if t >= 2:
                        pe.wait_ge(k_sb, t - 1)
                        pe.wait_ge(v_sb, t - 1)
                    for k in range(KC):
                        mm = nc.tensor.matmul(kv_ps[t % 2], xT[:, k, t * P:(t + 1) * P], wqkvT[:, k, C:3 * C],
                                              start=k == 0, stop=k == KC - 1)
                    mm.then_inc(kv_mm, 1)
                for n in range(KC * NCH):
                    g, ch = divmod(n, NCH)
                    if n >= 2:
                        pe.wait_ge(q_sb, n - 1)
                    for k in range(KC):
                        mm = nc.tensor.matmul(q_ps[n % 2], wqkvT[:, k, g * P:(g + 1) * P],
                                              xT[:, k, ch * WIDE:(ch + 1) * WIDE], start=k == 0, stop=k == KC - 1)
                    mm.then_inc(q_mm, 1)
                pe.wait_ge(k_sb, NT)
                pe.wait_ge(v_sb, NT)
                pe.wait_ge(ones_sb, 1)
                for n in range(B * KC):
                    b, g = divmod(n, KC)
                    if n >= 2:
                        pe.wait_ge(vk_sb, 2 * (n - 1))
                    for i in range(QT):
                        t = b * QT + i
                        mm = nc.tensor.matmul(vk_ps[n % 2][:, 0:P + 1], kmat[:, t, g * P:(g + 1) * P],
                                              vones[:, t, g, :], start=i == 0, stop=i == QT - 1)
                    mm.then_inc(vk_mm, 1)
                pe.wait_ge(q_sb, KC * NCH)
                for n, (b, g, ch) in enumerate(cols):
                    pe.wait_ge(vk_sb, 2 * (b * KC + g + 1))
                    if n >= 2:
                        pe.wait_ge(a_sb, n - 1)
                    rhs = qT[:, g, b * S + ch * WIDE:b * S + (ch + 1) * WIDE]
                    nc.tensor.matmul(num_ps[n % 2], vk_num[:, b * KC + g, :], rhs, start=True, stop=True)
                    nc.tensor.matmul(den_ps[n % 2], vk_den[:, b * KC + g, :], rhs, start=True, stop=True).then_inc(nd_mm, 1)
                for t in range(NT):
                    if t % QT == 0:
                        pe.wait_ge(a_sb, len(cols) // B * (t // QT + 1))
                    if t >= 2:
                        pe.wait_ge(z_sb, t - 1)
                    for k in range(KC):
                        mm = nc.tensor.matmul(y_ps[t % 2][:, 0:C], aT[:, k, t * P:(t + 1) * P], wprojT[:, k, :],
                                              start=k == 0, stop=k == KC - 1)
                    mm.then_inc(y_mm, 1)

            @block.scalar
            def _(act):
                for t in range(NT):
                    act.wait_ge(kv_mm, t + 1)
                    nc.scalar.activation(kmat[:, t, :], kv_ps[t % 2][:, 0:C], ACT.Relu).then_inc(k_sb, 1)
                for n in range(KC * NCH):
                    g, ch = divmod(n, NCH)
                    act.wait_ge(q_mm, n + 1)
                    nc.scalar.activation(qT[:, g, ch * WIDE:(ch + 1) * WIDE], q_ps[n % 2], ACT.Relu).then_inc(q_sb, 1)

            @block.vector
            def _(dve):
                for t in range(NT):
                    dve.wait_ge(kv_mm, t + 1)
                    dve.wait_ge(k_sb, t + 1)
                    nc.vector.tensor_copy(vones[:, t, :, 0:P],
                                          kv_ps[t % 2][:, C:2 * C].rearrange("p (g c) -> p g c", g=KC)).then_inc(v_sb, 1)
                for n in range(B * KC):
                    dve.wait_ge(vk_mm, n + 1)
                    mask = cst["headmask"]
                    nc.vector.tensor_tensor(vk_num[:, n, :], vk_ps[n % 2][:, 0:P], mask, ALU.mult).then_inc(vk_sb, 1)
                    nc.vector.tensor_scalar(vk_den[:, n, :], mask, vk_ps[n % 2][:, P:P + 1], None,
                                            ALU.mult).then_inc(vk_sb, 1)
                for n, (b, g, ch) in enumerate(cols):
                    dve.wait_ge(nd_mm, n + 1)
                    nc.vector.tensor_scalar(den[:, n % 2, :], den_ps[n % 2], EPS_DEN, None, ALU.add).then_inc(den_sb, 1)
                    dve.wait_ge(den_sb, n + 1)
                    nc.vector.reciprocal(rec[:, n % 2, :], den[:, n % 2, :]).then_inc(rec_sb, 1)
                    dve.wait_ge(rec_sb, n + 1)
                    nc.vector.tensor_tensor(aT[:, g, b * S + ch * WIDE:b * S + (ch + 1) * WIDE], num_ps[n % 2],
                                            rec[:, n % 2, :], ALU.mult).then_inc(a_sb, 1)
                dve.wait_ge(xb_sb, 1)
                for t in range(NT):
                    dve.wait_ge(y_mm, t + 1)
                    nc.vector.tensor_tensor(z[:, t, :], y_ps[t % 2][:, 0:C], x_tok[:, t, :], ALU.add).then_inc(z_sb, 1)


def phase_layernorm(nc, name, bank, cst, z, x_tok, xT, rows_out, x_hl=None):
    turned = xT if x_hl is None else x_hl[:, 0]
    with Memory(nc, name) as m:
        stats = m.sb("ln_stats", [P, NT, 6])
        meanvar = m.sb("ln_meanvar", [P, NT, 2])
        vareps = m.sb("ln_vareps", [P, NT])
        power = m.sb("ln_power", [P, NT])
        rstd = m.sb("ln_rstd", [P, NT])
        power_sb, stats_sb, mv_sb, ve_sb, rstd_sb = (m.sem(n) for n in ("power_sb", "stats_sb", "mv_sb", "ve_sb", "rstd_sb"))
        x_sb, xT_mm, xT_sb, rest_sb, stored = (m.sem(n) for n in ("x_sb", "xT_mm", "xT_sb", "rest_sb", "stored"))
        GT = 4
        with nc.Block() as block:
            @block.gpsimd
            def _(pool):
                nc.gpsimd.memset(power[:], -0.5).then_inc(power_sb, 1)
                for g in range(NT // GT):
                    sl = slice(g * GT, (g + 1) * GT)
                    pool.wait_ge(mv_sb, (g + 1) * GT)
                    nc.gpsimd.tensor_scalar(vareps[:, sl], meanvar[:, sl, 1], EPS_LN, None, ALU.add).then_inc(ve_sb, 1)
                    pool.wait_ge(ve_sb, g + 1)
                    pool.wait_ge(power_sb, 1)
                    nc.gpsimd.tensor_tensor(rstd[:, sl], vareps[:, sl], power[:, sl], ALU.pow).then_inc(rstd_sb, 1)

            @block.vector
            def _(dve):
                def rest(g):
                    for k in range(KC):
                        n, at = g * KC + k, slice(g * WIDE, (g + 1) * WIDE)
                        dve.wait_ge(xT_sb, n + 1)
                        nc.vector.tensor_tensor(x_hl[:, 1, k, at], bank[:, n % 4, :], x_hl[:, 0, k, at].bitcast(F32),
                                                ALU.subtract).then_inc(rest_sb, 1)

                for g in range(NT // GT + 1):
                    if g < NT // GT:
                        for t in range(g * GT, (g + 1) * GT):
                            nc.vector.bn_stats(stats[:, t, :], z[:, t, :]).then_inc(stats_sb, 1)
                        for t in range(g * GT, (g + 1) * GT):
                            dve.wait_ge(stats_sb, t + 1)
                            nc.vector.bn_aggr(meanvar[:, t, :], stats[:, t, :]).then_inc(mv_sb, 1)
                    if g:
                        dve.wait_ge(rstd_sb, g)
                        for t in range((g - 1) * GT, g * GT):
                            nc.vector.tensor_scalar(x_tok[:, t, :], z[:, t, :], meanvar[:, t, 0:1], rstd[:, t:t + 1],
                                                    ALU.subtract, ALU.mult).then_inc(x_sb, 1)
                    if g >= 2 and x_hl is not None:
                        rest(g - 2)
                if x_hl is not None:
                    rest(NT // GT - 1)

            @block.tensor
            def _(pe):
                if turned is None:
                    return
                for g in range(NT // GT):
                    for k in range(KC):
                        n = g * KC + k
                        if n >= 4:
                            pe.wait_ge(xT_sb if x_hl is None else rest_sb, n - 3)
                        for i in range(GT):
                            t = g * GT + i
                            pe.wait_ge(x_sb, t + 1)
                            mm = nc.tensor.transpose(bank[:, n % 4, i * P:(i + 1) * P], x_tok[:, t, k * P:(k + 1) * P],
                                                     cst["ident"])
                        mm.then_inc(xT_mm, 1)

            @block.scalar
            def _(act):
                if turned is None:
                    return
                for n in range(NT // GT * KC):
                    g, k = divmod(n, KC)
                    act.wait_ge(xT_mm, n + 1)
                    nc.scalar.copy(turned[:, k, g * WIDE:(g + 1) * WIDE], bank[:, n % 4, :]).then_inc(xT_sb, 1)

            @block.sync
            def _(sp):
                for g in range(NT // GT):
                    sp.wait_ge(x_sb, (g + 1) * GT)
                    for r in rows_out:
                        sp.dma_start(r[0:T, :].rearrange("(t p) c -> p t c", p=P)[:, g * GT:(g + 1) * GT, :],
                                     x_tok[:, g * GT:(g + 1) * GT, :]).then_inc(stored, 16)
                if rows_out:
                    sp.wait_ge(stored, 16 * len(rows_out) * (NT // GT))


def phase_route(nc, bank, cst, xT, routerT_in, bias_in, slot_row, slot_far, slot_w, tile_expert, wqk, wo, wqk_rows, vo,
                wqT_in, wq_in, wkvbT_in, wo_in, w_down, weights_loaded, down_in):
    N = NT * E
    ST = SLOT_TILES
    with Memory(nc, "route") as m:
        routerT = m.sb("routerT", [P, KC, E])
        bias = m.sb("bias", [P, E])
        logit = m.sb("logit", [P, NT, E])
        top = m.sb("top", [P, NT, 8])
        shifted = m.sb("shifted", [P, NT, E])
        expo = m.sb("expo", [P, NT, E])
        above = m.sb("above", [P, NT, E])
        tie = m.sb("tie", [P, NT, E])
        n_above = m.sb("n_above", [P, NT])
        room = m.sb("room", [P, NT])
        ones = m.sb("ones", [P, N])
        ties_so_far = m.sb("ties_so_far", [P, 1 + N])
        tie_rank = m.sb("tie_rank", [P, NT, E])
        fits = m.sb("fits", [P, NT, E])
        chosen = m.sb("chosen", [P, NT, E])
        picked = m.sb("picked", [P, NT, E])
        total = m.sb("total", [P, NT])
        rtotal = m.sb("rtotal", [P, NT])
        weight = m.sb("weight", [P, NT, E])
        earlier = m.sb("earlier", [P, NT + 1, E])
        up = m.sb("up", [P, E], I32)
        tiles_i = m.sb("tiles_i", [P, E], I32)
        tiles = m.sb("tiles", [P, E])
        tiles_end = m.sb("tiles_end", [P, E])
        start = m.sb("start", [P, E])
        place_a = m.sb("place_a", [P, NT, E])
        place_b = m.sb("place_b", [P, NT, E])
        key = m.sb("key", [P, NT, E])
        key4 = m.sb("key4", [P, NT, 8])
        match = m.sb("match", [P, 2, NT, E])
        match_w = m.sb("match_w", [P, 2, NT, E])
        place_i = m.sb("place_i", [P, NT, TOPK], I32)
        lo_i = m.sb("lo_i", [P, NT, TOPK], I32)
        hi_i = m.sb("hi_i", [P, NT, TOPK], I32)
        lo = m.sb("lo", [P, NT * TOPK])
        hi = m.sb("hi", [P, NT * TOPK])
        is_lo = m.sb("is_lo", [P, 2, TOPK, P], F32R)
        is_hi = m.sb("is_hi", [P, 4, 3, WIDTH_HOT], F32R)
        held = m.sb("held", [P, 3, NT, TOPK])
        weight_hi = m.sb("weight_hi", [P, NT, TOPK], F32R)
        token1 = m.sb("token1", [P, NT])
        filled = m.sb("filled", [P, ST])
        far = m.sb("far", [P, 1])
        slot_f = m.sb("slot_f", [P, ST])
        slot_e = m.sb("slot_e", [P, ST])
        slot_g = m.sb("slot_g", [P, ST])
        ends = m.sb("ends", [1, ST // 2, E])
        n_ends = m.sb("n_ends", [1, ST])
        HG = 2
        wqT = m.sb("wqT", [P, 2, HG, C])
        wkT = m.sb("wkT", [P, H, LORA])
        wvT = m.sb("wvT", [P, H, 2 * LORA])
        rope_loaded, wk_loaded, kv_loaded, zero_sb = (m.sem(n) for n in ("rope_loaded", "wk_loaded", "kv_loaded", "zero_sb"))
        wq_loaded = [m.sem(f"wq_loaded{s}") for s in range(2)]
        a_mm, a_sb, vo_mm, vo_sb, stored = (m.sem(n) for n in ("a_mm", "a_sb", "vo_mm", "vo_sb", "stored"))
        loaded, logit_mm, place_sb, dve_sb, count_mm, hot_sb, lo_sb, slot_mm = (
            m.sem(n) for n in ("loaded", "logit_mm", "place_sb", "dve_sb", "count_mm", "hot_sb", "lo_sb", "slot_mm"))
        expo_sb, shifted_sb, chosen_sb, spread_sb, lo4_sb = (
            m.sem(n) for n in ("expo_sb", "shifted_sb", "chosen_sb", "spread_sb", "lo4_sb"))
        logit_ps = bank[:, 0, 0:N]
        rank_ps = bank[:, 1, 0:N]
        tally_ps = bank[:, 2, 0:N]
        slot_ps = bank[:, 3, 0:3 * WIDTH_HOT]
        by_e = lambda a: a.rearrange("p (t e) -> p t e", e=E)
        over_e = lambda a: a.unsqueeze(2).to_broadcast([P, NT, E])

        with nc.Block() as block:
            @block.sync
            def _(sp):
                sp.dma_start(routerT[:], routerT_in.rearrange("(k p) e -> p k e", p=P)).then_inc(loaded, 16)
                sp.dma_start(bias[:], bias_in.partition_broadcast(P)).then_inc(loaded, 16)
                kvT = wkvbT_in.rearrange("(h x) l -> x h l", x=NOPE + VD)
                nopeT = wqT_in.rearrange("(h x) c -> x h c", x=QH)
                sp.dma_start(wkT[:], kvT[0:NOPE]).then_inc(wk_loaded, 16)
                for g in range(2):
                    sp.dma_start(wqT[:, g], nopeT[0:NOPE, g * HG:(g + 1) * HG]).then_inc(wq_loaded[g], 16)
                sp.wait_ge(zero_sb, 1)
                for odd in range(2):
                    sp.dma_start(wvT[:].rearrange("p (n two) x -> p two n x", two=2)[:, odd, :, odd * LORA:(odd + 1) * LORA],
                                 kvT.rearrange("x (n two) l -> x two n l", two=2)[NOPE:NOPE + VD, odd]).then_inc(kv_loaded, 16)
                sp.dma_start(wo[:], wo_in.rearrange("(h v) c -> v h c", v=VD)).then_inc(kv_loaded, 16)
                for k in range(KC):
                    sp.dma_start(wqk[:, k].rearrange("p (h x) -> p h x", h=H)[:, :, LORA:2 * LORA],
                                 wq_in[k * P:(k + 1) * P, :].rearrange("p (h x) -> p h x", h=H)[:, :, NOPE:QH]
                                 ).then_inc(rope_loaded, 16)
                sp.dma_start(w_down[:].rearrange("p (e k n) -> p e k n", e=E, k=2),
                             down_in.rearrange("e (k p) n -> p e k n", p=IH)).then_inc(weights_loaded, 16)
                for g in range(2, H // HG):
                    sp.wait_ge(a_mm, g - 1)
                    sp.dma_start(wqT[:, g % 2], nopeT[0:NOPE, g * HG:(g + 1) * HG]).then_inc(wq_loaded[g % 2], 16)
                sp.wait_ge(rope_loaded, 16 * KC)
                sp.wait_ge(a_sb, H // HG)
                for k in range(KC):
                    sp.dma_start(wqk_rows.rearrange("n p k x -> p k n x")[:, k],
                                 wqk[:, k].rearrange("p (n x) -> p n x", x=2 * P)).then_inc(stored, 16)
                sp.wait_ge(stored, 16 * KC)

            @block.tensor
            def _(pe):
                def fold_keys(g):
                    pe.wait_ge(wk_loaded, 16)
                    pe.wait_ge(wq_loaded[g % 2], 16 * (g // 2 + 1))
                    if g >= 2:
                        pe.wait_ge(a_sb, g - 1)
                    for k in range(KC):
                        for i in range(HG):
                            mm = nc.tensor.matmul(bank[:, 4 + g % 2, (k * HG + i) * LORA:(k * HG + i + 1) * LORA],
                                                  wqT[:, g % 2, i, k * P:(k + 1) * P], wkT[:, g * HG + i, :],
                                                  start=True, stop=True)
                    mm.then_inc(a_mm, 1)

                def fold_values(n):
                    pe.wait_ge(kv_loaded, 16 * 3)
                    if n >= 2:
                        pe.wait_ge(vo_sb, n - 1)
                    for odd in range(2):
                        mm = nc.tensor.matmul(bank[:, 6 + n % 2, 0:C], wvT[:, 2 * n + odd, :], wo[:, 2 * n + odd, :],
                                              start=odd == 0, stop=odd == 1)
                    mm.then_inc(vo_mm, 1)

                pe.wait_ge(loaded, 32)
                for t in range(NT):
                    for k in range(KC):
                        mm = nc.tensor.matmul(logit_ps[:, t * E:(t + 1) * E], xT[:, k, t * P:(t + 1) * P], routerT[:, k, :],
                                              start=k == 0, stop=k == KC - 1)
                mm.then_inc(logit_mm, 1)
                pe.wait_ge(chosen_sb, 1)
                flat = chosen[:].rearrange("p t e -> p (t e)")
                nc.tensor.matmul(rank_ps, cst["before"], flat, start=True, stop=True)
                nc.tensor.matmul(tally_ps, ones[:, 0:P], flat, start=True, stop=True).then_inc(count_mm, 1)
                for n in range(NT * TOPK):
                    t, k = divmod(n, TOPK)
                    if t % 4 == 3:
                        pe.wait_ge(lo4_sb, t // 4 + 1)
                    else:
                        pe.wait_ge(lo_sb, n + 1 - t // 4 * TOPK)
                    pe.wait_ge(hot_sb, n + 1)
                    nc.tensor.matmul(slot_ps, is_lo[:, t % 2, k, :], is_hi[:, n % 4].rearrange("p a s -> p (a s)"),
                                     start=n == 0, stop=n == NT * TOPK - 1).then_inc(slot_mm, 1)
                    if n % 8 == 1:
                        fold_keys(n // 8)
                    if n % 8 == 5:
                        fold_values(n // 8)

            @block.scalar
            def _(act):
                act.wait_ge(shifted_sb, 1)
                nc.scalar.activation(expo[:], shifted[:], ACT.Exp).then_inc(expo_sb, 1)
                for g in range(H // HG):
                    act.wait_ge(a_mm, g + 1)
                    for k in range(KC):
                        ins = nc.scalar.copy(
                            wqk[:, k].rearrange("p (h x) -> p h x", h=H)[:, g * HG:(g + 1) * HG, 0:LORA],
                            bank[:, 4 + g % 2, k * HG * LORA:(k + 1) * HG * LORA].rearrange("p (h x) -> p h x", h=HG))
                    ins.then_inc(a_sb, 1)
                    act.wait_ge(vo_mm, g + 1)
                    nc.scalar.copy(vo[:, g, :], bank[:, 6 + g % 2, 0:C]).then_inc(vo_sb, 1)

            @block.gpsimd
            def _(pool):
                nc.gpsimd.memset(wvT[:], 0.0).then_inc(zero_sb, 1)
                token = Count(spread_sb, pool)
                token.up(nc.gpsimd.iota(slot_g[:, 0:NT], pattern=[[P, NT]], base=1, channel_multiplier=1,
                                        allow_small_or_imprecise_dtypes=True))
                token.settle()
                token.up(nc.gpsimd.tensor_copy(token1[:], slot_g[:, 0:NT]))
                pool.wait_ge(place_sb, 1)
                for t in range(NT):
                    if t % 4 == 3:
                        continue
                    if t >= 2:
                        pool.wait_ge(slot_mm, (t - 1) * TOPK)
                    for k in range(TOPK):
                        n = t * TOPK + k
                        nc.gpsimd.tensor_scalar(is_lo[:, t % 2, k, :], cst["iota"], lo[:, n:n + 1], None,
                                                ALU.is_equal).then_inc(lo_sb, 1)

            @block.vector
            def _(dve):
                step = Count(dve_sb, dve)
                v = nc.vector
                step.up(v.memset(ones[:], 1.0))
                step.up(v.memset(ties_so_far[:, 0:1], 0.0))
                step.up(v.memset(earlier[:, 0, :], 0.0))
                dve.wait_ge(loaded, 32)
                dve.wait_ge(logit_mm, 1)
                step.up(v.tensor_tensor(logit[:], by_e(logit_ps), bias[:].unsqueeze(1).to_broadcast([P, NT, E]), ALU.add))
                step.settle()
                for t in range(NT):
                    step.up(v.max(top[:, t, :], logit[:, t, :]))
                step.settle()
                v.tensor_tensor(shifted[:], logit[:], over_e(top[:, :, 0]), ALU.subtract).then_inc(shifted_sb, 1)
                fourth = over_e(top[:, :, TOPK - 1])
                step.up(v.tensor_tensor(above[:], logit[:], fourth, ALU.is_gt))
                step.up(v.tensor_tensor(tie[:], logit[:], fourth, ALU.is_equal))
                step.settle()
                step.up(v.tensor_reduce(n_above[:], above[:], AX_X, ALU.add))
                step.up(v.tensor_tensor_scan(ties_so_far[:, 1:1 + N], ones[:], tie[:].rearrange("p t e -> p (t e)"), 0.0,
                                             ALU.mult, ALU.add))
                step.settle()
                step.up(v.tensor_scalar(room[:], n_above[:], -1.0, float(TOPK), ALU.mult, ALU.add))
                step.up(v.tensor_tensor(tie_rank[:], by_e(ties_so_far[:, 1:1 + N]), over_e(by_e(ties_so_far[:, 0:N])[:, :, 0]),
                                        ALU.subtract))
                step.settle()
                step.up(v.tensor_tensor(fits[:], tie_rank[:], over_e(room[:]), ALU.is_le))
                step.settle()
                step.up(v.tensor_tensor(picked[:], fits[:], tie[:], ALU.mult))
                step.settle()
                v.tensor_tensor(chosen[:], picked[:], above[:], ALU.add).then_inc(chosen_sb, 1)
                dve.wait_ge(chosen_sb, 1)
                dve.wait_ge(expo_sb, 1)
                step.up(v.tensor_tensor(fits[:], expo[:], chosen[:], ALU.mult))
                step.settle()
                step.up(v.tensor_reduce(total[:], fits[:], AX_X, ALU.add))
                step.settle()
                step.up(v.reciprocal(rtotal[:], total[:]))
                step.settle()
                step.up(v.tensor_tensor(weight[:], fits[:], over_e(rtotal[:]), ALU.mult))
                dve.wait_ge(count_mm, 1)
                for t in range(NT):
                    step.settle()
                    step.up(v.tensor_tensor(earlier[:, t + 1, :], tally_ps[:, t * E:(t + 1) * E], earlier[:, t, :], ALU.add))
                step.settle()
                step.up(v.tensor_scalar(up[:], earlier[:, NT, :], float(P - 1), None, ALU.add))
                step.settle()
                step.up(v.tensor_scalar(tiles_i[:], up[:], 7, None, ALU.arith_shift_right))
                step.settle()
                step.up(v.tensor_copy(tiles[:], tiles_i[:]))
                step.settle()
                step.up(v.tensor_tensor_scan(tiles_end[:], ones[:, 0:E], tiles[:], 0.0, ALU.mult, ALU.add))
                step.settle()
                step.up(v.tensor_tensor(start[:], tiles_end[:], tiles[:], ALU.subtract))
                step.settle()
                step.up(v.tensor_scalar(start[:], start[:], float(P), 1.0, ALU.mult, ALU.add))
                step.up(v.tensor_tensor(place_a[:], by_e(rank_ps), earlier[:, 0:NT, :], ALU.add))
                step.settle()
                step.up(v.tensor_tensor(place_b[:], place_a[:], start[:].unsqueeze(1).to_broadcast([P, NT, E]), ALU.add))
                step.settle()
                step.up(v.tensor_tensor(key[:], place_b[:], chosen[:], ALU.mult))
                step.settle()
                for t in range(NT):
                    step.up(v.max(key4[:, t, :], key[:, t, :]))
                step.settle()
                step.up(v.tensor_scalar(place_i[:], key4[:, :, 0:TOPK], -1.0, None, ALU.add))
                step.settle()
                step.up(v.tensor_scalar(lo_i[:], place_i[:], P - 1, None, ALU.bitwise_and))
                step.up(v.tensor_scalar(hi_i[:], place_i[:], 7, None, ALU.arith_shift_right))
                step.settle()
                v.tensor_copy(lo[:], lo_i[:].rearrange("p t k -> p (t k)")).then_inc(place_sb, 1)
                step.up(v.tensor_copy(hi[:], hi_i[:].rearrange("p t k -> p (t k)")))
                for k0 in range(0, TOPK, 2):
                    for k in (k0, k0 + 1):
                        step.up(v.tensor_tensor(match[:, k - k0], key[:], over_e(key4[:, :, k]), ALU.is_equal))
                    step.settle()
                    for k in (k0, k0 + 1):
                        step.up(v.tensor_tensor(match_w[:, k - k0], match[:, k - k0], weight[:], ALU.mult))
                    step.settle()
                    for k in (k0, k0 + 1):
                        step.up(v.tensor_reduce(held[:, 1, :, k], match_w[:, k - k0], AX_X, ALU.add))
                    step.settle()
                for t0 in (0, ST // 2):
                    step.up(v.tensor_tensor(ends[:], cst["iota"][0:1, t0:t0 + ST // 2].unsqueeze(2).to_broadcast([1, ST // 2, E]),
                                            tiles_end[0:1, :].unsqueeze(1).to_broadcast([1, ST // 2, E]), ALU.is_ge))
                    step.settle()
                    step.up(v.tensor_reduce(n_ends[:, t0:t0 + ST // 2], ends[:], AX_X, ALU.add))
                    step.settle()
                step.up(v.tensor_scalar(tile_expert[:], n_ends[:], float(E - 1), None, ALU.min))
                dve.wait_ge(spread_sb, 2)
                step.up(v.tensor_copy(held[:, 0], token1[:].unsqueeze(2).to_broadcast([P, NT, TOPK])))
                step.up(v.tensor_copy(weight_hi[:], held[:, 1]))
                step.settle()
                step.up(v.tensor_tensor(held[:, 2], held[:, 1], weight_hi[:].bitcast(F32), ALU.subtract))
                step.settle()
                for n in range(NT * TOPK):
                    t, k = divmod(n, TOPK)
                    if t % 4 == 3 and k == 0:
                        dve.wait_ge(slot_mm, (t - 1) * TOPK)
                        v.tensor_tensor(is_lo[:, t % 2], cst["iota"].unsqueeze(1).to_broadcast([P, TOPK, P]),
                                        lo[:, n:n + TOPK].unsqueeze(2).to_broadcast([P, TOPK, P]),
                                        ALU.is_equal).then_inc(lo4_sb, 1)
                    if n >= 4:
                        dve.wait_ge(slot_mm, n - 3)
                    v.scalar_tensor_tensor(is_hi[:, n % 4], cst["iota"][:, 0:WIDTH_HOT].unsqueeze(1).to_broadcast([P, 3, WIDTH_HOT]),
                                           hi[:, n:n + 1], held[:, :, t, k].unsqueeze(2).to_broadcast([P, 3, WIDTH_HOT]),
                                           ALU.is_equal, ALU.mult).then_inc(hot_sb, 1)
                dve.wait_ge(slot_mm, NT * TOPK)
                slots = slot_ps.rearrange("p (a s) -> p a s", a=3)[:, :, 0:ST]
                step.up(v.tensor_copy(slot_e[:], slots[:, 1]))
                step.settle()
                step.up(v.tensor_tensor(slot_w[:], slots[:, 2], slot_e[:], ALU.add))
                step.up(v.tensor_scalar(slot_f[:], slots[:, 0], -1.0, None, ALU.add))
                step.up(v.tensor_scalar(filled[:], slots[:, 0], 0.5, None, ALU.is_lt))
                step.up(v.tensor_scalar(far[:], cst["row"], float(FAR + 1), None, ALU.add))
                step.settle()
                step.up(v.tensor_scalar(slot_row[:], slot_f[:], 0.0, None, ALU.max))
                step.up(v.tensor_scalar(slot_e[:], filled[:], far[:, 0:1], None, ALU.mult))
                step.settle()
                step.up(v.tensor_tensor(slot_far[:], slot_f[:], slot_e[:], ALU.add))


def phase_experts(nc, bank, cst, w_gu, w_down, weights_loaded, weights_need, x_rows, sums, slot_row, slot_far, slot_w,
                  tile_expert):
    AHEAD = 3
    with Memory(nc, "moe") as m:
        row_at = m.sb("row_at", [P, AHEAD + 1], I32)
        far_at = m.sb("far_at", [P, 2], I32)
        xg = m.sb("xg", [P, AHEAD + 1, C])
        xgT = m.sb("xgT", [P, 2, KC, P])
        gate = m.sb("gate", [P, 2, I])
        hid = m.sb("hid", [P, 2, I])
        hidT = m.sb("hidT", [IH, 2, 2, P])
        y = m.sb("y", [P, 2, C])
        names = ("row_sb", "xT_mm", "xT_sb", "gu_mm", "gate_sb", "hid_sb", "hidT_mm", "hidT_sb", "y_mm", "y_sb", "far_sb")
        row_sb, xT_mm, xT_sb, gu_mm, gate_sb, hid_sb, hidT_mm, hidT_sb, y_mm, y_sb, far_sb = (m.sem(n) for n in names)
        go = m.sem("go")
        gathered = [m.sem(f"gathered{s}") for s in range(AHEAD + 1)]
        added = [m.sem(f"added{s}") for s in range(2)]
        xT_ps = [bank[:, s, 0:KC * P] for s in range(2)]
        gu_ps = [bank[:, 2 + s, 0:2 * I] for s in range(2)]
        hidT_ps = [bank[0:IH, 4 + s, 0:2 * P] for s in range(2)]
        y_ps = [bank[:, 6 + s, 0:C] for s in range(2)]
        ST = SLOT_TILES

        FIRST = 4
        ROUND = 8

        def run(engine, step):
            for r in range(FIRST):
                step(0, r)
            with engine.Fori(0, (ST - 2 * FIRST) // ROUND) as n:
                for i in range(ROUND):
                    step(n * (ROUND // 2), FIRST + i)
            for r in range(ST - FIRST, ST):
                step(0, r)

        def wait(engine, sem, u, r, more):
            if r + more > 0:
                engine.wait_ge(sem, u * 2 + (r + more))

        def wait_dma(engine, sems, u, r, more):
            n = len(sems)
            if r // n + more > 0:
                engine.wait_ge(sems[r % n], u * (32 // n) + 16 * (r // n + more))

        with nc.Block() as block:
            @block.gpsimd
            def _(pool):
                last_row, last_far = pool.to_reg(T - 1), pool.to_reg(FAR + P - 1)

                def gather(u, r):
                    s = r % (AHEAD + 1)
                    wait(pool, xT_mm, u, r, -AHEAD)
                    nc.gpsimd.tensor_copy(row_at[:, s:s + 1], slot_row[:, bass.ds(u * 2 + r, 1)]).then_inc(row_sb, 1)
                    wait(pool, row_sb, u, r, 1)
                    pool.sem_inc(go, 1)
                    nc.gpsimd.indirect_dma_start(xg[:, s, :], None, x_rows,
                                                 bass.IndirectOffsetOnAxis(row_at[:, s:s + 1], 0),
                                                 bounds_check=last_row).then_inc(gathered[s], 16)

                def scatter(u, r):
                    s = r % 2
                    wait_dma(pool, added, u, r, 0)
                    nc.gpsimd.tensor_copy(far_at[:, s:s + 1], slot_far[:, bass.ds(u * 2 + r, 1)]).then_inc(far_sb, 1)
                    wait(pool, far_sb, u, r, 1)
                    wait(pool, y_sb, u, r, 1)
                    pool.sem_inc(go, 1)
                    nc.gpsimd.indirect_dma_start(sums[s], bass.IndirectOffsetOnAxis(far_at[:, s:s + 1], 0), y[:, s, :], None,
                                                 bounds_check=last_far, compute_op=ALU.add).then_inc(added[s], 16)

                def step(u, r):
                    if r + AHEAD < ST:
                        gather(u, r + AHEAD)
                    if r >= 1:
                        scatter(u, r - 1)

                for r in range(AHEAD):
                    gather(0, r)
                run(pool, step)
                scatter(0, ST - 1)
                for s in range(2):
                    pool.wait_ge(added[s], 16 * (ST // 2))

            @block.tensor
            def _(pe):
                def turn_x(u, r):
                    s = r % 2
                    wait_dma(pe, gathered, u, r, 1)
                    wait(pe, xT_sb, u, r, -1)
                    for k in range(KC):
                        mm = nc.tensor.transpose(xT_ps[s][:, k * P:(k + 1) * P], xg[:, r % (AHEAD + 1), k * P:(k + 1) * P],
                                                 cst["ident"])
                    mm.then_inc(xT_mm, 1)

                def expert_of(u, r):
                    return pe.value_load(tile_expert[0:1, bass.ds(u * 2 + r, 1)], min_val=0, max_val=E - 1)

                def gate_up(u, r, e, k):
                    s = r % 2
                    if k == 0:
                        wait(pe, xT_sb, u, r, 1)
                        wait(pe, hid_sb, u, r, -1)
                    mm = nc.tensor.matmul(gu_ps[s], xgT[:, s, k, :], w_gu[:, bass.ds(e * (KC * 2 * I) + k * 2 * I, 2 * I)],
                                          start=k == 0, stop=k == KC - 1)
                    if k == KC - 1:
                        mm.then_inc(gu_mm, 1)

                def turn_hid(u, r):
                    s = r % 2
                    wait(pe, hid_sb, u, r, 1)
                    wait(pe, hidT_sb, u, r, -1)
                    for k in range(2):
                        mm = nc.tensor.transpose(hidT_ps[s][:, k * P:(k + 1) * P], hid[:, s, k * IH:(k + 1) * IH], cst["ident"])
                    mm.then_inc(hidT_mm, 1)

                def down(u, r, e):
                    s = r % 2
                    wait(pe, hidT_sb, u, r, 1)
                    wait(pe, y_sb, u, r, -1)
                    for k in range(2):
                        mm = nc.tensor.matmul(y_ps[s], hidT[:, s, k, :], w_down[:, bass.ds(e * 2 * C + k * C, C)],
                                              start=k == 0, stop=k == 1)
                    mm.then_inc(y_mm, 1)

                expert = {}

                def step(u, r):
                    if r in (FIRST, ST - FIRST):
                        expert[r - 1], expert[r] = expert_of(u, r - 1), expert_of(u, r)
                    gate_up(u, r, expert[r], 0)
                    if r >= 1:
                        turn_hid(u, r - 1)
                    gate_up(u, r, expert[r], 1)
                    if r + 1 < ST:
                        turn_x(u, r + 1)
                        if r != FIRST + ROUND - 1:
                            expert[r + 1] = expert_of(u, r + 1)
                    if r >= 1:
                        down(u, r - 1, expert[r - 1])

                pe.wait_ge(weights_loaded, weights_need)
                turn_x(0, 0)
                expert[0] = expert_of(0, 0)
                run(pe, step)
                turn_hid(0, ST - 1)
                down(0, ST - 1, expert[ST - 1])

            @block.scalar
            def _(act):
                def copy_x(u, r):
                    s = r % 2
                    wait(act, xT_mm, u, r, 1)
                    wait(act, gu_mm, u, r, -1)
                    nc.scalar.copy(xgT[:, s].rearrange("p k m -> p (k m)"), xT_ps[s]).then_inc(xT_sb, 1)

                def silu(u, r):
                    s = r % 2
                    wait(act, gu_mm, u, r, 1)
                    wait(act, hid_sb, u, r, -1)
                    nc.scalar.activation(gate[:, s, :], gu_ps[s][:, 0:I], ACT.Silu).then_inc(gate_sb, 1)

                def copy_y(u, r):
                    s = r % 2
                    wait(act, y_mm, u, r, 1)
                    wait_dma(act, added, u, r, 0)
                    nc.scalar.copy(y[:, s, :], y_ps[s]).then_inc(y_sb, 1)

                def step(u, r):
                    silu(u, r)
                    if r + 1 < ST:
                        copy_x(u, r + 1)
                    if r >= 1:
                        copy_y(u, r - 1)

                copy_x(0, 0)
                run(act, step)
                copy_y(0, ST - 1)

            @block.vector
            def _(dve):
                def multiply(u, r):
                    s = r % 2
                    wait(dve, gate_sb, u, r, 1)
                    wait(dve, hidT_mm, u, r, -1)
                    nc.vector.scalar_tensor_tensor(hid[:, s, :], gu_ps[s][:, I:2 * I], slot_w[:, bass.ds(u * 2 + r, 1)],
                                                   gate[:, s, :], ALU.mult, ALU.mult).then_inc(hid_sb, 1)

                def copy_hid(u, r):
                    s = r % 2
                    wait(dve, hidT_mm, u, r, 1)
                    wait(dve, y_mm, u, r, -1)
                    nc.vector.tensor_copy(hidT[:, s].rearrange("p k m -> p (k m)"), hidT_ps[s]).then_inc(hidT_sb, 1)

                def step(u, r):
                    if r >= 1:
                        copy_hid(u, r - 1)
                    multiply(u, r)

                run(dve, step)
                copy_hid(0, ST - 1)


def phase_collect(nc, z, sums):
    with Memory(nc, "collect") as m:
        odd = m.sb("odd", [P, NT, C])
        loaded = m.sem("loaded")
        G = 4
        with nc.Block() as block:
            @block.sync
            def _(sp):
                for g in range(G):
                    for dst, src in ((z, sums[0]), (odd, sums[1])):
                        sp.dma_start(dst[:, g * NT // G:(g + 1) * NT // G, :],
                                     src[g * T // G:(g + 1) * T // G, :].rearrange("(t p) c -> p t c", p=P)).then_inc(loaded, 16)

            @block.vector
            def _(dve):
                dve.wait_ge(loaded, 16 * 2 * G)
                nc.vector.tensor_tensor(z[:], z[:], odd[:], ALU.add)


def phase_latent(nc, name, bank, cst, xT, x_hl, power, k_hl, v_hl, wkva_in, scale_in, b):
    with Memory(nc, name) as m:
        wkva = m.sb("wkva", [P, KC, P])
        scale = m.sb("scale", [P, LORA])
        raw = m.sb("raw", [P, QT, P])
        square = m.sb("square", [P, QT, LORA])
        meansq = m.sb("meansq", [P, QT])
        sumsq = m.sb("sumsq", [P, QT])
        rrms = m.sb("rrms", [P, QT])
        unit = m.sb("unit", [P, QT, LORA])
        rows = m.sb("rows", [P, QT, P])
        by_cos = m.sb("by_cos", [P, QT, ROPE])
        by_sin = m.sb("by_sin", [P, QT, ROPE])
        ones = m.sb("ones", [P, QT, LORA])
        loaded, raw_mm, raw_sb, step_sb, meansq_sb, rrms_sb, rows_sb, turn_mm, k_sb, ones_sb, x_sb, v_sb = (
            m.sem(n) for n in ("loaded", "raw_mm", "raw_sb", "step_sb", "meansq_sb", "rrms_sb", "rows_sb", "turn_mm",
                               "k_sb", "ones_sb", "x_sb", "v_sb"))
        GT = 4
        G = QT // GT
        half = ROPE // 2
        x_own = xT[:, :, b * S:(b + 1) * S]
        with nc.Block() as block:
            @block.sync
            def _(sp):
                sp.dma_start(wkva[:], wkva_in.rearrange("(k p) n -> p k n", p=P)).then_inc(loaded, 16)
                sp.dma_start(scale[:], scale_in.partition_broadcast(P)).then_inc(loaded, 16)

            @block.gpsimd
            def _(pool):
                nc.gpsimd.memset(ones[:], 1.0).then_inc(ones_sb, 1)
                pool.wait_ge(meansq_sb, 1)
                nc.gpsimd.tensor_tensor(rrms[:], meansq[:], power[:, 0:QT], ALU.pow).then_inc(rrms_sb, 1)
                pool.wait_ge(x_sb, 1)
                nc.gpsimd.tensor_tensor(x_hl[:, 1], x_own, x_hl[:, 0].bitcast(F32), ALU.subtract)

            @block.tensor
            def _(pe):
                pe.wait_ge(loaded, 32)
                for t in range(QT):
                    for k in range(KC):
                        mm = nc.tensor.matmul(bank[:, t // GT, t % GT * P:(t % GT + 1) * P],
                                              xT[:, k, b * S + t * P:b * S + (t + 1) * P], wkva[:, k, :],
                                              start=k == 0, stop=k == KC - 1)
                    if t % GT == GT - 1:
                        mm.then_inc(raw_mm, 1)
                pe.wait_ge(rows_sb, 2)
                for t in range(QT):
                    mm = nc.tensor.transpose(bank[:, 4 + t // GT, t % GT * P:(t % GT + 1) * P], rows[:, t, :], cst["ident"])
                    if t % GT == GT - 1:
                        mm.then_inc(turn_mm, 1)

            @block.scalar
            def _(act):
                nc.scalar.copy(x_hl[:, 0], x_own).then_inc(x_sb, 1)
                act.wait_ge(ones_sb, 1)
                nc.scalar.copy(v_hl[:, 0, :, LORA:P], ones[:]).then_inc(v_sb, 1)
                for g in range(G):
                    act.wait_ge(turn_mm, g + 1)
                    nc.scalar.copy(k_hl[:, 0, g * WIDE:(g + 1) * WIDE], bank[:, 4 + g, :]).then_inc(k_sb, 1)

            @block.vector
            def _(dve):
                v, step = nc.vector, Count(step_sb, dve)
                for g in range(G):
                    dve.wait_ge(raw_mm, g + 1)
                    v.tensor_copy(raw[:, g * GT:(g + 1) * GT, :], bank[:, g, :].rearrange("p (t n) -> p t n", n=P)
                                  ).then_inc(raw_sb, 1)
                dve.wait_ge(raw_sb, G)
                step.up(v.tensor_tensor(square[:], raw[:, :, 0:LORA], raw[:, :, 0:LORA], ALU.mult))
                seq = lambda n: cst[n].rearrange("p (t x) -> p t x", x=ROPE)
                own = raw[:, :, LORA:P]
                step.settle()
                step.up(v.tensor_reduce(sumsq[:], square[:], AX_X, ALU.add))
                step.settle()
                v.tensor_scalar(meansq[:], sumsq[:], 1.0 / LORA, EPS_RMS, ALU.mult, ALU.add).then_inc(meansq_sb, 1)
                step.up(v.tensor_tensor(by_cos[:], own, seq("cos"), ALU.mult))
                for h in range(2):
                    step.up(v.tensor_tensor(by_sin[:, :, h * half:(h + 1) * half], own[:, :, (1 - h) * half:(2 - h) * half],
                                            seq("sin")[:, :, h * half:(h + 1) * half], ALU.mult))
                step.settle()
                step.up(v.tensor_tensor(rows[:, :, LORA:P], by_cos[:], by_sin[:], ALU.add))
                dve.wait_ge(rrms_sb, 1)
                dve.wait_ge(loaded, 32)
                step.up(v.tensor_tensor(unit[:], raw[:, :, 0:LORA], rrms[:].unsqueeze(2).to_broadcast([P, QT, LORA]), ALU.mult))
                step.settle()
                v.tensor_tensor(rows[:, :, 0:LORA], unit[:], scale[:].unsqueeze(1).to_broadcast([P, QT, LORA]),
                                ALU.mult).then_inc(rows_sb, 2)
                dve.wait_ge(rows_sb, 2)
                step.up(v.tensor_copy(v_hl[:, 0, :, 0:LORA], rows[:, :, 0:LORA]))
                dve.wait_ge(v_sb, 1)
                step.up(v.tensor_tensor(v_hl[:, 1, :, LORA:P], ones[:], v_hl[:, 0, :, LORA:P].bitcast(F32), ALU.subtract))
                step.settle()
                step.up(v.tensor_tensor(v_hl[:, 1, :, 0:LORA], rows[:, :, 0:LORA], v_hl[:, 0, :, 0:LORA].bitcast(F32),
                                        ALU.subtract))
                for g in range(G):
                    dve.wait_ge(k_sb, g + 1)
                    step.up(v.tensor_tensor(k_hl[:, 1, g * WIDE:(g + 1) * WIDE], bank[:, 4 + g, :],
                                            k_hl[:, 0, g * WIDE:(g + 1) * WIDE].bitcast(F32), ALU.subtract))


def phase_attention(nc, name, bank, cst, bf, x_hl, wqk_rows, k_hl, v_hl, oT):
    with Memory(nc, name) as m:
        w_raw = m.sb("w_raw", [P, KC, 2 * P])
        w_hl = m.sb("w_hl", [P, 2, KC, 2 * P], F32R)
        rows = m.sb("rows", [P, 2, 2, P])
        by_cos = m.sb("by_cos", [P, 2, 2, ROPE])
        by_sin = m.sb("by_sin", [P, 2, 2, ROPE])
        q_hl = [m.sb(f"q_hl{s}", [P, 2, 2, S], F32R) for s in range(2)]
        peak = m.sb("peak", [P, 2, 2, QT])
        whole = m.sb("whole", [P, 2, QT])
        minus = m.sb("minus", [P, 2, QT, P], BF16)
        prob = m.sb("prob", [P, 2, 2 * WIDE])
        prob_hi = m.sb("prob_hi", [P, 3, 2 * WIDE], F32R)
        prob_lo = m.sb("prob_lo", [P, 3, 2 * WIDE], F32R)
        den = m.sb("den", [P, 2, WIDE])
        rden = m.sb("rden", [P, 2, P])
        (w_loaded, w_hi_sb, w_sb, q_mm, rows_sb, rope_sb, rot_sb, turn_mm, q_hi_sb, q_lo_sb, max_mm, peak_sb, whole_sb,
         minus_sb, s_mm, prob_sb, hi_sb, lo_sb, pv_mm, sums_sb, rden_sb, o_sb) = (m.sem(n) for n in (
             "w_loaded", "w_hi_sb", "w_sb", "q_mm", "rows_sb", "rope_sb", "rot_sb", "turn_mm", "q_hi_sb", "q_lo_sb",
             "max_mm", "peak_sb", "whole_sb", "minus_sb", "s_mm", "prob_sb", "hi_sb", "lo_sb", "pv_mm", "sums_sb",
             "rden_sb", "o_sb"))
        max_ps, pv_ps = [bank[:, n, :] for n in (4, 5)], bank[:, 6, :]
        q_ps, turn_ps = bank[:, 7, 0:2 * P], bank[:, 7, 2 * P:4 * P]
        s_ps = [bank[:, 2 * s:2 * s + 2, :].rearrange("p a n -> p (a n)") for s in range(2)]

        pieces = []
        for i in range(QT):
            end = (i + 1) * P
            cut = 0 if end <= WIDE else WIDE - P if end == WIDE + P else WIDE
            if cut:
                pieces.append((i, 0, 0, cut, False))
            pieces.append((i, 1 if cut else 0, cut, end - cut, True))
        groups = [(qc, [(j, min(max(j * P, qc * WIDE), (qc + 1) * WIDE - 2 * P)) for j in (j0, j0 + 1)])
                  for qc in range(S // WIDE) for j0 in range(0, (qc + 1) * WIDE // P, 2)]
        NG, NP = len(groups), len(pieces)
        LOW = 4
        CHUNKS = S // WIDE
        AHEAD = 2
        HEADS = 4
        ROUNDS = H // HEADS
        PIECES_AT = [(0, 1, 2), (3, 4), (5, 6), (7, 8), (9, 10), (11,)]
        QUARTERS = WIDE // P

        def span(group):
            qc, tiles = group
            end = (qc + 1) * WIDE
            a, z = WIDE - (end - tiles[0][1]), WIDE + end - tiles[1][1]
            return a, z, [(a, WIDE), (WIDE, z)]

        def by_head(engine, sem, u, r, k, more):
            engine.wait_ge(sem, u * (HEADS * k) + (r * k + more + 2 * k))

        def by_pair(engine, sem, u, r, k, more):
            engine.wait_ge(sem, u * (HEADS // 2 * k) + (r * k + more + 2 * k))

        def rounds(engine, step, peel_first=False):
            def steps(u, last):
                for r in range(HEADS):
                    for x in range(NG):
                        more = not (last and r == HEADS - 1)
                        step(u, r, x, more, PIECES_AT[x] if more else (), *made_at(r, x, last))

            if peel_first:
                steps(0, False)
            with engine.Fori(int(peel_first), ROUNDS - 1) as u:
                steps(u, False)
            steps(ROUNDS - 1, True)

        def is_round(u, n):
            return isinstance(u, int) and u == n

        def made_at(r, x, last):
            ahead = r // 2 + 1 if r % 2 == 0 or x == 0 else r // 2 + 2
            t = x + 2 if r % 2 == 0 else {0: QT, 4: 0, 5: 1}.get(x)
            if t is None or last and ahead >= HEADS // 2:
                return None, None
            return (ahead, t) if t < QT else None, (ahead, t - 1) if t else None

        with nc.Block() as block:
            @block.sync
            def _(sp):
                def load(n, u, r):
                    by_pair(sp, w_sb, u, r, 1, 0)
                    sp.dma_start(w_raw[:], wqk_rows[n]).then_inc(w_loaded, 16)

                load(0, 0, 0)
                with sp.Fori(0, ROUNDS - 1) as u:
                    for r in (1, 2):
                        load(u * 2 + r, u, r)
                load(PAIRS - 1, ROUNDS - 1, 1)

            @block.tensor
            def _(pe):
                def queries(u, r, t):
                    by_pair(pe, w_sb, u, r, 1, 1)
                    by_pair(pe, rows_sb, u, r, QT, t)
                    by_pair(pe, q_lo_sb, u, r, QT, max(t - 1, 0))
                    n = 0
                    for xs, ws in ((0, 0), (0, 1), (1, 0)):
                        for k in range(KC):
                            mm = nc.tensor.matmul(q_ps, x_hl[:, xs, k, t * P:(t + 1) * P], w_hl[:, ws, k, :],
                                                  start=n == 0, stop=n == 3 * KC - 1)
                            n += 1
                    mm.then_inc(q_mm, 1)

                def turn(u, r, t):
                    by_pair(pe, rows_sb, u, r, QT, min(t + 2, QT))
                    by_pair(pe, rot_sb, u, r, QT, t + 1)
                    by_pair(pe, q_lo_sb, u, r, QT, t)
                    for i in range(2):
                        mm = nc.tensor.transpose(turn_ps[:, i * P:(i + 1) * P], rows[:, t % 2, i, :], cst["ident"])
                    mm.then_inc(turn_mm, 1)

                def max_piece(u, r, y):
                    i, _, k0, w, diagonal = pieces[y]
                    by_pair(pe, q_hi_sb, u, r // 2, QT, i + 1)
                    by_head(pe, peak_sb, u, r, NP, y - 1)
                    ps = max_ps[y % 2]
                    mm = nc.tensor.matmul(ps[:, 0:w], q_hl[r // 2 % 2][:, 0, r % 2, i * P:(i + 1) * P],
                                          k_hl[:, 0, k0:k0 + w], start=True, stop=not diagonal)
                    if diagonal:
                        mm = nc.tensor.matmul(ps[:, w - P:w], bf["late_q"], bf["ident"], start=False, stop=True)
                    mm.then_inc(max_mm, 1)

                def scores(u, r, x, half):
                    qc, tiles = groups[x]
                    (j, q0), (a, z) = tiles[half], span(groups[x])[2][half]
                    if half == 0:
                        by_pair(pe, q_lo_sb, u, r // 2, QT, QT)
                        by_head(pe, prob_sb, u, r, NG, x - 1)
                        by_head(pe, minus_sb, u, r, CHUNKS, 1 + qc)
                    ps, w = s_ps[x % 2][:, a:z], z - a
                    for n, (ks, qs) in enumerate(((0, 0), (0, 1), (1, 0))):
                        nc.tensor.matmul(ps, k_hl[:, ks, j * P:(j + 1) * P], q_hl[r // 2 % 2][:, qs, r % 2, q0:q0 + w],
                                         start=n == 0, stop=False)
                    if q0 <= j * P:
                        cols = (j + 1) * P - q0
                        nc.tensor.matmul(ps[:, 0:cols], bf["late_k"], bf["late_cols"][:, 2 * P - cols:2 * P],
                                         start=False, stop=False)
                    mm = nc.tensor.matmul(ps, bf["ones"], minus[:, r % 2].rearrange("p i m -> p (i m)")[:, q0:q0 + w],
                                          start=False, stop=True)
                    if half:
                        mm.then_inc(s_mm, 1)

                def values(u, r, x, half):
                    qc, tiles = groups[x]
                    (j, q0), (a, z) = tiles[half], span(groups[x])[2][half]
                    if half == 0:
                        by_head(pe, lo_sb, u, r, NG, x + 1)
                        if j == 0:
                            by_head(pe, sums_sb, u, r, CHUNKS, qc)
                    last = j == (qc + 1) * WIDE // P - 1
                    for n, (vs, part) in enumerate(((0, prob_hi), (1, prob_hi), (0, prob_lo))):
                        mm = nc.tensor.matmul(pv_ps[:, q0 - qc * WIDE:WIDE], v_hl[:, vs, j, :], part[:, x % 3, a:z],
                                              start=j == 0 and n == 0, stop=last and n == 2)
                    if half:
                        mm.then_inc(pv_mm, 1)

                def step(u, r, x, more, peak_pieces, made, turned):
                    ahead = (u, r, x + AHEAD) if x + AHEAD < NG else (u, r + 1, x + AHEAD - NG) if more else None
                    if ahead:
                        scores(*ahead, 0)
                    for y in peak_pieces[:1]:
                        max_piece(u, r + 1, y)
                    if made:
                        queries(u, *made)
                    if ahead:
                        scores(*ahead, 1)
                    for y in peak_pieces[2:]:
                        max_piece(u, r + 1, y - 1)
                    if turned:
                        turn(u, *turned)
                    values(u, r, x, 0)
                    for y in peak_pieces[1:][-1:]:
                        max_piece(u, r + 1, y)
                    values(u, r, x, 1)

                for t in range(QT):
                    queries(0, 0, t)
                    if t:
                        turn(0, 0, t - 1)
                turn(0, 0, QT - 1)
                for y in range(NP):
                    max_piece(0, 0, y)
                queries(0, 1, 0)
                scores(0, 0, 0, 0)
                scores(0, 0, 0, 1)
                queries(0, 1, 1)
                scores(0, 0, 1, 0)
                turn(0, 1, 0)
                scores(0, 0, 1, 1)
                rounds(pe, step)

            @block.scalar
            def _(act):
                def row(u, r, t):
                    by_pair(act, q_mm, u, r, QT, t + 1)
                    by_pair(act, turn_mm, u, r, QT, t - 1)
                    nc.scalar.copy(rows[:, t % 2].rearrange("p h m -> p (h m)"), q_ps).then_inc(rows_sb, 1)

                def q_high(u, r, t):
                    by_pair(act, turn_mm, u, r, QT, t + 1)
                    if t == 0:
                        by_head(act, s_mm, u, 2 * (r - 1), NG, 0)
                    nc.scalar.copy(q_hl[r % 2][:, 0, :, t * P:(t + 1) * P],
                                   turn_ps.rearrange("p (h m) -> p h m", m=P)).then_inc(q_hi_sb, 1)

                def probs(u, r, x):
                    a, z, _ = span(groups[x])
                    by_head(act, s_mm, u, r, NG, x + 1)
                    by_head(act, lo_sb, u, r, NG, x - 1)
                    nc.scalar.activation(prob[:, x % 2, a:z], s_ps[x % 2][:, a:z], ACT.Exp,
                                         scale=SCALE).then_inc(prob_sb, 1)

                def highs(u, r, x):
                    a, z, _ = span(groups[x])
                    by_head(act, prob_sb, u, r, NG, x + 1)
                    by_head(act, pv_mm, u, r, NG, x - 2)
                    nc.scalar.copy(prob_hi[:, x % 3, a:z], prob[:, x % 2, a:z]).then_inc(hi_sb, 1)

                def sums(u, r, qc):
                    n = [y for y in range(NG) if groups[y][0] == qc][-1]
                    half = slice(r % 2 * LORA, (r % 2 + 1) * LORA)
                    by_head(act, pv_mm, u, r, NG, n + 1)
                    by_pair(act, o_sb, u, r // 2, CHUNKS * QUARTERS, (qc + 1 - CHUNKS) * QUARTERS)
                    nc.scalar.copy(den[half, qc, :], pv_ps[LORA:P])
                    nc.scalar.copy(oT[half, bass.ds(u * (HEADS // 2) + r // 2, 1), qc * WIDE:(qc + 1) * WIDE].rearrange(
                        "p a m -> p (a m)"), pv_ps[0:LORA]).then_inc(sums_sb, 1)

                def step(u, r, x, more, peak_pieces, made, turned):
                    if x == 2:
                        sums(u, r, 0)
                    if made:
                        row(u, *made)
                    ahead = (u, r, x + AHEAD) if x + AHEAD < NG else (u, r + 1, x + AHEAD - NG) if more else None
                    if ahead:
                        probs(*ahead)
                    if turned:
                        q_high(u, *turned)
                    if ahead:
                        highs(*ahead)
                    if x == NG - 1:
                        sums(u, r, 1)

                for sem, n in ((rows_sb, QT), (q_hi_sb, QT), (prob_sb, NG), (hi_sb, NG), (sums_sb, CHUNKS)):
                    act.sem_inc(sem, 2 * n)
                for t in range(QT):
                    row(0, 0, t)
                    if t:
                        q_high(0, 0, t - 1)
                q_high(0, 0, QT - 1)
                row(0, 1, 0)
                probs(0, 0, 0)
                highs(0, 0, 0)
                row(0, 1, 1)
                probs(0, 0, 1)
                q_high(0, 1, 0)
                highs(0, 0, 1)
                rounds(act, step)

            @block.gpsimd
            def _(pool):
                def rotated(u, r, t):
                    by_pair(pool, rope_sb, u, r, 3 * QT, 3 * (t + 1))
                    nc.gpsimd.tensor_tensor(rows[:, t % 2, :, LORA:P], by_cos[:, t % 2], by_sin[:, t % 2],
                                            ALU.add).then_inc(rot_sb, 1)

                def low(u, r, x):
                    a, z, _ = span(groups[x])
                    by_head(pool, hi_sb, u, r, NG, x + 1)
                    nc.gpsimd.tensor_tensor(prob_lo[:, x % 3, a:z], prob[:, x % 2, a:z],
                                            prob_hi[:, x % 3, a:z].bitcast(F32), ALU.subtract).then_inc(lo_sb, 1)

                def step(u, r, x, more, peak_pieces, made, turned):
                    if made:
                        rotated(u, *made)
                    if x + AHEAD < NG:
                        low(u, r, x + AHEAD)
                    elif more:
                        low(u, r + 1, x + AHEAD - NG)

                for sem, n in ((rot_sb, QT), (lo_sb, NG)):
                    pool.sem_inc(sem, 2 * n)
                for t in range(QT):
                    rotated(0, 0, t)
                rotated(0, 1, 0)
                low(0, 0, 0)
                rotated(0, 1, 1)
                low(0, 0, 1)
                rounds(pool, step)

            @block.vector
            def _(dve):
                def weights(u, r):
                    by_pair(dve, w_loaded, u, r, 16, 16)
                    by_pair(dve, q_mm, u, r, QT, 0)
                    nc.vector.tensor_copy(w_hl[:, 0], w_raw[:]).then_inc(w_hi_sb, 1)
                    by_pair(dve, w_hi_sb, u, r, 1, 1)
                    nc.vector.tensor_tensor(w_hl[:, 1], w_raw[:], w_hl[:, 0].bitcast(F32), ALU.subtract).then_inc(w_sb, 1)

                def rope(u, r, t):
                    half = ROPE // 2
                    own = rows[:, t % 2, :, LORA:P]
                    at = lambda name: cst[name][:, t * ROPE:(t + 1) * ROPE].unsqueeze(1)
                    by_pair(dve, rows_sb, u, r, QT, t + 1)
                    by_pair(dve, rot_sb, u, r, QT, t - 1)
                    nc.vector.tensor_tensor(by_cos[:, t % 2], own, at("cos").to_broadcast([P, 2, ROPE]),
                                            ALU.mult).then_inc(rope_sb, 1)
                    for h in range(2):
                        nc.vector.tensor_tensor(by_sin[:, t % 2, :, h * half:(h + 1) * half],
                                                own[:, :, (1 - h) * half:(2 - h) * half],
                                                at("sin")[:, :, h * half:(h + 1) * half].to_broadcast([P, 2, half]),
                                                ALU.mult).then_inc(rope_sb, 1)

                def q_low(u, r, t):
                    own = q_hl[r % 2][:, :, :, t * P:(t + 1) * P]
                    by_pair(dve, q_hi_sb, u, r, QT, t + 1)
                    nc.vector.tensor_tensor(own[:, 1], turn_ps.rearrange("p (h m) -> p h m", m=P), own[:, 0].bitcast(F32),
                                            ALU.subtract).then_inc(q_lo_sb, 1)

                def peaks(u, r, y):
                    i, n, _, w, _ = pieces[y]
                    by_head(dve, max_mm, u, r, NP, y + 1)
                    nc.vector.tensor_reduce(peak[:, r % 2, n, i:i + 1], max_ps[y % 2][:, 0:w], AX_X, ALU.max).then_inc(peak_sb, 1)

                def spread(u, r, qc):
                    n = [y for y in range(NP) if pieces[y][0] < LOW * (qc + 1)][-1]
                    by_head(dve, peak_sb, u, r, NP, n + 1)
                    at = slice(qc * LOW, (qc + 1) * LOW)
                    if qc:
                        nc.vector.tensor_tensor(whole[:, r % 2, at], peak[:, r % 2, 0, at], peak[:, r % 2, 1, at],
                                                ALU.max).then_inc(whole_sb, 1)
                    else:
                        nc.vector.tensor_copy(whole[:, r % 2, at], peak[:, r % 2, 0, at]).then_inc(whole_sb, 1)
                    by_head(dve, whole_sb, u, r, CHUNKS, qc + 1)
                    by_head(dve, s_mm, u, r, NG, -NG)
                    nc.vector.scalar_tensor_tensor(minus[:, r % 2, at, :],
                                                   bf["ident"].unsqueeze(1).to_broadcast([P, LOW, P]), -1.0,
                                                   whole[:, r % 2, at].unsqueeze(2).to_broadcast([P, LOW, P]),
                                                   ALU.mult, ALU.mult).then_inc(minus_sb, 1)

                def divide(u, r, qc, n):
                    k, done = CHUNKS * QUARTERS, qc * QUARTERS + n
                    a = qc * WIDE + n * P
                    own = oT[:, bass.ds(u * (HEADS // 2) + r, 1), a:a + P].rearrange("p a m -> p (a m)")
                    by_head(dve, sums_sb, u, 2 * r + 1, CHUNKS, qc + 1)
                    by_pair(dve, o_sb, u, r, k, done - 1)
                    nc.vector.reciprocal(rden[:, n % 2, :], den[:, qc, n * P:(n + 1) * P]).then_inc(rden_sb, 1)
                    by_pair(dve, rden_sb, u, r, k, done + 1)
                    nc.vector.tensor_tensor(own, own, rden[:, n % 2, :], ALU.mult).then_inc(o_sb, 1)

                def step(u, r, x, more, peak_pieces, made, turned):
                    for y in peak_pieces[:1]:
                        peaks(u, r + 1, y)
                    if made:
                        rope(u, *made)
                    for y in peak_pieces[2:]:
                        peaks(u, r + 1, y - 1)
                    if more and x == NG - 1:
                        spread(u, r + 1, 1)
                    if turned:
                        q_low(u, *turned)
                    for y in peak_pieces[1:][-1:]:
                        peaks(u, r + 1, y)
                    if more and x == 1:
                        spread(u, r + 1, 0)
                    if r % 2 and x == 1 and not is_round(u, ROUNDS - 1):
                        weights(u, r // 2 + 2)
                    if r % 2 and x >= 2:
                        divide(u, r // 2, 0, x - 2)
                    if r % 2 == 0 and x < QUARTERS and not (is_round(u, 0) and r == 0):
                        divide(u, r // 2 - 1, 1, x)

                for sem, n in ((w_hi_sb, 1), (w_sb, 1), (rope_sb, 3 * QT), (q_lo_sb, QT), (peak_sb, NP), (whole_sb, CHUNKS),
                               (minus_sb, CHUNKS), (rden_sb, CHUNKS * QUARTERS), (o_sb, CHUNKS * QUARTERS)):
                    dve.sem_inc(sem, 2 * n)
                for sem, n in ((w_loaded, 16), (q_mm, QT), (turn_mm, QT), (max_mm, NP), (s_mm, NG), (pv_mm, NG)):
                    dve.sem_inc(sem, 2 * n)
                weights(0, 0)
                for t in range(QT):
                    rope(0, 0, t)
                    if t:
                        q_low(0, 0, t - 1)
                q_low(0, 0, QT - 1)
                for y in range(NP):
                    peaks(0, 0, y)
                    if y == LOW - 1:
                        spread(0, 0, 0)
                spread(0, 0, 1)
                weights(0, 1)
                rope(0, 1, 0)
                rope(0, 1, 1)
                q_low(0, 1, 0)
                rounds(dve, step, peel_first=True)
                for n in range(QUARTERS):
                    divide(ROUNDS - 1, 1, 1, n)


def phase_output(nc, name, bank, z, x_tok, oT, vo, b):
    with Memory(nc, name) as m:
        y_mm, z_sb = m.sem("y_mm"), m.sem("z_sb")
        with nc.Block() as block:
            @block.tensor
            def _(pe):
                for t in range(QT):
                    if t >= 4:
                        pe.wait_ge(z_sb, t - 3)
                    for n in range(H // 2):
                        mm = nc.tensor.matmul(bank[:, t % 4, 0:C], oT[:, n, t * P:(t + 1) * P], vo[:, n, :],
                                              start=n == 0, stop=n == H // 2 - 1)
                    mm.then_inc(y_mm, 1)

            @block.vector
            def _(dve):
                for t in range(QT):
                    dve.wait_ge(y_mm, t + 1)
                    nc.vector.tensor_tensor(z[:, b * QT + t, :], bank[:, t % 4, 0:C], x_tok[:, b * QT + t, :],
                                            ALU.add).then_inc(z_sb, 1)


def start_ffn_loads(nc, raw, down_raw, loaded, gateT_in, upT_in, downT_in):
    whole = HID // P * P
    with nc.Block() as block:
        @block.sync
        def _(sp):
            for a, src in enumerate((gateT_in, upT_in)):
                for k in range(KC):
                    sp.dma_start(raw[:, a, k, :], src[k * P:(k + 1) * P, :]).then_inc(loaded, 16)
            sp.dma_start(down_raw[:, 0:HID // P, :], downT_in[0:whole, :].rearrange("(n p) c -> p n c", p=P)).then_inc(loaded, 16)
            sp.dma_start(down_raw[0:HID - whole, HID // P, :], downT_in[whole:HID, :]).then_inc(loaded, 16)


def phase_feed_forward(nc, bank, x_hl, x_tok, z, raw, down_raw, raw_loaded, s_gate_in, s_up_in, s_down_in):
    NHT = len(HT)
    with Memory(nc, "ffn") as m:
        w = m.sb("w", [P, 2, KC, HID], F32R)
        down = m.sb("down", [P, NHT, C], F32R)
        s_gate = m.sb("s_gate", [P, NHT])
        s_up = m.sb("s_up", [P, NHT])
        s_down = m.sb("s_down", [P, C])
        gate = m.sb("gated", [P, 2, WIDE])
        hid = m.sb("hid", [P, 2, WIDE])
        hid_hl = m.sb("hid_hl", [P, 2, 2, NHT, WIDE], F32R)
        scaled = m.sb("scaled", [P, 2, C])
        scales, w_sb, down_sb = (m.sem(n) for n in ("scales", "w_sb", "down_sb"))
        gu_mm, gate_sb, hid_sb, hi_sb, lo_sb, y_mm, scaled_sb, z_sb = (
            m.sem(n) for n in ("gu_mm", "gate_sb", "hid_sb", "hi_sb", "lo_sb", "y_mm", "scaled_sb", "z_sb"))
        CT = WIDE // P
        with nc.Block() as block:
            @block.sync
            def _(sp):
                for vec, dst in ((s_gate_in, s_gate), (s_up_in, s_up)):
                    for n, (h0, hw) in enumerate(HT):
                        sp.dma_start(dst[0:hw, n:n + 1], vec[h0:h0 + hw].unsqueeze(1)).then_inc(scales, 16)
                sp.dma_start(s_down[:], s_down_in.partition_broadcast(P)).then_inc(scales, 16)

            @block.tensor
            def _(pe):
                def gate_up(ch):
                    for n, (h0, hw) in enumerate(HT):
                        x = ch * NHT + n
                        if x >= 2:
                            pe.wait_ge(hid_sb, x - 1)
                        for a in range(2):
                            for i in range(2 * KC):
                                part, k = divmod(i, KC)
                                mm = nc.tensor.matmul(bank[0:hw, 2 * (x % 2) + a, :], w[:, a, k, h0:h0 + hw],
                                                      x_hl[:, part, k, ch * WIDE:(ch + 1) * WIDE],
                                                      start=i == 0, stop=i == 2 * KC - 1)
                        mm.then_inc(gu_mm, 1)

                def down_of(ch):
                    pe.wait_ge(lo_sb, (ch + 1) * NHT)
                    for i in range(CT):
                        t = ch * CT + i
                        if t >= 4:
                            pe.wait_ge(z_sb, t - 3)
                        for part in range(2):
                            for n, (h0, hw) in enumerate(HT):
                                mm = nc.tensor.matmul(bank[:, 4 + t % 4, 0:C], hid_hl[0:hw, part, ch % 2, n, i * P:(i + 1) * P],
                                                      down[0:hw, n, :], start=part == 0 and n == 0,
                                                      stop=part == 1 and n == NHT - 1)
                        mm.then_inc(y_mm, 1)

                pe.wait_ge(w_sb, 2)
                for ch in range(NCH):
                    gate_up(ch)
                    if ch == 1:
                        pe.wait_ge(down_sb, 2)
                    if ch:
                        down_of(ch - 1)
                down_of(NCH - 1)

            @block.scalar
            def _(act):
                def high(x):
                    n, ch = x % NHT, x // NHT
                    hw = HT[n][1]
                    act.wait_ge(hid_sb, x + 1)
                    if n == 0 and ch >= 2:
                        act.wait_ge(y_mm, (ch - 1) * CT)
                    nc.scalar.copy(hid_hl[0:hw, 0, ch % 2, n, :], hid[0:hw, x % 2, :]).then_inc(hi_sb, 1)

                act.wait_ge(scales, 16 * (2 * NHT + 1))
                for x in range(NCH * NHT):
                    n = x % NHT
                    hw = HT[n][1]
                    act.wait_ge(gu_mm, x + 1)
                    if x >= 2:
                        act.wait_ge(hid_sb, x - 1)
                    nc.scalar.activation(gate[0:hw, x % 2, :], bank[0:hw, 2 * (x % 2), :], ACT.Silu,
                                         scale=s_gate[0:hw, n:n + 1]).then_inc(gate_sb, 1)
                    if x:
                        high(x - 1)
                high(NCH * NHT - 1)

            @block.gpsimd
            def _(pool):
                for x in range(NCH * NHT):
                    n, ch = x % NHT, x // NHT
                    hw = HT[n][1]
                    pool.wait_ge(hi_sb, x + 1)
                    nc.gpsimd.tensor_tensor(hid_hl[0:hw, 1, ch % 2, n, :], hid[0:hw, x % 2, :],
                                            hid_hl[0:hw, 0, ch % 2, n, :].bitcast(F32), ALU.subtract).then_inc(lo_sb, 1)

            @block.vector
            def _(dve):
                def sum_of(ch):
                    for t in range(ch * CT, (ch + 1) * CT):
                        dve.wait_ge(y_mm, t + 1)
                        nc.vector.tensor_tensor(scaled[:, t % 2, :], bank[:, 4 + t % 4, 0:C], s_down[:],
                                                ALU.mult).then_inc(scaled_sb, 1)
                        dve.wait_ge(scaled_sb, t + 1)
                        nc.vector.tensor_tensor(z[:, t, :], scaled[:, t % 2, :], x_tok[:, t, :], ALU.add).then_inc(z_sb, 1)

                dve.wait_ge(raw_loaded, 16 * 6)
                for a in range(2):
                    nc.vector.tensor_scalar(w[:, a], raw[:, a], -ZERO_POINT, None, ALU.add).then_inc(w_sb, 1)
                whole = HID // P
                nc.vector.tensor_scalar(down[:, 0:whole, :], down_raw[:, 0:whole, :], -ZERO_POINT, None,
                                        ALU.add).then_inc(down_sb, 1)
                rest = HT[whole][1]
                nc.vector.tensor_scalar(down[0:rest, whole, :], down_raw[0:rest, whole, :], -ZERO_POINT, None,
                                        ALU.add).then_inc(down_sb, 1)
                dve.wait_ge(scales, 16 * (2 * NHT + 1))
                for ch in range(NCH):
                    for n, (h0, hw) in enumerate(HT):
                        x = ch * NHT + n
                        dve.wait_ge(gate_sb, x + 1)
                        if x >= 2:
                            dve.wait_ge(lo_sb, x - 1)
                        nc.vector.scalar_tensor_tensor(hid[0:hw, x % 2, :], bank[0:hw, 2 * (x % 2) + 1, :],
                                                       s_up[0:hw, n:n + 1], gate[0:hw, x % 2, :], ALU.mult,
                                                       ALU.mult).then_inc(hid_sb, 1)
                    if ch:
                        sum_of(ch - 1)
                sum_of(NCH - 1)


def phase_start(nc, cst_tile, cst, bf, ones_f, power, table_in, w_gu, w_down, weights_loaded, gate_in, up_in, down_in, zero, sums):
    with Memory(nc, "start") as m:
        loaded, zero_sb, made_sb = m.sem("loaded"), m.sem("zero_sb"), m.sem("made_sb")
        with nc.Block() as block:
            @block.sync
            def _(sp):
                sp.dma_start(cst_tile[:], table_in).then_inc(loaded, 16)
                sp.wait_ge(loaded, 16)

            @block.gpsimd
            def _(pool):
                nc.gpsimd.memset(power[:], -0.5).then_inc(made_sb, 1)
                nc.gpsimd.memset(bf["ones"], 1.0).then_inc(made_sb, 1)

            @block.vector
            def _(dve):
                nc.vector.memset(zero[:], 0.0).then_inc(zero_sb, 1)
                dve.wait_ge(loaded, 16)
                for name in ("ident", "late_q", "late_k", "late_cols"):
                    nc.vector.tensor_copy(bf[name], cst[name])


def program(nc, x, xT_in, wqkvT, wprojT, bproj, routerT, rbias, gate, up, down, wqT, wq, wkva, wkvbT, wo, kvscale,
            gateT, s_gate, upT, s_up, downT, s_down, table, out):
    x_rows = nc.dram_tensor("x_rows", (T, C), F32).ap()
    wqk_rows = nc.dram_tensor("wqk_rows", (PAIRS, P, KC, 2 * P), F32).ap()
    sums = [nc.dram_tensor(f"sums{s}", (FAR + P, C), F32).ap() for s in range(2)]
    with Memory(nc, "all") as m:
        bank = m.ps("bank", [P, 8, WIDE])
        at, width = const_columns()
        cst_tile = m.sb("cst", [P, width])
        cst = {n: cst_tile[:, a:z] for n, (a, z) in at.items()}
        bft = m.sb("bf", [P, 6, P], BF16)
        bf = {n: bft[:, i, :] for i, n in enumerate(("ident", "ones", "late_q", "late_k"))}
        bf["late_cols"] = bft[:, 4:6, :].rearrange("p a m -> p (a m)")
        power = m.sb("power", [P, NT])
        x_tok = m.sb("x_tok", [P, NT, C])
        xT = m.sb("xT", [P, KC, T])
        vo = m.sb("vo", [P, PAIRS, C])
        with Memory(nc, "early") as me:
            z = me.sb("z", [P, NT, C])
            weights_loaded = me.sem("weights_loaded")
            with Memory(nc, "zeros") as mz:
                zero = mz.sb("zero", [P, C])
                phase_start(nc, cst_tile, cst, bf, None, power, table, None, None, None, None, None, None, zero, sums)
                zeroed = mz.sem("zeroed")
                with nc.Block() as block:
                    @block.sync
                    def _(sp):
                        for n in range(FAR // P + 1):
                            sp.dma_start(sums[1][n * P:(n + 1) * P, :], zero[:]).then_inc(zeroed, 16)
                        sp.dma_start(sums[0][FAR:FAR + P, :], zero[:]).then_inc(zeroed, 16)
                        sp.wait_ge(zeroed, 16 * (FAR // P + 2))
            w_gu = me.sb("w_gu", [P, E * KC * 2 * I])
            phase_linear_attention(nc, bank, cst, x_tok, xT, z, x, xT_in, wqkvT, wprojT, bproj, w_gu, weights_loaded, gate, up)
            phase_layernorm(nc, "ln1", bank, cst, z, x_tok, xT, [x_rows, sums[0]])
            slot_row = me.sb("slot_row", [P, SLOT_TILES], I32)
            slot_far = me.sb("slot_far", [P, SLOT_TILES], I32)
            slot_w = me.sb("slot_w", [P, SLOT_TILES])
            tile_expert = me.sb("tile_expert", [1, SLOT_TILES], I32)
            w_down = me.sb("w_down", [IH, E * 2 * C])
            phase_route(nc, bank, cst, xT, routerT, rbias, slot_row, slot_far, slot_w, tile_expert,
                        z[:].rearrange("p (k t) c -> p k (t c)", k=KC), x_tok, wqk_rows, vo, wqT, wq, wkvbT, wo,
                        w_down, weights_loaded, down)
            phase_experts(nc, bank, cst, w_gu, w_down, weights_loaded, 16 * (2 * E + 1), x_rows, sums, slot_row, slot_far,
                          slot_w, tile_expert)
            phase_collect(nc, z, sums)
            phase_layernorm(nc, "ln2", bank, cst, z, x_tok, xT, [])
        with Memory(nc, "late") as ml:
            x_hl = ml.sb("x_hl", [P, 2, KC, S], F32R)
            k_hl = ml.sb("k_hl", [P, 2, S], F32R)
            v_hl = ml.sb("v_hl", [P, 2, QT, P], F32R)
            oT = ml.sb("oT", [P, PAIRS, S])
            for b in range(B):
                phase_latent(nc, f"latent{b}", bank, cst, xT, x_hl, power, k_hl, v_hl, wkva, kvscale, b)
                phase_attention(nc, f"att{b}", bank, cst, bf, x_hl, wqk_rows, k_hl, v_hl, oT)
                phase_output(nc, f"out{b}", bank, x_tok, x_tok, oT, vo, b)
        with Memory(nc, "last") as ml:
            z = ml.sb("z", [P, NT, C])
            x_hl = ml.sb("x_hl", [P, 2, KC, T], F32R)
            raw = ml.sb("raw", [P, 2, KC, HID], I32)
            down_raw = ml.sb("down_raw", [P, len(HT), C], I32)
            raw_loaded = ml.sem("raw_loaded")
            start_ffn_loads(nc, raw, down_raw, raw_loaded, gateT, upT, downT)
            phase_layernorm(nc, "ln3", bank, cst, x_tok, z, None, [], x_hl)
            phase_feed_forward(nc, bank, x_hl, z, x_tok, raw, down_raw, raw_loaded, s_gate, s_up, s_down)
            phase_layernorm(nc, "ln4", bank, cst, x_tok, z, None, [out])


def kernel(**a):
    import concourse.bacc as bacc
    from concourse.bass_utils import run_bass_kernel_spmd

    x = np.asarray(a["L0_attn_x"]).reshape(T, C)
    turned = lambda n: np.asarray(a[n]).T
    ins = {
        "x": x, "xT": x.T, "wqkvT": turned("L0_attn_w_qkv"), "wprojT": turned("L0_attn_w_proj"), "bproj": a["L0_attn_b_proj"],
        "routerT": turned("L0_ffn_router_w"), "rbias": a["L0_ffn_expert_bias"], "gate": a["L0_ffn_gate_proj"],
        "up": a["L0_ffn_up_proj"], "down": a["L0_ffn_down_proj"], "wqT": turned("L1_attn_wq"), "wq": a["L1_attn_wq"],
        "wkva": a["L1_attn_wkv_a"], "wkvbT": turned("L1_attn_wkv_b"), "wo": a["L1_attn_wo"],
        "kvscale": a["L1_attn_kv_norm_scale"], "gateT": turned("L1_ffn_wq_gate"), "s_gate": a["L1_ffn_s_gate"],
        "upT": turned("L1_ffn_wq_up"), "s_up": a["L1_ffn_s_up"], "downT": turned("L1_ffn_wq_down"),
        "s_down": a["L1_ffn_s_down"], "table": const_table(),
    }
    nc = bacc.Bacc("TRN2", target_bir_lowering=False, num_devices=1)
    arrays, aps = {}, []
    for name, v in ins.items():
        v = np.ascontiguousarray(v)
        arrays[f"in_{name}"] = v
        aps.append(nc.dram_tensor(f"in_{name}", v.shape, mybir.dt.from_np(v.dtype), kind="ExternalInput").ap())
    out = nc.dram_tensor("out_x", (T, C), F32, kind="ExternalOutput").ap()
    program(nc, *aps, out)
    r = run_bass_kernel_spmd(nc, [arrays], core_ids=[0])
    return r.results[0]["out_x"].reshape(B, S, C)
```

```python
from contextlib import ExitStack

import numpy as np

import concourse.bass as bass
from concourse import mybir

F32 = mybir.dt.float32
F32R = mybir.dt.float32r
BF16 = mybir.dt.bfloat16
I32 = mybir.dt.int32
U32 = mybir.dt.uint32
ALU = mybir.AluOpType
ACT = mybir.ActivationFunctionType
AX_X = mybir.AxisListType.X

P = 128
B, S, C = 2, 1024, 256
T = B * S
NT = T // P
KC = C // P
WIDE = 512
NCH = T // WIDE
EPS_LN = 1e-5

EPS_DEN = 1e-15
HD = 32

E, TOPK, I = 16, 4, 224
IH = I // 2
SLOT_TILES = T * TOPK // P + E - 1
WIDTH_HOT = 86
FAR = 2048

H, NOPE, ROPE, VD, LORA = 16, 128, 64, 128, 64
QH = NOPE + ROPE
SCALE = QH ** -0.5
EPS_RMS = 1e-6
QT = S // P
PAIRS = H // 2
MASKED = -1e30

HID = 704
ZERO_POINT = 128.0
HT = [(n * P, min(P, HID - n * P)) for n in range((HID + P - 1) // P)]


def const_columns():
    at, n = {}, 0
    for name, width in (("ident", P), ("before", P), ("iota", P), ("headmask", P), ("late_q", P), ("late_k", P),
                        ("late_cols", 2 * P), ("row", 1), ("cos", QT * ROPE), ("sin", QT * ROPE)):
        at[name] = (n, n + width)
        n += width
    return at, n


def const_table():
    at, n = const_columns()
    t = np.zeros((P, n), np.float32)
    p, f = np.arange(P)[:, None], np.arange(P)[None, :]

    def put(name, v):
        t[:, at[name][0]:at[name][1]] = v

    put("ident", p == f)
    put("before", p < f)
    put("iota", np.broadcast_to(f, (P, P)))
    put("headmask", p // HD == f // HD)
    put("late_q", np.where(p > f, MASKED, 0.0))
    put("late_k", np.where(f >= p, MASKED, 0.0))
    q = np.arange(2 * P)[None, :] - P
    put("late_cols", p == np.maximum(q + 1, 0))
    put("row", p)
    inv = (np.float32(1.0) / np.float32(10000.0) ** (np.arange(0, ROPE, 2, dtype=np.float32) / np.float32(ROPE)))
    ang = np.arange(S, dtype=np.float32)[:, None] * inv.astype(np.float32)
    cos, sin = np.cos(ang), np.sin(ang)
    lay = lambda a: a.reshape(QT, P, ROPE).transpose(1, 0, 2).reshape(P, QT * ROPE)
    put("cos", lay(np.concatenate([cos, cos], 1)))
    put("sin", lay(np.concatenate([-sin, sin], 1)))
    return t


class Memory:

    def __init__(self, nc, name):
        self.nc, self.name, self.stack, self.sems = nc, name, ExitStack(), []

    def __enter__(self):
        return self

    def __exit__(self, *a):
        if self.sems and a[0] is None:
            self.nc.clear_and_free_semaphores(self.sems)
            self.nc.all_engine_barrier(sem_only=True)
        return self.stack.__exit__(*a)

    def sb(self, name, shape, dt=F32):
        return self.stack.enter_context(self.nc.sbuf_tensor(f"{self.name}_{name}", shape, dt))

    def ps(self, name, shape, dt=F32):
        return self.stack.enter_context(self.nc.psum_tensor(f"{self.name}_{name}", shape, dt))

    def sem(self, name):
        self.sems.append(self.nc.alloc_semaphore(f"{self.name}_{name}"))
        return self.sems[-1]


class Count:

    def __init__(self, sem, engine):
        self.sem, self.engine, self.n = sem, engine, 0

    def up(self, ins):
        ins.then_inc(self.sem, 1)
        self.n += 1

    def settle(self):
        self.engine.wait_ge(self.sem, self.n)


def phase_linear_attention(nc, bank, cst_tile, table_in, cst, bf, x_tok, xT, z, x_in, xT_in, wqkvT_in, wprojT_in,
                           bproj_in, w_gu, weights_loaded, logit_ps, gate_in, up_in, zero, sums, power, x_rows, router_w,
                           router_b, router_loaded, routerT_in, bias_in, zeroed, rows_stored):
    LATE = 5
    PASSES = ((0, 0), (1, 0), (0, 1))
    PER = P // HD
    NUM = P + PER
    with Memory(nc, "lin") as m:
        wqkvT = m.sb("wqkvT", [P, KC, 3 * C])
        bproj = m.sb("bproj", [P, C])
        w_hl = m.sb("w_hl", [P, 2, KC, 3 * C], F32R)
        x_hl = m.sb("x_hl", [P, 2, 2, KC, WIDE], F32R)
        wprojT = m.sb("wprojT", [P, KC, C])
        kmat = m.sb("kmat", [P, NT, C])
        vones = m.sb("vones", [P, NT, KC, P + 1])
        qT = xT
        vk = m.sb("vk", [P, B * KC, NUM])
        norm = LayerNorm(nc, m, z, x_tok, power, 0, NT, 2)
        dens = m.sb("dens", [P, 2, KC, PER])
        rec = m.sb("rec", [P, 2, KC, PER])
        a_tok = m.sb("a_tok", [P, 2, KC, PER, HD])
        aT = m.sb("aT", [P, 2, KC, P])
        loaded_w = [m.sem(f"loaded_w{n}") for n in range(2)]
        loaded_wp, loaded_x, loaded_cst, zero_sb = (
            m.sem(n) for n in ("loaded_wp", "loaded_x", "loaded_cst", "zero_sb"))
        loaded_xT = [m.sem(f"loaded_xT{ch}") for ch in range(NCH)]
        w_hi_sb, w_lo_sb, x_hi_sb, x_lo_sb = (m.sem(n) for n in ("w_hi_sb", "w_lo_sb", "x_hi_sb", "x_lo_sb"))
        kv_mm, k_sb, v_sb, q_mm, q_sb = (m.sem(n) for n in ("kv_mm", "k_sb", "v_sb", "q_mm", "q_sb"))
        W_PARTS = (slice(C, 3 * C), slice(0, C))
        CT = WIDE // P
        vk_mm, vk_sb, nd_mm, den_sb, rec_sb, a_sb = (m.sem(n) for n in ("vk_mm", "vk_sb", "nd_mm", "den_sb", "rec_sb", "a_sb"))
        turn_mm, aT_sb, y_mm, z_sb, xb_sb, ones_sb, xT_mm, xT_sb = (
            m.sem(n) for n in ("turn_mm", "aT_sb", "y_mm", "z_sb", "xb_sb", "ones_sb", "xT_mm", "xT_sb"))
        xT_ps = bank[:, 4, :]
        kv_ps = [bank[:, n, :] for n in (0, 1)]
        q_ps = [bank[:, n, :] for n in (2, 3)]
        vk_ps = [bank[:, n, :] for n in (4, 5)]
        nd_ps = [bank[:, n, 0:KC * NUM].rearrange("p (g n) -> p g n", g=KC) for n in (0, 1)]
        turn_ps = [bank[:, n, 0:C] for n in (2, 3)]
        y_ps = [bank[:, n, :] for n in (6, 7)]

        with nc.Block() as block:
            @block.sync
            def _(sp):
                for ch in range(NCH):
                    at = slice(ch * WIDE, (ch + 1) * WIDE)
                    sp.dma_start(xT[:, :, at], xT_in.rearrange("(k p) t -> p k t", p=P)[:, :, at]).then_inc(loaded_xT[ch], 16)
                sp.dma_start(cst_tile[:], table_in).then_inc(loaded_cst, 16)
                sp.dma_start(x_tok[:], x_in.rearrange("(t p) c -> p t c", p=P)).then_inc(loaded_x, 16)
                sp.dma_start(bproj[:], bproj_in.partition_broadcast(P)).then_inc(loaded_x, 16)
                sp.dma_start(router_w[:], routerT_in.rearrange("(k p) e -> p k e", p=P)).then_inc(router_loaded, 16)
                sp.dma_start(router_b[:], bias_in.partition_broadcast(P)).then_inc(router_loaded, 16)
                sp.wait_ge(zero_sb, 1)
                for n in range(FAR // P + 1):
                    sp.dma_start(sums[1][n * P:(n + 1) * P, :], zero[:]).then_inc(zeroed, 16)
                sp.dma_start(sums[0][FAR:FAR + P, :], zero[:]).then_inc(zeroed, 16)
                gu = w_gu[:].rearrange("p (e k n) -> p e k n", e=E, k=KC)
                for e in range(E):
                    for a, src in enumerate((gate_in, up_in)):
                        sp.dma_start(gu[:, e, :, a * I:(a + 1) * I], src[e].rearrange("(k p) n -> p k n", p=P)
                                     ).then_inc(weights_loaded, 16)
                for g in range(NCH):
                    sp.wait_ge(norm.x_sb, (g + 1) * NT // NCH)
                    at = slice(g * NT // NCH, (g + 1) * NT // NCH)
                    for r in (x_rows, sums[0]):
                        sp.dma_start(r[0:T, :].rearrange("(t p) c -> p t c", p=P)[:, at, :], x_tok[:, at, :]
                                     ).then_inc(rows_stored, 16)

            @block.gpsimd
            def _(pool):
                nc.gpsimd.memset(vones[:, :, :, P:P + 1], 1.0).then_inc(ones_sb, 1)
                nc.gpsimd.memset(zero[:], 0.0).then_inc(zero_sb, 1)
                nc.gpsimd.memset(power[:], -0.5).then_inc(ones_sb, 1)
                nc.gpsimd.memset(bf["ones"], 1.0)
                pool.wait_ge(loaded_x, 32)
                nc.gpsimd.tensor_tensor(x_tok[:], x_tok[:], bproj[:].unsqueeze(1).to_broadcast([P, NT, C]),
                                        ALU.add).then_inc(xb_sb, 1)
                pool.wait_ge(ones_sb, 2)
                for g in range(norm.groups):
                    norm.deviations(pool, g)

            @block.tensor
            def _(pe):
                for ch in range(NCH):
                    for i in range(CT):
                        t = ch * CT + i
                        if t >= 2:
                            pe.wait_ge(k_sb, t - 1)
                            pe.wait_ge(v_sb, t - 1)
                        for n, (xs, ws) in enumerate(PASSES):
                            if t == 0:
                                pe.wait_ge(w_lo_sb if ws else w_hi_sb, 1)
                            if i == 0:
                                pe.wait_ge(x_lo_sb if xs else x_hi_sb, ch + 1)
                            for k in range(KC):
                                mm = nc.tensor.matmul(kv_ps[t % 2], x_hl[:, ch % 2, xs, k, i * P:(i + 1) * P],
                                                      w_hl[:, ws, k, C:3 * C], start=n == 0 and k == 0,
                                                      stop=n == len(PASSES) - 1 and k == KC - 1)
                        mm.then_inc(kv_mm, 1)
                    pe.wait_ge(w_lo_sb, 2)
                    for g in range(KC):
                        if ch:
                            pe.wait_ge(q_sb, KC * (ch - 1) + g + 1)
                        for n, (xs, ws) in enumerate(PASSES):
                            for k in range(KC):
                                mm = nc.tensor.matmul(q_ps[g], w_hl[:, ws, k, g * P:(g + 1) * P], x_hl[:, ch % 2, xs, k, :],
                                                      start=n == 0 and k == 0, stop=n == len(PASSES) - 1 and k == KC - 1)
                        mm.then_inc(q_mm, 1)
                pe.wait_ge(k_sb, NT)
                pe.wait_ge(v_sb, NT)
                pe.wait_ge(ones_sb, 1)
                for n in range(B * KC):
                    b, g = divmod(n, KC)
                    if n >= 2:
                        pe.wait_ge(vk_sb, 2 * (n - 1))
                    for i in range(QT):
                        t = b * QT + i
                        mm = nc.tensor.matmul(vk_ps[n % 2][:, 0:P + 1], kmat[:, t, g * P:(g + 1) * P],
                                              vones[:, t, g, :], start=i == 0, stop=i == QT - 1)
                    mm.then_inc(vk_mm, 1)
                pe.wait_ge(q_sb, KC * NCH)
                pe.wait_ge(loaded_wp, 16)
                pe.wait_ge(loaded_cst, 16)
                pe.wait_ge(router_loaded, 32)

                def logits(g):
                    pe.wait_ge(xT_sb, g + 1)
                    for t in (2 * g, 2 * g + 1):
                        for k in range(KC):
                            nc.tensor.matmul(logit_ps[:, t, :], xT[:, k, t * P:(t + 1) * P], router_w[:, k, :],
                                             start=k == 0, stop=k == KC - 1)

                def turn_x(g):
                    if g:
                        logits(g - 1)
                    for k in range(KC):
                        for t in (2 * g, 2 * g + 1):
                            pe.wait_ge(norm.x_sb, t + 1)
                            mm = nc.tensor.transpose(xT_ps[:, (2 * k + t % 2) * P:(2 * k + t % 2 + 1) * P],
                                                     x_tok[:, t, k * P:(k + 1) * P], cst["ident"])
                    mm.then_inc(xT_mm, 1)

                for i in range(NT + 2):
                    if i < NT:
                        pe.wait_ge(vk_sb, 2 * KC * (i // QT + 1))
                        if i >= 2:
                            pe.wait_ge(a_sb, i - 1)
                        for g in range(KC):
                            mm = nc.tensor.matmul(nd_ps[i % 2][:, g], qT[:, g, i * P:(i + 1) * P], vk[:, i // QT * KC + g, :],
                                                  start=True, stop=True)
                        mm.then_inc(nd_mm, 1)
                    if 1 <= i <= NT:
                        t = i - 1
                        pe.wait_ge(a_sb, t + 1)
                        if t >= 2:
                            pe.wait_ge(aT_sb, t - 1)
                        for g in range(KC):
                            mm = nc.tensor.transpose(turn_ps[t % 2][:, g * P:(g + 1) * P],
                                                     a_tok[:, t % 2, g].rearrange("p h d -> p (h d)"), cst["ident"])
                        mm.then_inc(turn_mm, 1)
                    if i >= 2:
                        t = i - 2
                        pe.wait_ge(aT_sb, t + 1)
                        if t >= 2:
                            pe.wait_ge(z_sb, t - 1)
                        for k in range(KC):
                            mm = nc.tensor.matmul(y_ps[t % 2][:, 0:C], aT[:, t % 2, k, :], wprojT[:, k, :],
                                                  start=k == 0, stop=k == KC - 1)
                        mm.then_inc(y_mm, 1)
                        if t % 2 and t >= LATE:
                            turn_x((t - LATE) // 2)
                for g in range((NT - LATE + 1) // 2, NT // 2):
                    turn_x(g)
                logits(NT // 2 - 1)

            @block.scalar
            def _(act):
                for n, cols in enumerate(W_PARTS):
                    act.dma_start(wqkvT[:, :, cols], wqkvT_in.rearrange("(k p) n -> p k n", p=P)[:, :, cols]).then_inc(
                        loaded_w[n], 16)
                act.dma_start(wprojT[:], wprojT_in.rearrange("(k p) n -> p k n", p=P)).then_inc(loaded_wp, 16)

                def w_high(n):
                    act.wait_ge(loaded_w[n], 16)
                    nc.scalar.copy(w_hl[:, 0, :, W_PARTS[n]], wqkvT[:, :, W_PARTS[n]]).then_inc(w_hi_sb, 1)

                def x_high(ch):
                    act.wait_ge(loaded_xT[ch], 16)
                    if ch >= 2:
                        act.wait_ge(q_mm, KC * (ch - 1))
                    nc.scalar.copy(x_hl[:, ch % 2, 0], xT[:, :, ch * WIDE:(ch + 1) * WIDE]).then_inc(x_hi_sb, 1)

                w_high(0)
                w_high(1)
                for ch in range(NCH):
                    for i in range(CT):
                        t = ch * CT + i
                        act.wait_ge(kv_mm, t + 1)
                        nc.scalar.activation(kmat[:, t, :], kv_ps[t % 2][:, 0:C], ACT.Relu).then_inc(k_sb, 1)
                        if i == 0 and ch + 1 < NCH:
                            x_high(ch + 1)
                    for g in range(KC):
                        act.wait_ge(q_mm, KC * ch + g + 1)
                        nc.scalar.activation(qT[:, g, ch * WIDE:(ch + 1) * WIDE], q_ps[g], ACT.Relu).then_inc(q_sb, 1)

                def copy_x(g):
                    act.wait_ge(xT_mm, g + 1)
                    nc.scalar.copy(xT[:, :, 2 * g * P:2 * (g + 1) * P], xT_ps.rearrange("p (k m) -> p k m", k=KC)
                                   ).then_inc(xT_sb, 1)

                for t in range(NT):
                    act.wait_ge(turn_mm, t + 1)
                    if t >= 2:
                        act.wait_ge(y_mm, t - 1)
                    nc.scalar.copy(aT[:, t % 2].rearrange("p g m -> p (g m)"), turn_ps[t % 2]).then_inc(aT_sb, 1)
                    if t % 2 == 0 and t >= LATE + 1:
                        copy_x((t - LATE - 1) // 2)
                for g in range((NT - LATE) // 2, NT // 2):
                    copy_x(g)

            @block.vector
            def _(dve):
                def w_low(n):
                    dve.wait_ge(w_hi_sb, n + 1)
                    cols = W_PARTS[n]
                    nc.vector.tensor_tensor(w_hl[:, 1, :, cols], wqkvT[:, :, cols], w_hl[:, 0, :, cols].bitcast(F32),
                                            ALU.subtract).then_inc(w_lo_sb, 1)

                def x_low(ch):
                    dve.wait_ge(x_hi_sb, ch + 1)
                    nc.vector.tensor_tensor(x_hl[:, ch % 2, 1], xT[:, :, ch * WIDE:(ch + 1) * WIDE],
                                            x_hl[:, ch % 2, 0].bitcast(F32), ALU.subtract).then_inc(x_lo_sb, 1)

                dve.wait_ge(loaded_xT[0], 16)
                nc.vector.tensor_copy(x_hl[:, 0, 0], xT[:, :, 0:WIDE]).then_inc(x_hi_sb, 1)
                x_low(0)
                w_low(0)
                w_low(1)
                for t in range(NT):
                    dve.wait_ge(kv_mm, t + 1)
                    dve.wait_ge(k_sb, t + 1)
                    nc.vector.tensor_copy(vones[:, t, :, 0:P],
                                          kv_ps[t % 2][:, C:2 * C].rearrange("p (g c) -> p g c", g=KC)).then_inc(v_sb, 1)
                    ch, i = divmod(t, CT)
                    if i == 1 and ch + 1 < NCH:
                        x_low(ch + 1)
                dve.wait_ge(loaded_cst, 16)
                for name in ("ident", "late_q", "late_k", "late_cols"):
                    nc.vector.tensor_copy(bf[name], cst[name])
                for n in range(B * KC):
                    dve.wait_ge(vk_mm, n + 1)
                    mask = cst["headmask"]
                    nc.vector.tensor_tensor(vk[:, n, 0:P], vk_ps[n % 2][:, 0:P], mask, ALU.mult).then_inc(vk_sb, 1)
                    nc.vector.tensor_scalar(vk[:, n, P:NUM], mask.rearrange("p (h d) -> p h d", d=HD)[:, :, 0],
                                            vk_ps[n % 2][:, P:P + 1], None, ALU.mult).then_inc(vk_sb, 1)
                dve.wait_ge(xb_sb, 1)
                for i in range(NT + 2):
                    if i < NT:
                        dve.wait_ge(nd_mm, i + 1)
                        nc.vector.tensor_scalar(dens[:, i % 2], nd_ps[i % 2][:, :, P:NUM], EPS_DEN, None,
                                                ALU.add).then_inc(den_sb, 1)
                        dve.wait_ge(den_sb, i + 1)
                        nc.vector.reciprocal(rec[:, i % 2], dens[:, i % 2]).then_inc(rec_sb, 1)
                        dve.wait_ge(rec_sb, i + 1)
                        if i >= 2:
                            dve.wait_ge(turn_mm, i - 1)
                        nc.vector.tensor_tensor(a_tok[:, i % 2],
                                                nd_ps[i % 2][:, :, 0:P].rearrange("p g (h d) -> p g h d", d=HD),
                                                rec[:, i % 2].unsqueeze(3).to_broadcast([P, KC, PER, HD]),
                                                ALU.mult).then_inc(a_sb, 1)
                    if i >= 2:
                        t = i - 2
                        dve.wait_ge(y_mm, t + 1)
                        nc.vector.tensor_tensor(z[:, t, :], y_ps[t % 2][:, 0:C], x_tok[:, t, :], ALU.add).then_inc(z_sb, 1)
                        if t % 2:
                            dve.wait_ge(z_sb, t + 1)
                            norm.statistics(dve, t // 2)
                            if t >= 2:
                                norm.normalise(dve, t // 2 - 1)
                norm.normalise(dve, NT // 2 - 1)


class LayerNorm:

    def __init__(self, nc, m, z, x, power, first, count, group):
        self.nc, self.z, self.x, self.power, self.first, self.group = nc, z, x, power, first, group
        self.groups = count // group
        self.stats = m.sb("ln_stats", [P, count, 6])
        self.meanvar = m.sb("ln_meanvar", [P, count, 2])
        self.vareps = m.sb("ln_vareps", [P, count])
        self.rstd = m.sb("ln_rstd", [P, count])
        self.stats_sb, self.mv_sb, self.ve_sb, self.rstd_sb, self.x_sb = (
            m.sem(n) for n in ("ln_stats_sb", "ln_mv_sb", "ln_ve_sb", "ln_rstd_sb", "ln_x_sb"))

    def tiles(self, g):
        return range(g * self.group, (g + 1) * self.group)

    def statistics(self, dve, g):
        for i in self.tiles(g):
            self.nc.vector.bn_stats(self.stats[:, i, :], self.z[:, self.first + i, :]).then_inc(self.stats_sb, 1)
        for i in self.tiles(g):
            dve.wait_ge(self.stats_sb, i + 1)
            self.nc.vector.bn_aggr(self.meanvar[:, i, :], self.stats[:, i, :]).then_inc(self.mv_sb, 1)

    def deviations(self, pool, g):
        at = slice(g * self.group, (g + 1) * self.group)
        pool.wait_ge(self.mv_sb, (g + 1) * self.group)
        self.nc.gpsimd.tensor_scalar(self.vareps[:, at], self.meanvar[:, at, 1], EPS_LN, None, ALU.add).then_inc(self.ve_sb, 1)
        pool.wait_ge(self.ve_sb, g + 1)
        self.nc.gpsimd.tensor_tensor(self.rstd[:, at], self.vareps[:, at], self.power[:, at],
                                     ALU.pow).then_inc(self.rstd_sb, 1)

    def normalise(self, engine, g):
        engine.wait_ge(self.rstd_sb, g + 1)
        for i in self.tiles(g):
            engine.tensor_scalar(self.x[:, self.first + i, :], self.z[:, self.first + i, :], self.meanvar[:, i, 0:1],
                                 self.rstd[:, i:i + 1], ALU.subtract, ALU.mult).then_inc(self.x_sb, 1)


def phase_route(nc, bank, cst, xT, logit_ps, bias, router_loaded, slot_row, slot_far, slot_w, tile_expert, wqk, wo,
                wqk_rows, vo, wqk_stored, wqT_in, wq_in, wkvbT_in, wo_in, w_down, weights_loaded, down_in):
    N = NT * E
    ST = SLOT_TILES
    with Memory(nc, "route") as m:
        logit = m.sb("logit", [P, NT, E])
        top = m.sb("top", [P, NT, 8])
        shifted = m.sb("shifted", [P, NT, E])
        expo = m.sb("expo", [P, NT, E])
        above = m.sb("above", [P, NT, E])
        tie = m.sb("tie", [P, NT, E])
        n_above = m.sb("n_above", [P, NT])
        room = m.sb("room", [P, NT])
        ones = m.sb("ones", [P, N])
        ties_so_far = m.sb("ties_so_far", [P, 1 + N])
        tie_rank = m.sb("tie_rank", [P, NT, E])
        fits = m.sb("fits", [P, NT, E])
        chosen = m.sb("chosen", [P, NT, E])
        picked = m.sb("picked", [P, NT, E])
        total = m.sb("total", [P, NT])
        rtotal = m.sb("rtotal", [P, NT])
        weight = m.sb("weight", [P, NT, E])
        earlier = m.sb("earlier", [P, NT + 1, E])
        up = m.sb("up", [P, E], I32)
        tiles_i = m.sb("tiles_i", [P, E], I32)
        tiles = m.sb("tiles", [P, E])
        tiles_end = m.sb("tiles_end", [P, E])
        start = m.sb("start", [P, E])
        place_a = m.sb("place_a", [P, NT, E])
        place_b = m.sb("place_b", [P, NT, E])
        key = m.sb("key", [P, NT, E])
        key4 = m.sb("key4", [P, NT, 8])
        match = m.sb("match", [P, 2, NT, E])
        match_w = m.sb("match_w", [P, 2, NT, E])
        place_i = m.sb("place_i", [P, NT, TOPK], I32)
        lo_i = m.sb("lo_i", [P, NT, TOPK], I32)
        hi_i = m.sb("hi_i", [P, NT, TOPK], I32)
        lo = m.sb("lo", [P, NT * TOPK])
        hi = m.sb("hi", [P, NT * TOPK])
        is_lo = m.sb("is_lo", [P, 2, TOPK, P], F32R)
        is_hi = m.sb("is_hi", [P, 4, 3, WIDTH_HOT], F32R)
        held = m.sb("held", [P, 3, NT, TOPK])
        weight_hi = m.sb("weight_hi", [P, NT, TOPK], F32R)
        token1 = m.sb("token1", [P, NT])
        empty = m.sb("empty", [P, ST])
        far = m.sb("far", [P, 1])
        slot_f = m.sb("slot_f", [P, ST])
        slot_w_hi = m.sb("slot_w_hi", [P, ST])
        spare = m.sb("spare", [P, ST])
        token1_i = m.sb("token1_i", [P, NT], I32)
        HALF = (ST + 1) // 2
        ends = m.sb("ends", [1, HALF, E])
        n_ends = m.sb("n_ends", [1, ST])
        HG = 2
        wqT = m.sb("wqT", [P, 2, HG, C])
        wvT = xT[:, 0, :].rearrange("p (h x) -> p h x", h=H)
        wkT = xT[:, 1, 0:H * LORA].rearrange("p (h x) -> p h x", h=H)
        rope_loaded, wk_loaded, kv_loaded, zero_sb = (m.sem(n) for n in ("rope_loaded", "wk_loaded", "kv_loaded", "zero_sb"))
        wq_loaded = [m.sem(f"wq_loaded{s}") for s in range(2)]
        vo_raw = m.sb("vo_raw", [P, 2, C])
        a_mm, a_sb, vo_mm, vo_sb, vo_lo_sb = (m.sem(n) for n in ("a_mm", "a_sb", "vo_mm", "vo_sb", "vo_lo_sb"))
        place_sb, dve_sb, count_mm, hot_sb, lo_sb, slot_mm = (
            m.sem(n) for n in ("place_sb", "dve_sb", "count_mm", "hot_sb", "lo_sb", "slot_mm"))
        expo_sb, shifted_sb, chosen_sb, spread_sb, lo4_sb = (
            m.sem(n) for n in ("expo_sb", "shifted_sb", "chosen_sb", "spread_sb", "lo4_sb"))
        rank_ps = bank[:, 1, 0:N]
        tally_ps = bank[:, 2, 0:N]
        slot_ps = bank[:, 3, 0:3 * WIDTH_HOT]
        by_e = lambda a: a.rearrange("p (t e) -> p t e", e=E)
        over_e = lambda a: a.unsqueeze(2).to_broadcast([P, NT, E])

        with nc.Block() as block:
            @block.sync
            def _(sp):
                kvT = wkvbT_in.rearrange("(h x) l -> x h l", x=NOPE + VD)
                nopeT = wqT_in.rearrange("(h x) c -> x h c", x=QH)
                for g in range(2):
                    sp.dma_start(wqT[:, g], nopeT[0:NOPE, g * HG:(g + 1) * HG]).then_inc(wq_loaded[g], 16)
                sp.dma_start(wkT, kvT[0:NOPE]).then_inc(wk_loaded, 16)
                sp.wait_ge(zero_sb, 1)
                for odd in range(2):
                    sp.dma_start(wvT.rearrange("p (n two) x -> p two n x", two=2)[:, odd, :, odd * LORA:(odd + 1) * LORA],
                                 kvT.rearrange("x (n two) l -> x two n l", two=2)[NOPE:NOPE + VD, odd]).then_inc(kv_loaded, 16)
                sp.dma_start(wo[:], wo_in.rearrange("(h v) c -> v h c", v=VD)).then_inc(kv_loaded, 16)
                for k in range(KC):
                    sp.dma_start(wqk[:, k].rearrange("p (h x) -> p h x", h=H)[:, :, LORA:2 * LORA],
                                 wq_in[k * P:(k + 1) * P, :].rearrange("p (h x) -> p h x", h=H)[:, :, NOPE:QH]
                                 ).then_inc(rope_loaded, 16)
                sp.dma_start(w_down[:].rearrange("p (e k n) -> p e k n", e=E, k=2),
                             down_in.rearrange("e (k p) n -> p e k n", p=IH)).then_inc(weights_loaded, 16)
                for g in range(2, H // HG):
                    sp.wait_ge(a_mm, g - 1)
                    sp.dma_start(wqT[:, g % 2], nopeT[0:NOPE, g * HG:(g + 1) * HG]).then_inc(wq_loaded[g % 2], 16)
                sp.wait_ge(rope_loaded, 16 * KC)
                sp.wait_ge(a_sb, H // HG)
                for k in range(KC):
                    sp.dma_start(wqk_rows.rearrange("n p k x -> p k n x")[:, k],
                                 wqk[:, k].rearrange("p (n x) -> p n x", x=2 * P)).then_inc(wqk_stored, 16)

            @block.tensor
            def _(pe):
                def fold_keys(g):
                    if g == 1:
                        pe.wait_ge(shifted_sb, 1)
                    pe.wait_ge(wk_loaded, 16)
                    pe.wait_ge(wq_loaded[g % 2], 16 * (g // 2 + 1))
                    if g >= 2:
                        pe.wait_ge(a_sb, g - 1)
                    for k in range(KC):
                        for i in range(HG):
                            mm = nc.tensor.matmul(bank[:, 4 + g % 2, (k * HG + i) * LORA:(k * HG + i + 1) * LORA],
                                                  wqT[:, g % 2, i, k * P:(k + 1) * P], wkT[:, g * HG + i, :],
                                                  start=True, stop=True)
                    mm.then_inc(a_mm, 1)

                def fold_values(n):
                    pe.wait_ge(kv_loaded, 16 * 3)
                    if n >= 2:
                        pe.wait_ge(vo_sb, n - 1)
                    for odd in range(2):
                        mm = nc.tensor.matmul(bank[:, 6 + n % 2, 0:C], wvT[:, 2 * n + odd, :], wo[:, 2 * n + odd, :],
                                              start=odd == 0, stop=odd == 1)
                    mm.then_inc(vo_mm, 1)

                pe.wait_ge(chosen_sb, 1)
                flat = chosen[:].rearrange("p t e -> p (t e)")
                nc.tensor.matmul(rank_ps, cst["before"], flat, start=True, stop=True)
                nc.tensor.matmul(tally_ps, ones[:, 0:P], flat, start=True, stop=True).then_inc(count_mm, 1)
                for n in range(NT * TOPK):
                    t, k = divmod(n, TOPK)
                    if t % 4 == 3:
                        pe.wait_ge(lo4_sb, t // 4 + 1)
                    else:
                        pe.wait_ge(lo_sb, n + 1 - t // 4 * TOPK)
                    pe.wait_ge(hot_sb, n + 1)
                    nc.tensor.matmul(slot_ps, is_lo[:, t % 2, k, :], is_hi[:, n % 4].rearrange("p a s -> p (a s)"),
                                     start=n == 0, stop=n == NT * TOPK - 1).then_inc(slot_mm, 1)
                    if n % 8 == 1:
                        fold_keys(n // 8)
                    if n % 8 == 5:
                        fold_values(n // 8)

            @block.scalar
            def _(act):
                act.wait_ge(shifted_sb, 1)
                nc.scalar.activation(expo[:], shifted[:], ACT.Exp).then_inc(expo_sb, 1)
                for g in range(H // HG):
                    act.wait_ge(a_mm, g + 1)
                    for k in range(KC):
                        ins = nc.scalar.copy(
                            wqk[:, k].rearrange("p (h x) -> p h x", h=H)[:, g * HG:(g + 1) * HG, 0:LORA],
                            bank[:, 4 + g % 2, k * HG * LORA:(k + 1) * HG * LORA].rearrange("p (h x) -> p h x", h=HG))
                    ins.then_inc(a_sb, 1)
                    act.wait_ge(vo_mm, g + 1)
                    if g >= 2:
                        act.wait_ge(vo_lo_sb, g - 1)
                    nc.scalar.copy(vo_raw[:, g % 2, :], bank[:, 6 + g % 2, 0:C])
                    nc.scalar.copy(vo[:, 0, g, :], bank[:, 6 + g % 2, 0:C]).then_inc(vo_sb, 1)

            @block.gpsimd
            def _(pool):
                nc.gpsimd.memset(wvT, 0.0).then_inc(zero_sb, 1)
                token = Count(spread_sb, pool)
                token.up(nc.gpsimd.iota(token1_i[:], pattern=[[P, NT]], base=1, channel_multiplier=1))
                token.settle()
                token.up(nc.gpsimd.tensor_copy(token1[:], token1_i[:]))
                pool.wait_ge(place_sb, 1)

                def values_low(n):
                    pool.wait_ge(vo_sb, n + 1)
                    nc.gpsimd.tensor_tensor(vo[:, 1, n, :], vo_raw[:, n % 2, :], vo[:, 0, n, :].bitcast(F32),
                                            ALU.subtract).then_inc(vo_lo_sb, 1)

                for t in range(NT):
                    if t % 2 == 0 and t >= 4:
                        values_low(t // 2 - 2)
                    if t % 4 == 3:
                        continue
                    if t >= 2:
                        pool.wait_ge(slot_mm, (t - 1) * TOPK)
                    for k in range(TOPK):
                        n = t * TOPK + k
                        nc.gpsimd.tensor_scalar(is_lo[:, t % 2, k, :], cst["iota"], lo[:, n:n + 1], None,
                                                ALU.is_equal).then_inc(lo_sb, 1)
                for n in range(PAIRS - 2, PAIRS):
                    values_low(n)

            @block.vector
            def _(dve):
                step = Count(dve_sb, dve)
                v = nc.vector
                step.up(v.memset(ones[:], 1.0))
                step.up(v.memset(ties_so_far[:, 0:1], 0.0))
                step.up(v.memset(earlier[:, 0, :], 0.0))
                dve.wait_ge(router_loaded, 32)
                step.up(v.tensor_tensor(logit[:], logit_ps, bias[:].unsqueeze(1).to_broadcast([P, NT, E]), ALU.add))
                step.settle()
                for t in range(NT):
                    step.up(v.max(top[:, t, :], logit[:, t, :]))
                step.settle()
                v.tensor_tensor(shifted[:], logit[:], over_e(top[:, :, 0]), ALU.subtract).then_inc(shifted_sb, 1)
                fourth = over_e(top[:, :, TOPK - 1])
                step.up(v.tensor_tensor(above[:], logit[:], fourth, ALU.is_gt))
                step.up(v.tensor_tensor(tie[:], logit[:], fourth, ALU.is_equal))
                step.settle()
                step.up(v.tensor_reduce(n_above[:], above[:], AX_X, ALU.add))
                step.up(v.tensor_tensor_scan(ties_so_far[:, 1:1 + N], ones[:], tie[:].rearrange("p t e -> p (t e)"), 0.0,
                                             ALU.mult, ALU.add))
                step.settle()
                step.up(v.tensor_scalar(room[:], n_above[:], -1.0, float(TOPK), ALU.mult, ALU.add))
                step.up(v.tensor_tensor(tie_rank[:], by_e(ties_so_far[:, 1:1 + N]), over_e(by_e(ties_so_far[:, 0:N])[:, :, 0]),
                                        ALU.subtract))
                step.settle()
                step.up(v.tensor_tensor(fits[:], tie_rank[:], over_e(room[:]), ALU.is_le))
                step.settle()
                step.up(v.tensor_tensor(picked[:], fits[:], tie[:], ALU.mult))
                step.settle()
                v.tensor_tensor(chosen[:], picked[:], above[:], ALU.add).then_inc(chosen_sb, 1)
                dve.wait_ge(chosen_sb, 1)
                dve.wait_ge(expo_sb, 1)
                step.up(v.tensor_tensor(fits[:], expo[:], chosen[:], ALU.mult))
                step.settle()
                step.up(v.tensor_reduce(total[:], fits[:], AX_X, ALU.add))
                step.settle()
                step.up(v.reciprocal(rtotal[:], total[:]))
                step.settle()
                step.up(v.tensor_tensor(weight[:], fits[:], over_e(rtotal[:]), ALU.mult))
                dve.wait_ge(count_mm, 1)
                for t in range(NT):
                    step.settle()
                    step.up(v.tensor_tensor(earlier[:, t + 1, :], tally_ps[:, t * E:(t + 1) * E], earlier[:, t, :], ALU.add))
                step.settle()
                step.up(v.tensor_scalar(up[:], earlier[:, NT, :], float(P - 1), None, ALU.add))
                step.settle()
                step.up(v.tensor_scalar(tiles_i[:], up[:], 7, None, ALU.arith_shift_right))
                step.settle()
                step.up(v.tensor_copy(tiles[:], tiles_i[:]))
                step.settle()
                step.up(v.tensor_tensor_scan(tiles_end[:], ones[:, 0:E], tiles[:], 0.0, ALU.mult, ALU.add))
                step.settle()
                step.up(v.tensor_tensor(start[:], tiles_end[:], tiles[:], ALU.subtract))
                step.settle()
                step.up(v.tensor_scalar(start[:], start[:], float(P), 1.0, ALU.mult, ALU.add))
                step.up(v.tensor_tensor(place_a[:], by_e(rank_ps), earlier[:, 0:NT, :], ALU.add))
                step.settle()
                step.up(v.tensor_tensor(place_b[:], place_a[:], start[:].unsqueeze(1).to_broadcast([P, NT, E]), ALU.add))
                step.settle()
                step.up(v.tensor_tensor(key[:], place_b[:], chosen[:], ALU.mult))
                step.settle()
                for t in range(NT):
                    step.up(v.max(key4[:, t, :], key[:, t, :]))
                step.settle()
                step.up(v.tensor_scalar(place_i[:], key4[:, :, 0:TOPK], -1.0, None, ALU.add))
                step.settle()
                step.up(v.tensor_scalar(lo_i[:], place_i[:], P - 1, None, ALU.bitwise_and))
                step.up(v.tensor_scalar(hi_i[:], place_i[:], 7, None, ALU.arith_shift_right))
                step.settle()
                v.tensor_copy(lo[:], lo_i[:].rearrange("p t k -> p (t k)")).then_inc(place_sb, 1)
                step.up(v.tensor_copy(hi[:], hi_i[:].rearrange("p t k -> p (t k)")))
                for k0 in range(0, TOPK, 2):
                    for k in (k0, k0 + 1):
                        step.up(v.tensor_tensor(match[:, k - k0], key[:], over_e(key4[:, :, k]), ALU.is_equal))
                    step.settle()
                    for k in (k0, k0 + 1):
                        step.up(v.tensor_tensor(match_w[:, k - k0], match[:, k - k0], weight[:], ALU.mult))
                    step.settle()
                    for k in (k0, k0 + 1):
                        step.up(v.tensor_reduce(held[:, 1, :, k], match_w[:, k - k0], AX_X, ALU.add))
                    step.settle()
                for t0, n in ((0, HALF), (HALF, ST - HALF)):
                    step.up(v.tensor_tensor(ends[:, 0:n], cst["iota"][0:1, t0:t0 + n].unsqueeze(2).to_broadcast([1, n, E]),
                                            tiles_end[0:1, :].unsqueeze(1).to_broadcast([1, n, E]), ALU.is_ge))
                    step.settle()
                    step.up(v.tensor_reduce(n_ends[:, t0:t0 + n], ends[:, 0:n], AX_X, ALU.add))
                    step.settle()
                step.up(v.tensor_scalar(tile_expert[:], n_ends[:], float(E - 1), None, ALU.min))
                dve.wait_ge(spread_sb, 2)
                step.up(v.tensor_copy(held[:, 0], token1[:].unsqueeze(2).to_broadcast([P, NT, TOPK])))
                step.up(v.tensor_copy(weight_hi[:], held[:, 1]))
                step.settle()
                step.up(v.tensor_tensor(held[:, 2], held[:, 1], weight_hi[:].bitcast(F32), ALU.subtract))
                step.settle()
                for n in range(NT * TOPK):
                    t, k = divmod(n, TOPK)
                    if t % 4 == 3 and k == 0:
                        dve.wait_ge(slot_mm, (t - 1) * TOPK)
                        v.tensor_tensor(is_lo[:, t % 2], cst["iota"].unsqueeze(1).to_broadcast([P, TOPK, P]),
                                        lo[:, n:n + TOPK].unsqueeze(2).to_broadcast([P, TOPK, P]),
                                        ALU.is_equal).then_inc(lo4_sb, 1)
                    if n >= 4:
                        dve.wait_ge(slot_mm, n - 3)
                    v.scalar_tensor_tensor(is_hi[:, n % 4],
                                           cst["iota"][:, 0:WIDTH_HOT].unsqueeze(1).to_broadcast([P, 3, WIDTH_HOT]),
                                           hi[:, n:n + 1], held[:, :, t, k].unsqueeze(2).to_broadcast([P, 3, WIDTH_HOT]),
                                           ALU.is_equal, ALU.mult).then_inc(hot_sb, 1)
                dve.wait_ge(slot_mm, NT * TOPK)
                slots = slot_ps.rearrange("p (a s) -> p a s", a=3)[:, :, 0:ST]
                step.up(v.tensor_copy(slot_w_hi[:], slots[:, 1]))
                step.settle()
                step.up(v.tensor_tensor(slot_w[:], slots[:, 2], slot_w_hi[:], ALU.add))
                step.up(v.tensor_scalar(slot_f[:], slots[:, 0], -1.0, None, ALU.add))
                step.up(v.tensor_scalar(empty[:], slots[:, 0], 0.5, None, ALU.is_lt))
                step.up(v.tensor_scalar(far[:], cst["row"], float(FAR + 1), None, ALU.add))
                step.settle()
                step.up(v.tensor_scalar(slot_row[:], slot_f[:], 0.0, None, ALU.max))
                step.up(v.tensor_scalar(spare[:], empty[:], far[:, 0:1], None, ALU.mult))
                step.settle()
                step.up(v.tensor_tensor(slot_far[:], slot_f[:], spare[:], ALU.add))


def phase_experts(nc, bank, cst, w_gu, w_down, weights_loaded, weights_need, zeroed, rows_stored, x_rows, sums,
                  slot_row, slot_far, slot_w, tile_expert):
    AHEAD = 3
    with Memory(nc, "moe") as m:
        row_at = m.sb("row_at", [P, AHEAD + 1], I32)
        far_at = m.sb("far_at", [P, 2], I32)
        xg = m.sb("xg", [P, AHEAD + 1, C])
        xgT = m.sb("xgT", [P, 2, KC, P])
        gate = m.sb("gate", [P, 2, I])
        hid = m.sb("hid", [P, 2, I])
        hidT = m.sb("hidT", [IH, 2, 2, P])
        y = m.sb("y", [P, 2, C])
        names = ("row_sb", "xT_mm", "xT_sb", "gu_mm", "gate_sb", "hid_sb", "hidT_mm", "hidT_sb", "y_mm", "y_sb", "far_sb")
        row_sb, xT_mm, xT_sb, gu_mm, gate_sb, hid_sb, hidT_mm, hidT_sb, y_mm, y_sb, far_sb = (m.sem(n) for n in names)
        go = m.sem("go")
        gathered = [m.sem(f"gathered{s}") for s in range(AHEAD + 1)]
        added = [m.sem(f"added{s}") for s in range(2)]
        xT_ps = [bank[:, s, 0:KC * P] for s in range(2)]
        gu_ps = [bank[:, 2 + s, 0:2 * I] for s in range(2)]
        hidT_ps = [bank[0:IH, 4 + s, 0:2 * P] for s in range(2)]
        y_ps = [bank[:, 6 + s, 0:C] for s in range(2)]
        ST = SLOT_TILES
        FIRST = 4
        ROUND = 12
        LAST = FIRST + (ST - FIRST) // ROUND * ROUND

        def run(engine, step):
            for r in range(FIRST):
                step(0, r)
            with engine.Fori(0, (ST - FIRST) // ROUND) as n:
                for i in range(ROUND):
                    step(n * (ROUND // 2), FIRST + i)
            for r in range(LAST, ST):
                step(0, r)

        def wait(engine, sem, u, r, more):
            if r + more > 0:
                engine.wait_ge(sem, u * 2 + (r + more))

        def wait_dma(engine, sems, u, r, more):
            n = len(sems)
            if r // n + more > 0:
                engine.wait_ge(sems[r % n], u * (32 // n) + 16 * (r // n + more))

        with nc.Block() as block:
            @block.gpsimd
            def _(pool):
                last_row, last_far = pool.to_reg(T - 1), pool.to_reg(FAR + P - 1)

                def gather(u, r):
                    s = r % (AHEAD + 1)
                    wait(pool, xT_mm, u, r, -AHEAD)
                    nc.gpsimd.tensor_copy(row_at[:, s:s + 1], slot_row[:, bass.ds(u * 2 + r, 1)]).then_inc(row_sb, 1)
                    wait(pool, row_sb, u, r, 1)
                    pool.sem_inc(go, 1)
                    nc.gpsimd.indirect_dma_start(xg[:, s, :], None, x_rows,
                                                 bass.IndirectOffsetOnAxis(row_at[:, s:s + 1], 0),
                                                 bounds_check=last_row).then_inc(gathered[s], 16)

                def scatter(u, r):
                    s = r % 2
                    wait_dma(pool, added, u, r, 0)
                    nc.gpsimd.tensor_copy(far_at[:, s:s + 1], slot_far[:, bass.ds(u * 2 + r, 1)]).then_inc(far_sb, 1)
                    wait(pool, far_sb, u, r, 1)
                    wait(pool, y_sb, u, r, 1)
                    pool.sem_inc(go, 1)
                    nc.gpsimd.indirect_dma_start(sums[s], bass.IndirectOffsetOnAxis(far_at[:, s:s + 1], 0), y[:, s, :], None,
                                                 bounds_check=last_far, compute_op=ALU.add).then_inc(added[s], 16)

                def step(u, r):
                    if r + AHEAD < ST:
                        gather(u, r + AHEAD)
                    if r >= 1:
                        scatter(u, r - 1)

                pool.wait_ge(rows_stored, 16 * 2 * NCH)
                pool.wait_ge(zeroed, 16 * (FAR // P + 2))
                for r in range(AHEAD):
                    gather(0, r)
                run(pool, step)
                scatter(0, ST - 1)
                for s in range(2):
                    pool.wait_ge(added[s], 16 * len(range(s, ST, 2)))

            @block.tensor
            def _(pe):
                def turn_x(u, r):
                    s = r % 2
                    wait_dma(pe, gathered, u, r, 1)
                    wait(pe, xT_sb, u, r, -1)
                    for k in range(KC):
                        mm = nc.tensor.transpose(xT_ps[s][:, k * P:(k + 1) * P], xg[:, r % (AHEAD + 1), k * P:(k + 1) * P],
                                                 cst["ident"])
                    mm.then_inc(xT_mm, 1)

                def expert_of(u, r):
                    return pe.value_load(tile_expert[0:1, bass.ds(u * 2 + r, 1)], min_val=0, max_val=E - 1)

                def gate_up(u, r, e, k):
                    s = r % 2
                    if k == 0:
                        wait(pe, xT_sb, u, r, 1)
                        wait(pe, hid_sb, u, r, -1)
                    mm = nc.tensor.matmul(gu_ps[s], xgT[:, s, k, :], w_gu[:, bass.ds(e * (KC * 2 * I) + k * 2 * I, 2 * I)],
                                          start=k == 0, stop=k == KC - 1)
                    if k == KC - 1:
                        mm.then_inc(gu_mm, 1)

                def turn_hid(u, r):
                    s = r % 2
                    wait(pe, hid_sb, u, r, 1)
                    wait(pe, hidT_sb, u, r, -1)
                    for k in range(2):
                        mm = nc.tensor.transpose(hidT_ps[s][:, k * P:(k + 1) * P], hid[:, s, k * IH:(k + 1) * IH],
                                                 cst["ident"])
                    mm.then_inc(hidT_mm, 1)

                def down(u, r, e):
                    s = r % 2
                    wait(pe, hidT_sb, u, r, 1)
                    wait(pe, y_sb, u, r, -1)
                    for k in range(2):
                        mm = nc.tensor.matmul(y_ps[s], hidT[:, s, k, :], w_down[:, bass.ds(e * 2 * C + k * C, C)],
                                              start=k == 0, stop=k == 1)
                    mm.then_inc(y_mm, 1)

                expert = {}

                def step(u, r):
                    if r in (FIRST, LAST):
                        expert[r] = expert_of(u, r)
                    gate_up(u, r, expert[r], 0)
                    if r in (FIRST, LAST):
                        expert[r - 1] = expert_of(u, r - 1)
                    if r >= 1:
                        turn_hid(u, r - 1)
                    gate_up(u, r, expert[r], 1)
                    if r + 1 < ST:
                        turn_x(u, r + 1)
                        if r != FIRST + ROUND - 1:
                            expert[r + 1] = expert_of(u, r + 1)
                    if r >= 1:
                        down(u, r - 1, expert[r - 1])

                pe.wait_ge(weights_loaded, weights_need)
                turn_x(0, 0)
                expert[0] = expert_of(0, 0)
                run(pe, step)
                turn_hid(0, ST - 1)
                down(0, ST - 1, expert[ST - 1])

            @block.scalar
            def _(act):
                def copy_x(u, r):
                    s = r % 2
                    wait(act, xT_mm, u, r, 1)
                    wait(act, gu_mm, u, r, -1)
                    nc.scalar.copy(xgT[:, s].rearrange("p k m -> p (k m)"), xT_ps[s]).then_inc(xT_sb, 1)

                def silu(u, r):
                    s = r % 2
                    wait(act, gu_mm, u, r, 1)
                    wait(act, hid_sb, u, r, -1)
                    nc.scalar.activation(gate[:, s, :], gu_ps[s][:, 0:I], ACT.Silu).then_inc(gate_sb, 1)

                def copy_y(u, r):
                    s = r % 2
                    wait(act, y_mm, u, r, 1)
                    wait_dma(act, added, u, r, 0)
                    nc.scalar.copy(y[:, s, :], y_ps[s]).then_inc(y_sb, 1)

                def step(u, r):
                    silu(u, r)
                    if r + 1 < ST:
                        copy_x(u, r + 1)
                    if r >= 1:
                        copy_y(u, r - 1)

                copy_x(0, 0)
                run(act, step)
                copy_y(0, ST - 1)

            @block.vector
            def _(dve):
                def multiply(u, r):
                    s = r % 2
                    wait(dve, gate_sb, u, r, 1)
                    wait(dve, hidT_mm, u, r, -1)
                    nc.vector.scalar_tensor_tensor(hid[:, s, :], gu_ps[s][:, I:2 * I], slot_w[:, bass.ds(u * 2 + r, 1)],
                                                   gate[:, s, :], ALU.mult, ALU.mult).then_inc(hid_sb, 1)

                def copy_hid(u, r):
                    s = r % 2
                    wait(dve, hidT_mm, u, r, 1)
                    wait(dve, y_mm, u, r, -1)
                    nc.vector.tensor_copy(hidT[:, s].rearrange("p k m -> p (k m)"), hidT_ps[s]).then_inc(hidT_sb, 1)

                def step(u, r):
                    if r >= 1:
                        copy_hid(u, r - 1)
                    multiply(u, r)

                run(dve, step)
                copy_hid(0, ST - 1)


class Latent:

    GT = 4
    G = QT // GT

    def __init__(self, nc, m, bank, cst, power, xT, x_hl, k_hl, v_hl, w_raw, w_hl, first_loaded, wkva_in, scale_in,
                 wqk_rows, wqk_stored, b):
        self.nc, self.cst, self.power, self.b = nc, cst, power, b
        self.x_hl, self.k_hl, self.v_hl = x_hl, k_hl, v_hl
        self.w_raw, self.w_hl, self.first_loaded = w_raw, w_hl, first_loaded
        self.wkva_in, self.scale_in, self.wqk_rows, self.wqk_stored = wkva_in, scale_in, wqk_rows, wqk_stored
        self.x_own = xT[:, :, b * S:(b + 1) * S]
        self.wkva = m.sb("wkva", [P, KC, P])
        self.scale = m.sb("scale", [P, LORA])
        self.raw = m.sb("raw", [P, QT, P])
        self.square = m.sb("square", [P, QT, LORA])
        self.meansq = m.sb("meansq", [P, QT])
        self.sumsq = m.sb("sumsq", [P, QT])
        self.rrms = m.sb("rrms", [P, QT])
        self.unit = m.sb("unit", [P, QT, LORA])
        self.rows = m.sb("rows", [P, QT, P])
        self.by_cos = m.sb("by_cos", [P, QT, ROPE])
        self.by_sin = m.sb("by_sin", [P, QT, ROPE])
        self.ones = m.sb("ones", [P, QT, LORA])
        (self.loaded, self.raw_mm, self.raw_sb, self.step_sb, self.meansq_sb, self.rrms_sb, self.rows_sb, self.turn_mm,
         self.k_sb, self.ones_sb, self.x_sb, self.v_sb) = (m.sem(n) for n in (
             "kv_loaded", "raw_mm", "raw_sb", "step_sb", "meansq_sb", "rrms_sb", "rows_sb", "turn_mm", "k_sb", "ones_sb",
             "x_sb", "v_sb"))
        self.raw_ps = [bank[:, n, :] for n in (6, 7)]
        self.turn_ps = [bank[:, n, :] for n in (4, 5)]

    def load(self, sp):
        sp.dma_start(self.wkva[:], self.wkva_in.rearrange("(k p) n -> p k n", p=P)).then_inc(self.loaded, 16)
        sp.dma_start(self.scale[:], self.scale_in.partition_broadcast(P)).then_inc(self.loaded, 16)
        sp.wait_ge(self.wqk_stored, 16 * KC)
        sp.dma_start(self.w_raw[:], self.wqk_rows[0]).then_inc(self.first_loaded, 16)

    def make_ones(self, pool):
        self.nc.gpsimd.memset(self.ones[:], 1.0).then_inc(self.ones_sb, 1)

    def rms(self, pool):
        pool.wait_ge(self.meansq_sb, 1)
        self.nc.gpsimd.tensor_tensor(self.rrms[:], self.meansq[:], self.power[:, 0:QT], ALU.pow).then_inc(self.rrms_sb, 1)

    def input_rest(self, engine, k):
        engine.wait_ge(self.x_sb, 1)
        engine.tensor_tensor(self.x_hl[:, 1, k], self.x_own[:, k], self.x_hl[:, 0, k].bitcast(F32), ALU.subtract)

    def project(self, pe):
        pe.wait_ge(self.loaded, 32)
        for t in range(QT):
            for k in range(KC):
                mm = self.nc.tensor.matmul(self.raw_ps[t // self.GT][:, t % self.GT * P:(t % self.GT + 1) * P],
                                           self.x_own[:, k, t * P:(t + 1) * P], self.wkva[:, k, :],
                                           start=k == 0, stop=k == KC - 1)
            if t % self.GT == self.GT - 1:
                mm.then_inc(self.raw_mm, 1)

    def turn(self, pe):
        pe.wait_ge(self.rows_sb, 2)
        for t in range(QT):
            mm = self.nc.tensor.transpose(self.turn_ps[t // self.GT][:, t % self.GT * P:(t % self.GT + 1) * P],
                                          self.rows[:, t, :], self.cst["ident"])
            if t % self.GT == self.GT - 1:
                mm.then_inc(self.turn_mm, 1)

    def highs(self, act):
        self.nc.scalar.copy(self.x_hl[:, 0], self.x_own).then_inc(self.x_sb, 1)
        act.wait_ge(self.ones_sb, 1)
        self.nc.scalar.copy(self.v_hl[:, 0, :, LORA:P], self.ones[:]).then_inc(self.v_sb, 1)

    def key_highs(self, act):
        for g in range(self.G):
            act.wait_ge(self.turn_mm, g + 1)
            self.nc.scalar.copy(self.k_hl[:, 0, g * WIDE:(g + 1) * WIDE], self.turn_ps[g]).then_inc(self.k_sb, 1)

    def finish_rows(self, dve):
        v, step = self.nc.vector, Count(self.step_sb, dve)
        self.step = step
        half = ROPE // 2
        raw, rows = self.raw, self.rows
        for g in range(self.G):
            dve.wait_ge(self.raw_mm, g + 1)
            v.tensor_copy(raw[:, g * self.GT:(g + 1) * self.GT, :], self.raw_ps[g].rearrange("p (t n) -> p t n", n=P)
                          ).then_inc(self.raw_sb, 1)
        dve.wait_ge(self.raw_sb, self.G)
        step.up(v.tensor_tensor(self.square[:], raw[:, :, 0:LORA], raw[:, :, 0:LORA], ALU.mult))
        seq = lambda n: self.cst[n].rearrange("p (t x) -> p t x", x=ROPE)
        own = raw[:, :, LORA:P]
        step.settle()
        step.up(v.tensor_reduce(self.sumsq[:], self.square[:], AX_X, ALU.add))
        step.settle()
        v.tensor_scalar(self.meansq[:], self.sumsq[:], 1.0 / LORA, EPS_RMS, ALU.mult, ALU.add).then_inc(self.meansq_sb, 1)
        step.up(v.tensor_tensor(self.by_cos[:], own, seq("cos"), ALU.mult))
        for h in range(2):
            step.up(v.tensor_tensor(self.by_sin[:, :, h * half:(h + 1) * half], own[:, :, (1 - h) * half:(2 - h) * half],
                                    seq("sin")[:, :, h * half:(h + 1) * half], ALU.mult))
        step.settle()
        step.up(v.tensor_tensor(rows[:, :, LORA:P], self.by_cos[:], self.by_sin[:], ALU.add))
        dve.wait_ge(self.rrms_sb, 1)
        dve.wait_ge(self.loaded, 32)
        step.up(v.tensor_tensor(self.unit[:], raw[:, :, 0:LORA], self.rrms[:].unsqueeze(2).to_broadcast([P, QT, LORA]),
                                ALU.mult))
        step.settle()
        v.tensor_tensor(rows[:, :, 0:LORA], self.unit[:], self.scale[:].unsqueeze(1).to_broadcast([P, QT, LORA]),
                        ALU.mult).then_inc(self.rows_sb, 2)
        dve.wait_ge(self.rows_sb, 2)
        v_hl = self.v_hl
        step.up(v.tensor_copy(v_hl[:, 0, :, 0:LORA], rows[:, :, 0:LORA]))
        dve.wait_ge(self.v_sb, 1)
        step.up(v.tensor_tensor(v_hl[:, 1, :, LORA:P], self.ones[:], v_hl[:, 0, :, LORA:P].bitcast(F32), ALU.subtract))
        step.settle()
        step.up(v.tensor_tensor(v_hl[:, 1, :, 0:LORA], rows[:, :, 0:LORA], v_hl[:, 0, :, 0:LORA].bitcast(F32), ALU.subtract))

    def weights(self, dve):
        dve.wait_ge(self.first_loaded, 16 * (self.b + 1))
        self.step.up(self.nc.vector.tensor_copy(self.w_hl[:, 0], self.w_raw[:]))
        self.step.settle()
        self.step.up(self.nc.vector.tensor_tensor(self.w_hl[:, 1], self.w_raw[:], self.w_hl[:, 0].bitcast(F32), ALU.subtract))

    def key_rest(self, dve):
        for g in range(self.G):
            dve.wait_ge(self.k_sb, g + 1)
            self.step.up(self.nc.vector.tensor_tensor(self.k_hl[:, 1, g * WIDE:(g + 1) * WIDE], self.turn_ps[g],
                                                      self.k_hl[:, 0, g * WIDE:(g + 1) * WIDE].bitcast(F32), ALU.subtract))


def phase_collect(nc, bank, cst, power, sums, z, x_tok, xT, latent_of):
    with Memory(nc, "collect") as m:
        odd = m.sb("odd", [P, NT, C])
        GT = 4
        G = NT // GT
        norm = LayerNorm(nc, m, z, x_tok, power, 0, NT, GT)
        loaded = [m.sem(f"loaded{g}") for g in range(G)]
        z_sb, xT_mm, xT_sb = (m.sem(n) for n in ("z_sb", "xT_mm", "xT_sb"))
        latent = latent_of(m, 0)
        OWN = S // WIDE
        with nc.Block() as block:
            def load(engine, dst, src):
                for g in range(G):
                    engine.dma_start(dst[:, g * GT:(g + 1) * GT, :],
                                     src[g * T // G:(g + 1) * T // G, :].rearrange("(t p) c -> p t c", p=P)
                                     ).then_inc(loaded[g], 16)

            @block.sync
            def _(sp):
                load(sp, z, sums[0])
                latent.load(sp)

            @block.gpsimd
            def _(pool):
                for g in range(G):
                    at = slice(g * GT, (g + 1) * GT)
                    pool.wait_ge(loaded[g], 32)
                    nc.gpsimd.tensor_tensor(z[:, at, :], z[:, at, :], odd[:, at, :], ALU.add).then_inc(z_sb, 1)
                    if g:
                        norm.deviations(pool, g - 1)
                norm.deviations(pool, G - 1)
                latent.make_ones(pool)
                latent.rms(pool)
                for k in range(KC):
                    latent.input_rest(pool, k)

            @block.vector
            def _(dve):
                for g in range(G):
                    dve.wait_ge(z_sb, g + 1)
                    norm.statistics(dve, g)
                    if g:
                        norm.normalise(dve, g - 1)
                norm.normalise(dve, G - 1)
                latent.finish_rows(dve)
                latent.weights(dve)
                latent.key_rest(dve)

            @block.tensor
            def _(pe):
                for g in range(G):
                    if g == OWN:
                        pe.wait_ge(xT_sb, OWN * KC)
                        latent.project(pe)
                    for k in range(KC):
                        n = g * KC + k
                        if n >= 4:
                            pe.wait_ge(xT_sb, n - 3)
                        for i in range(GT):
                            t = g * GT + i
                            pe.wait_ge(norm.x_sb, t + 1)
                            mm = nc.tensor.transpose(bank[:, n % 4, i * P:(i + 1) * P], x_tok[:, t, k * P:(k + 1) * P],
                                                     cst["ident"])
                        mm.then_inc(xT_mm, 1)
                latent.turn(pe)

            @block.scalar
            def _(act):
                load(act, odd, sums[1])
                for n in range(G * KC):
                    g, k = divmod(n, KC)
                    act.wait_ge(xT_mm, n + 1)
                    nc.scalar.copy(xT[:, k, g * WIDE:(g + 1) * WIDE], bank[:, n % 4, :]).then_inc(xT_sb, 1)
                act.wait_ge(xT_sb, OWN * KC)
                latent.highs(act)
                latent.key_highs(act)


def phase_attention(nc, name, bank, cst, bf, x_hl, wqk_rows, w_raw, w_hl, k_hl, v_hl, oT, last_den):
    with Memory(nc, name) as m:
        rows = m.sb("rows", [P, 2, 2, P])
        by_cos = m.sb("by_cos", [P, 2, 2, ROPE])
        by_sin = m.sb("by_sin", [P, 2, 2, ROPE])
        q_hl = [m.sb(f"q_hl{s}", [P, 2, 2, S], F32R) for s in range(2)]
        peak = m.sb("peak", [P, 2, 2, QT])
        whole = m.sb("whole", [P, 2, QT])
        minus = m.sb("minus", [P, 2, QT, P], BF16)
        prob = m.sb("prob", [P, 2, 2 * WIDE])
        prob_hi = m.sb("prob_hi", [P, 3, 2 * WIDE], F32R)
        prob_lo = m.sb("prob_lo", [P, 3, 2 * WIDE], F32R)
        den = [m.sb("den", [P, WIDE]), last_den]
        rden = m.sb("rden", [P, 2, P])
        (w_loaded, w_hi_sb, w_sb, q_mm, rows_sb, rope_sb, rot_sb, turn_mm, q_hi_sb, q_lo_sb, max_mm, peak_sb, whole_sb,
         minus_sb, s_mm, prob_sb, hi_sb, lo_sb, pv_mm, sums_sb, rden_sb, o_sb) = (m.sem(n) for n in (
             "w_loaded", "w_hi_sb", "w_sb", "q_mm", "rows_sb", "rope_sb", "rot_sb", "turn_mm", "q_hi_sb", "q_lo_sb",
             "max_mm", "peak_sb", "whole_sb", "minus_sb", "s_mm", "prob_sb", "hi_sb", "lo_sb", "pv_mm", "sums_sb",
             "rden_sb", "o_sb"))
        max_ps, pv_ps = [bank[:, n, :] for n in (4, 5)], bank[:, 6, :]
        q_ps, turn_ps = bank[:, 7, 0:2 * P], bank[:, 7, 2 * P:4 * P]
        first_q_ps, first_turn_ps = [bank[:, n, 0:2 * P] for n in (0, 1)], [bank[:, n, 0:2 * P] for n in (2, 3)]
        s_ps = [bank[:, 2 * s:2 * s + 2, :].rearrange("p a n -> p (a n)") for s in range(2)]

        pieces = []
        for i in range(QT):
            end = (i + 1) * P
            cut = 0 if end <= WIDE else WIDE - P if end == WIDE + P else WIDE
            if cut:
                pieces.append((i, 0, 0, cut, False))
            pieces.append((i, 1 if cut else 0, cut, end - cut, True))
        groups = [(qc, [(j, min(max(j * P, qc * WIDE), (qc + 1) * WIDE - 2 * P)) for j in (j0, j0 + 1)])
                  for qc in range(S // WIDE) for j0 in range(0, (qc + 1) * WIDE // P, 2)]
        NG, NP = len(groups), len(pieces)
        pieces_of = lambda i: [y for y in range(NP) if pieces[y][0] == i]
        LOW = 4
        CHUNKS = S // WIDE
        AHEAD = 2
        HEADS = 4
        ROUNDS = H // HEADS
        PIECES_AT = [(0, 1, 2), (3, 4), (5, 6), (7, 8), (9, 10), (11,)]
        QUARTERS = WIDE // P

        def span(group):
            qc, tiles = group
            end = (qc + 1) * WIDE
            a, z = WIDE - (end - tiles[0][1]), WIDE + end - tiles[1][1]
            return a, z, [(a, WIDE), (WIDE, z)]

        def by_head(engine, sem, u, r, k, more):
            engine.wait_ge(sem, u * (HEADS * k) + (r * k + more + 2 * k))

        def by_pair(engine, sem, u, r, k, more):
            engine.wait_ge(sem, u * (HEADS // 2 * k) + (r * k + more + 2 * k))

        def rounds(engine, step, peel_first=False):
            def steps(u, last):
                for r in range(HEADS):
                    for x in range(NG):
                        more = not (last and r == HEADS - 1)
                        step(u, r, x, more, PIECES_AT[x] if more else (), *made_at(r, x, last))

            if peel_first:
                steps(0, False)
            with engine.Fori(int(peel_first), ROUNDS - 1) as u:
                steps(u, False)
            steps(ROUNDS - 1, True)

        def is_round(u, n):
            return isinstance(u, int) and u == n

        def q_bank(u, r, t):
            return first_q_ps[t % 2] if is_round(u, 0) and r == 0 else q_ps

        def turn_bank(u, r, t):
            return first_turn_ps[t % 2] if is_round(u, 0) and r == 0 else turn_ps

        def made_at(r, x, last):
            ahead = r // 2 + 1 if r % 2 == 0 or x == 0 else r // 2 + 2
            t = x + 2 if r % 2 == 0 else {0: QT, 4: 0, 5: 1}.get(x)
            if t is None or last and ahead >= HEADS // 2:
                return None, None
            return (ahead, t) if t < QT else None, (ahead, t - 1) if t else None

        with nc.Block() as block:
            @block.sync
            def _(sp):
                def load(n, u, r):
                    by_pair(sp, w_sb, u, r, 1, -1)
                    sp.dma_start(w_raw[:], wqk_rows[n]).then_inc(w_loaded, 16)

                with sp.Fori(0, ROUNDS - 1) as u:
                    for r in (1, 2):
                        load(u * 2 + r, u, r)
                load(PAIRS - 1, ROUNDS - 1, 1)

            @block.tensor
            def _(pe):
                def queries(u, r, t):
                    by_pair(pe, w_sb, u, r, 1, 0)
                    if is_round(u, 0) and r == 0:
                        by_pair(pe, rows_sb, u, r, QT, t - 1)
                    else:
                        by_pair(pe, rows_sb, u, r, QT, t)
                        by_pair(pe, q_lo_sb, u, r, QT, max(t - 1, 0))
                    n = 0
                    for xs, ws in ((0, 0), (0, 1), (1, 0)):
                        for k in range(KC):
                            mm = nc.tensor.matmul(q_bank(u, r, t), x_hl[:, xs, k, t * P:(t + 1) * P], w_hl[:, ws, k, :],
                                                  start=n == 0, stop=n == 3 * KC - 1)
                            n += 1
                    mm.then_inc(q_mm, 1)

                def turn(u, r, t):
                    if is_round(u, 0) and r == 0:
                        by_pair(pe, rows_sb, u, r, QT, t + 1)
                        by_pair(pe, q_lo_sb, u, r, QT, t - 1)
                    else:
                        by_pair(pe, rows_sb, u, r, QT, min(t + 2, QT))
                        by_pair(pe, q_lo_sb, u, r, QT, t)
                    by_pair(pe, rot_sb, u, r, QT, t + 1)
                    for i in range(2):
                        mm = nc.tensor.transpose(turn_bank(u, r, t)[:, i * P:(i + 1) * P], rows[:, t % 2, i, :], cst["ident"])
                    mm.then_inc(turn_mm, 1)

                def max_piece(u, r, y):
                    i, _, k0, w, diagonal = pieces[y]
                    by_pair(pe, q_hi_sb, u, r // 2, QT, i + 1)
                    by_head(pe, peak_sb, u, r, NP, y - 1)
                    ps = max_ps[y % 2]
                    mm = nc.tensor.matmul(ps[:, 0:w], q_hl[r // 2 % 2][:, 0, r % 2, i * P:(i + 1) * P],
                                          k_hl[:, 0, k0:k0 + w], start=True, stop=not diagonal)
                    if diagonal:
                        mm = nc.tensor.matmul(ps[:, w - P:w], bf["late_q"], bf["ident"], start=False, stop=True)
                    mm.then_inc(max_mm, 1)

                def scores(u, r, x, half):
                    qc, tiles = groups[x]
                    (j, q0), (a, z) = tiles[half], span(groups[x])[2][half]
                    if half == 0:
                        by_pair(pe, q_lo_sb, u, r // 2, QT, QT)
                        by_head(pe, prob_sb, u, r, NG, x - 1)
                        by_head(pe, minus_sb, u, r, CHUNKS, 1 + qc)
                    ps, w = s_ps[x % 2][:, a:z], z - a
                    for n, (ks, qs) in enumerate(((0, 0), (0, 1), (1, 0))):
                        nc.tensor.matmul(ps, k_hl[:, ks, j * P:(j + 1) * P], q_hl[r // 2 % 2][:, qs, r % 2, q0:q0 + w],
                                         start=n == 0, stop=False)
                    if q0 <= j * P:
                        cols = (j + 1) * P - q0
                        nc.tensor.matmul(ps[:, 0:cols], bf["late_k"], bf["late_cols"][:, 2 * P - cols:2 * P],
                                         start=False, stop=False)
                    mm = nc.tensor.matmul(ps, bf["ones"], minus[:, r % 2].rearrange("p i m -> p (i m)")[:, q0:q0 + w],
                                          start=False, stop=True)
                    if half:
                        mm.then_inc(s_mm, 1)

                def values(u, r, x, half):
                    qc, tiles = groups[x]
                    (j, q0), (a, z) = tiles[half], span(groups[x])[2][half]
                    if half == 0:
                        by_head(pe, lo_sb, u, r, NG, x + 1)
                        if j == 0:
                            by_head(pe, sums_sb, u, r, CHUNKS, qc)
                    last = j == (qc + 1) * WIDE // P - 1
                    for n, (vs, part) in enumerate(((0, prob_hi), (1, prob_hi), (0, prob_lo))):
                        mm = nc.tensor.matmul(pv_ps[:, q0 - qc * WIDE:WIDE], v_hl[:, vs, j, :], part[:, x % 3, a:z],
                                              start=j == 0 and n == 0, stop=last and n == 2)
                    if half:
                        mm.then_inc(pv_mm, 1)

                def step(u, r, x, more, peak_pieces, made, turned):
                    ahead = (u, r, x + AHEAD) if x + AHEAD < NG else (u, r + 1, x + AHEAD - NG) if more else None
                    if ahead:
                        scores(*ahead, 0)
                    for y in peak_pieces[:1]:
                        max_piece(u, r + 1, y)
                    if made:
                        queries(u, *made)
                    if ahead:
                        scores(*ahead, 1)
                    for y in peak_pieces[2:]:
                        max_piece(u, r + 1, y - 1)
                    if turned:
                        turn(u, *turned)
                    values(u, r, x, 0)
                    for y in peak_pieces[1:][-1:]:
                        max_piece(u, r + 1, y)
                    values(u, r, x, 1)

                for t in range(QT + 2):
                    if t < QT:
                        queries(0, 0, t)
                    if 1 <= t <= QT:
                        turn(0, 0, t - 1)
                    if t == QT + 1:
                        scores(0, 0, 0, 0)
                        scores(0, 0, 0, 1)
                    for y in pieces_of(t - 2):
                        max_piece(0, 0, y)
                queries(0, 1, 0)
                queries(0, 1, 1)
                scores(0, 0, 1, 0)
                turn(0, 1, 0)
                scores(0, 0, 1, 1)
                rounds(pe, step)

            @block.scalar
            def _(act):
                def row(u, r, t):
                    by_pair(act, q_mm, u, r, QT, t + 1)
                    by_pair(act, turn_mm, u, r, QT, t - 1)
                    nc.scalar.copy(rows[:, t % 2].rearrange("p h m -> p (h m)"), q_bank(u, r, t)).then_inc(rows_sb, 1)

                def q_high(u, r, t):
                    by_pair(act, turn_mm, u, r, QT, t + 1)
                    if t == 0:
                        by_head(act, s_mm, u, 2 * (r - 1), NG, 0)
                    nc.scalar.copy(q_hl[r % 2][:, 0, :, t * P:(t + 1) * P],
                                   turn_bank(u, r, t).rearrange("p (h m) -> p h m", m=P)).then_inc(q_hi_sb, 1)

                def probs(u, r, x):
                    a, z, _ = span(groups[x])
                    by_head(act, s_mm, u, r, NG, x + 1)
                    by_head(act, lo_sb, u, r, NG, x - 1)
                    nc.scalar.activation(prob[:, x % 2, a:z], s_ps[x % 2][:, a:z], ACT.Exp,
                                         scale=SCALE).then_inc(prob_sb, 1)

                def highs(u, r, x):
                    a, z, _ = span(groups[x])
                    by_head(act, prob_sb, u, r, NG, x + 1)
                    by_head(act, pv_mm, u, r, NG, x - 2)
                    nc.scalar.copy(prob_hi[:, x % 3, a:z], prob[:, x % 2, a:z]).then_inc(hi_sb, 1)

                def sums(u, r, qc):
                    n = [y for y in range(NG) if groups[y][0] == qc][-1]
                    half = slice(r % 2 * LORA, (r % 2 + 1) * LORA)
                    by_head(act, pv_mm, u, r, NG, n + 1)
                    by_pair(act, o_sb, u, r // 2, CHUNKS * QUARTERS, (qc + 1 - CHUNKS) * QUARTERS)
                    nc.scalar.copy(den[qc][half, :], pv_ps[LORA:P])
                    nc.scalar.copy(oT[half, bass.ds(u * (HEADS // 2) + r // 2, 1), qc * WIDE:(qc + 1) * WIDE].rearrange(
                        "p a m -> p (a m)"), pv_ps[0:LORA]).then_inc(sums_sb, 1)

                def step(u, r, x, more, peak_pieces, made, turned):
                    if x == 2:
                        sums(u, r, 0)
                    if made:
                        row(u, *made)
                    ahead = (u, r, x + AHEAD) if x + AHEAD < NG else (u, r + 1, x + AHEAD - NG) if more else None
                    if ahead:
                        probs(*ahead)
                    if turned:
                        q_high(u, *turned)
                    if ahead:
                        highs(*ahead)
                    if x == NG - 1:
                        sums(u, r, 1)

                for sem, n in ((rows_sb, QT), (q_hi_sb, QT), (prob_sb, NG), (hi_sb, NG), (sums_sb, CHUNKS)):
                    act.sem_inc(sem, 2 * n)
                for t in range(QT):
                    row(0, 0, t)
                    if t:
                        q_high(0, 0, t - 1)
                q_high(0, 0, QT - 1)
                probs(0, 0, 0)
                highs(0, 0, 0)
                row(0, 1, 0)
                row(0, 1, 1)
                probs(0, 0, 1)
                q_high(0, 1, 0)
                highs(0, 0, 1)
                rounds(act, step)

            @block.gpsimd
            def _(pool):
                def rotated(u, r, t):
                    by_pair(pool, rope_sb, u, r, 3 * QT, 3 * (t + 1))
                    nc.gpsimd.tensor_tensor(rows[:, t % 2, :, LORA:P], by_cos[:, t % 2], by_sin[:, t % 2],
                                            ALU.add).then_inc(rot_sb, 1)

                def low(u, r, x):
                    a, z, _ = span(groups[x])
                    by_head(pool, hi_sb, u, r, NG, x + 1)
                    nc.gpsimd.tensor_tensor(prob_lo[:, x % 3, a:z], prob[:, x % 2, a:z],
                                            prob_hi[:, x % 3, a:z].bitcast(F32), ALU.subtract).then_inc(lo_sb, 1)

                def step(u, r, x, more, peak_pieces, made, turned):
                    if made:
                        rotated(u, *made)
                    if x + AHEAD < NG:
                        low(u, r, x + AHEAD)
                    elif more:
                        low(u, r + 1, x + AHEAD - NG)

                for sem, n in ((rot_sb, QT), (lo_sb, NG)):
                    pool.sem_inc(sem, 2 * n)
                for t in range(QT):
                    rotated(0, 0, t)
                low(0, 0, 0)
                rotated(0, 1, 0)
                rotated(0, 1, 1)
                low(0, 0, 1)
                rounds(pool, step)

            @block.vector
            def _(dve):
                def weights(u, r):
                    by_pair(dve, w_loaded, u, r, 16, 0)
                    by_pair(dve, q_mm, u, r, QT, 0)
                    nc.vector.tensor_copy(w_hl[:, 0], w_raw[:]).then_inc(w_hi_sb, 1)
                    by_pair(dve, w_hi_sb, u, r, 1, 0)
                    nc.vector.tensor_tensor(w_hl[:, 1], w_raw[:], w_hl[:, 0].bitcast(F32), ALU.subtract).then_inc(w_sb, 1)

                def rope(u, r, t):
                    half = ROPE // 2
                    own = rows[:, t % 2, :, LORA:P]
                    at = lambda name: cst[name][:, t * ROPE:(t + 1) * ROPE].unsqueeze(1)
                    by_pair(dve, rows_sb, u, r, QT, t + 1)
                    by_pair(dve, rot_sb, u, r, QT, t - 1)
                    nc.vector.tensor_tensor(by_cos[:, t % 2], own, at("cos").to_broadcast([P, 2, ROPE]),
                                            ALU.mult).then_inc(rope_sb, 1)
                    for h in range(2):
                        nc.vector.tensor_tensor(by_sin[:, t % 2, :, h * half:(h + 1) * half],
                                                own[:, :, (1 - h) * half:(2 - h) * half],
                                                at("sin")[:, :, h * half:(h + 1) * half].to_broadcast([P, 2, half]),
                                                ALU.mult).then_inc(rope_sb, 1)

                def q_low(u, r, t):
                    own = q_hl[r % 2][:, :, :, t * P:(t + 1) * P]
                    by_pair(dve, q_hi_sb, u, r, QT, t + 1)
                    nc.vector.tensor_tensor(own[:, 1], turn_bank(u, r, t).rearrange("p (h m) -> p h m", m=P),
                                            own[:, 0].bitcast(F32), ALU.subtract).then_inc(q_lo_sb, 1)

                def peaks(u, r, y):
                    i, n, _, w, _ = pieces[y]
                    by_head(dve, max_mm, u, r, NP, y + 1)
                    nc.vector.tensor_reduce(peak[:, r % 2, n, i:i + 1], max_ps[y % 2][:, 0:w], AX_X,
                                            ALU.max).then_inc(peak_sb, 1)

                def spread(u, r, qc):
                    n = [y for y in range(NP) if pieces[y][0] < LOW * (qc + 1)][-1]
                    by_head(dve, peak_sb, u, r, NP, n + 1)
                    at = slice(qc * LOW, (qc + 1) * LOW)
                    if qc:
                        nc.vector.tensor_tensor(whole[:, r % 2, at], peak[:, r % 2, 0, at], peak[:, r % 2, 1, at],
                                                ALU.max).then_inc(whole_sb, 1)
                    else:
                        nc.vector.tensor_copy(whole[:, r % 2, at], peak[:, r % 2, 0, at]).then_inc(whole_sb, 1)
                    by_head(dve, whole_sb, u, r, CHUNKS, qc + 1)
                    by_head(dve, s_mm, u, r, NG, -NG)
                    nc.vector.scalar_tensor_tensor(minus[:, r % 2, at, :],
                                                   bf["ident"].unsqueeze(1).to_broadcast([P, LOW, P]), -1.0,
                                                   whole[:, r % 2, at].unsqueeze(2).to_broadcast([P, LOW, P]),
                                                   ALU.mult, ALU.mult).then_inc(minus_sb, 1)

                def divide(u, r, qc, n):
                    k, done = CHUNKS * QUARTERS, qc * QUARTERS + n
                    a = qc * WIDE + n * P
                    own = oT[:, bass.ds(u * (HEADS // 2) + r, 1), a:a + P].rearrange("p a m -> p (a m)")
                    by_head(dve, sums_sb, u, 2 * r + 1, CHUNKS, qc + 1)
                    by_pair(dve, o_sb, u, r, k, done - 1)
                    nc.vector.reciprocal(rden[:, n % 2, :], den[qc][:, n * P:(n + 1) * P]).then_inc(rden_sb, 1)
                    by_pair(dve, rden_sb, u, r, k, done + 1)
                    nc.vector.tensor_tensor(own, own, rden[:, n % 2, :], ALU.mult).then_inc(o_sb, 1)

                def step(u, r, x, more, peak_pieces, made, turned):
                    for y in peak_pieces[:1]:
                        peaks(u, r + 1, y)
                    if made:
                        rope(u, *made)
                    for y in peak_pieces[2:]:
                        peaks(u, r + 1, y - 1)
                    if more and x == NG - 1:
                        spread(u, r + 1, 1)
                    if turned:
                        q_low(u, *turned)
                    for y in peak_pieces[1:][-1:]:
                        peaks(u, r + 1, y)
                    if more and x == 1:
                        spread(u, r + 1, 0)
                    if r % 2 and x == 1 and not is_round(u, ROUNDS - 1):
                        weights(u, r // 2 + 2)
                    if r % 2 and x >= 2:
                        divide(u, r // 2, 0, x - 2)
                    if r % 2 == 0 and x < QUARTERS and not (is_round(u, 0) and r == 0):
                        divide(u, r // 2 - 1, 1, x)

                for sem, n in ((w_sb, 1), (q_lo_sb, QT), (w_hi_sb, 1), (rope_sb, 3 * QT), (peak_sb, NP), (whole_sb, CHUNKS),
                               (minus_sb, CHUNKS), (rden_sb, CHUNKS * QUARTERS), (o_sb, CHUNKS * QUARTERS)):
                    dve.sem_inc(sem, 2 * n)
                for sem, n in ((w_loaded, 16), (q_mm, QT), (turn_mm, QT), (max_mm, NP), (s_mm, NG), (pv_mm, NG)):
                    dve.sem_inc(sem, 2 * n)
                for t in range(QT + 2):
                    if t < QT:
                        rope(0, 0, t)
                    if 1 <= t <= QT:
                        q_low(0, 0, t - 1)
                    if t == QT + 1:
                        weights(0, 1)
                    for y in pieces_of(t - 2):
                        peaks(0, 0, y)
                        if y == LOW - 1:
                            spread(0, 0, 0)
                spread(0, 0, 1)
                rope(0, 1, 0)
                rope(0, 1, 1)
                q_low(0, 1, 0)
                rounds(dve, step, peel_first=True)


def phase_output(nc, name, bank, cst, power, x_tok, oT, last_den, vo, b, latent_of=None, x_hl=None, quantised=None):
    with Memory(nc, name) as m:
        z = x_tok
        norm = LayerNorm(nc, m, z, x_tok, power, b * QT, QT, 2)
        y_mm, z_sb, x_mm, hi_sb, lo_sb = (m.sem(n) for n in ("y_mm", "z_sb", "x_mm", "hi_sb", "lo_sb"))
        GT = 4
        units = [(g, k) for g in range(NT // GT) for k in range(KC)] if x_hl is not None else []
        early = len(units) // B
        x_ps = [bank[:, 4 + n, :] for n in range(4)]
        latent = latent_of(m, b + 1) if latent_of else None
        y_ps = [bank[:, n, 0:C] for n in range(4)]
        o_hl = m.sb("o_hl", [P, 2, 2, PAIRS, P], F32R)
        o_hi_sb, o_lo_sb = m.sem("o_hi_sb"), m.sem("o_lo_sb")
        rden = m.sb("rden", [P, 2, P])
        rden_sb, divided = m.sem("rden_sb"), m.sem("divided")
        CT = WIDE // P
        PASSES = ((0, 0), (0, 1), (1, 0))
        with nc.Block() as block:
            @block.sync
            def _(sp):
                if latent:
                    latent.load(sp)
                if quantised:
                    quantised.load(sp)

            @block.tensor
            def _(pe):
                def turn(n):
                    g, k = units[n]
                    if n >= 4:
                        pe.wait_ge(lo_sb, n - 3)
                    for i in range(GT):
                        t = g * GT + i
                        if t >= QT:
                            pe.wait_ge(norm.x_sb, t - QT + 1)
                        mm = nc.tensor.transpose(x_ps[n % 4][:, i * P:(i + 1) * P], x_tok[:, t, k * P:(k + 1) * P],
                                                 cst["ident"])
                    mm.then_inc(x_mm, 1)

                if latent:
                    latent.project(pe)
                for n in range(early):
                    turn(n)
                for t in range(QT):
                    if latent and t == 3:
                        latent.turn(pe)
                    if t >= 4:
                        pe.wait_ge(z_sb, t - 3)
                    pe.wait_ge(o_hi_sb, t + 1)
                    for i, (os, vs) in enumerate(PASSES):
                        if os:
                            pe.wait_ge(o_lo_sb, t + 1)
                        for n in range(PAIRS):
                            mm = nc.tensor.matmul(y_ps[t % 4], o_hl[:, t % 2, os, n, :], vo[:, vs, n, :],
                                                  start=i == 0 and n == 0, stop=i == len(PASSES) - 1 and n == PAIRS - 1)
                    mm.then_inc(y_mm, 1)
                for n in range(early, len(units)):
                    turn(n)

            @block.scalar
            def _(act):
                def o_high(t):
                    if t >= 2:
                        act.wait_ge(y_mm, t - 1)
                    if t >= CT:
                        act.wait_ge(divided, t - CT + 1)
                    nc.scalar.copy(o_hl[:, t % 2, 0], oT[:, :, t * P:(t + 1) * P]).then_inc(o_hi_sb, 1)

                def high(n):
                    g, k = units[n]
                    act.wait_ge(x_mm, n + 1)
                    nc.scalar.copy(x_hl[:, 0, k, g * WIDE:(g + 1) * WIDE], x_ps[n % 4]).then_inc(hi_sb, 1)

                for t in range(2):
                    o_high(t)
                for n in range(early):
                    high(n)
                if latent:
                    latent.highs(act)
                for t in range(2, QT):
                    o_high(t)
                    if latent and t == 3:
                        latent.key_highs(act)
                for n in range(early, len(units)):
                    high(n)

            @block.gpsimd
            def _(pool):
                def o_low(t):
                    pool.wait_ge(o_hi_sb, t + 1)
                    nc.gpsimd.tensor_tensor(o_hl[:, t % 2, 1], oT[:, :, t * P:(t + 1) * P], o_hl[:, t % 2, 0].bitcast(F32),
                                            ALU.subtract).then_inc(o_lo_sb, 1)

                if latent:
                    latent.make_ones(pool)
                for t in range(2):
                    o_low(t)
                if latent:
                    latent.rms(pool)
                for t in range(2, QT):
                    o_low(t)
                    if t % 2:
                        norm.deviations(pool, (t - 3) // 2)
                norm.deviations(pool, norm.groups - 1)

            @block.vector
            def _(dve):
                def low(n):
                    g, k = units[n]
                    dve.wait_ge(hi_sb, n + 1)
                    at = slice(g * WIDE, (g + 1) * WIDE)
                    nc.vector.tensor_tensor(x_hl[:, 1, k, at], x_ps[n % 4], x_hl[:, 0, k, at].bitcast(F32),
                                            ALU.subtract).then_inc(lo_sb, 1)

                for n in range(CT):
                    if n >= 2:
                        dve.wait_ge(divided, n - 1)
                    own = oT[:, PAIRS - 1, WIDE + n * P:WIDE + (n + 1) * P]
                    nc.vector.reciprocal(rden[:, n % 2, :], last_den[:, n * P:(n + 1) * P]).then_inc(rden_sb, 1)
                    dve.wait_ge(rden_sb, n + 1)
                    nc.vector.tensor_tensor(own, own, rden[:, n % 2, :], ALU.mult).then_inc(divided, 1)
                if latent:
                    latent.finish_rows(dve)
                for n in range(early):
                    low(n)
                for t in range(QT):
                    if latent and t == 4:
                        latent.key_rest(dve)
                    if latent and t == 2:
                        latent.weights(dve)
                    if latent and t in (5, 6):
                        latent.input_rest(dve, t - 5)
                    dve.wait_ge(y_mm, t + 1)
                    nc.vector.tensor_tensor(z[:, b * QT + t, :], y_ps[t % 4], x_tok[:, b * QT + t, :],
                                            ALU.add).then_inc(z_sb, 1)
                    if quantised and t == 3:
                        quantised.shift(nc, dve)
                    if t % 2:
                        dve.wait_ge(z_sb, t + 1)
                        norm.statistics(dve, t // 2)
                        if t >= 2:
                            norm.normalise(dve, t // 2 - 1)
                norm.normalise(dve, QT // 2 - 1)
                for n in range(early, len(units)):
                    low(n)


class QuantisedWeights:

    def __init__(self, m, xT, gateT_in, upT_in, downT_in, s_gate_in, s_up_in, s_down_in):
        self.scale_ins = s_gate_in, s_up_in, s_down_in
        self.ins = gateT_in, upT_in, downT_in
        self.gate_up = xT.rearrange("p k t -> p (k t)")[:, 0:2 * KC * HID].rearrange("p (a k n) -> p a k n", a=2, k=KC
                                                                                     ).bitcast(I32)
        self.down = m.sb("raw_down", [P, len(HT), C], I32)
        self.w = m.sb("w", [P, 2, KC, HID], F32R)
        self.w_down = m.sb("w_down", [P, len(HT), C], F32R)
        self.s_gate = m.sb("s_gate", [P, len(HT)])
        self.s_up = m.sb("s_up", [P, len(HT)])
        self.s_down = m.sb("s_down", [P, C])
        self.loaded, self.w_sb, self.scales = m.sem("raw_loaded"), m.sem("w_sb"), m.sem("scales")

    def shift(self, nc, dve):
        dve.wait_ge(self.loaded, 16 * 6)
        whole = HID // P
        rest = HT[whole][1]
        for dst, src in ((self.w[:, 0], self.gate_up[:, 0]), (self.w[:, 1], self.gate_up[:, 1]),
                         (self.w_down[:, 0:whole, :], self.down[:, 0:whole, :]),
                         (self.w_down[0:rest, whole, :], self.down[0:rest, whole, :])):
            nc.vector.tensor_scalar(dst, src, -ZERO_POINT, None, ALU.add).then_inc(self.w_sb, 1)

    def load(self, sp):
        gateT_in, upT_in, downT_in = self.ins
        whole = HID // P * P
        for a, src in enumerate((gateT_in, upT_in)):
            for k in range(KC):
                sp.dma_start(self.gate_up[:, a, k, :], src[k * P:(k + 1) * P, :]).then_inc(self.loaded, 16)
        sp.dma_start(self.down[:, 0:HID // P, :], downT_in[0:whole, :].rearrange("(n p) c -> p n c", p=P)
                     ).then_inc(self.loaded, 16)
        sp.dma_start(self.down[0:HID - whole, HID // P, :], downT_in[whole:HID, :]).then_inc(self.loaded, 16)
        s_gate_in, s_up_in, s_down_in = self.scale_ins
        for vec, dst in ((s_gate_in, self.s_gate), (s_up_in, self.s_up)):
            for n, (h0, hw) in enumerate(HT):
                sp.dma_start(dst[0:hw, n:n + 1], vec[h0:h0 + hw].unsqueeze(1)).then_inc(self.scales, 16)
        sp.dma_start(self.s_down[:], s_down_in.partition_broadcast(P)).then_inc(self.scales, 16)


def phase_feed_forward(nc, bank, x_hl, x_tok, power, quantised, out):
    NHT = len(HT)
    with Memory(nc, "ffn") as m:
        w, down = quantised.w, quantised.w_down
        s_gate, s_up, s_down, scales = quantised.s_gate, quantised.s_up, quantised.s_down, quantised.scales
        gate = m.sb("gated", [P, 2, WIDE])
        hid = m.sb("hid", [P, 2, WIDE])
        hid_hl = m.sb("hid_hl", [P, 2, 2, NHT, WIDE], F32R)
        scaled = m.sb("scaled", [P, 2, C])
        z = x_tok
        norm = LayerNorm(nc, m, z, x_tok, power, 0, NT, 2)
        stored = m.sem("stored")
        gu_mm, gate_sb, hid_sb, hi_sb, lo_sb, y_mm, scaled_sb, z_sb = (
            m.sem(n) for n in ("gu_mm", "gate_sb", "hid_sb", "hi_sb", "lo_sb", "y_mm", "scaled_sb", "z_sb"))
        CT = WIDE // P
        FIRST_DOWN = 2
        norm_at = {ch * NHT + FIRST_DOWN + 2 * (i + 1): (ch - 1) * CT // 2 + i for ch in range(1, NCH) for i in range(CT // 2)}
        with nc.Block() as block:
            @block.sync
            def _(sp):
                for g in range(norm.groups):
                    sp.wait_ge(norm.x_sb, 2 * (g + 1))
                    at = slice(2 * g, 2 * (g + 1))
                    sp.dma_start(out.rearrange("(t p) c -> p t c", p=P)[:, at, :], x_tok[:, at, :]).then_inc(stored, 16)
                sp.wait_ge(stored, 16 * norm.groups)

            @block.tensor
            def _(pe):
                def gate_up(ch, n):
                    h0, hw = HT[n]
                    x = ch * NHT + n
                    if x >= 2:
                        pe.wait_ge(hid_sb, x - 1)
                    for a in range(2):
                        for i in range(2 * KC):
                            part, k = divmod(i, KC)
                            mm = nc.tensor.matmul(bank[0:hw, 2 * (x % 2) + a, :], w[:, a, k, h0:h0 + hw],
                                                  x_hl[:, part, k, ch * WIDE:(ch + 1) * WIDE],
                                                  start=i == 0, stop=i == 2 * KC - 1)
                    mm.then_inc(gu_mm, 1)

                def down_of(t):
                    ch, i = divmod(t, CT)
                    if t >= 4:
                        pe.wait_ge(z_sb, t - 3)
                    for part in range(2):
                        for n, (h0, hw) in enumerate(HT):
                            if t % CT == 0:
                                pe.wait_ge(lo_sb if part else hi_sb, ch * NHT + n + 1)
                            mm = nc.tensor.matmul(bank[:, 4 + t % 4, 0:C], hid_hl[0:hw, part, ch % 2, n, i * P:(i + 1) * P],
                                                  down[0:hw, n, :], start=part == 0 and n == 0,
                                                  stop=part == 1 and n == NHT - 1)
                    mm.then_inc(y_mm, 1)

                pe.wait_ge(quantised.w_sb, 4)
                for ch in range(NCH):
                    for n in range(NHT):
                        gate_up(ch, n)
                        if ch and 0 <= n - FIRST_DOWN < CT:
                            down_of((ch - 1) * CT + n - FIRST_DOWN)
                for t in range(NT - CT, NT):
                    down_of(t)

            @block.scalar
            def _(act):
                def high(x):
                    n, ch = x % NHT, x // NHT
                    hw = HT[n][1]
                    act.wait_ge(hid_sb, x + 1)
                    if n == 0 and ch >= 2:
                        act.wait_ge(y_mm, (ch - 1) * CT)
                    nc.scalar.copy(hid_hl[0:hw, 0, ch % 2, n, :], hid[0:hw, x % 2, :]).then_inc(hi_sb, 1)

                act.wait_ge(scales, 16 * (2 * NHT + 1))
                for x in range(NCH * NHT):
                    n = x % NHT
                    hw = HT[n][1]
                    act.wait_ge(gu_mm, x + 1)
                    if x >= 2:
                        act.wait_ge(hid_sb, x - 1)
                    nc.scalar.activation(gate[0:hw, x % 2, :], bank[0:hw, 2 * (x % 2), :], ACT.Silu,
                                         scale=s_gate[0:hw, n:n + 1]).then_inc(gate_sb, 1)
                    if x:
                        high(x - 1)
                high(NCH * NHT - 1)

            @block.gpsimd
            def _(pool):
                for x in range(NCH * NHT):
                    n, ch = x % NHT, x // NHT
                    hw = HT[n][1]
                    if x in norm_at:
                        norm.deviations(pool, norm_at[x])
                    pool.wait_ge(hi_sb, x + 1)
                    nc.gpsimd.tensor_tensor(hid_hl[0:hw, 1, ch % 2, n, :], hid[0:hw, x % 2, :],
                                            hid_hl[0:hw, 0, ch % 2, n, :].bitcast(F32), ALU.subtract).then_inc(lo_sb, 1)
                for g in range((NT - CT) // 2 - 1, NT // 2):
                    norm.deviations(pool, g)

            @block.vector
            def _(dve):
                def sum_of(t):
                    dve.wait_ge(y_mm, t + 1)
                    nc.vector.tensor_tensor(scaled[:, t % 2, :], bank[:, 4 + t % 4, 0:C], s_down[:],
                                            ALU.mult).then_inc(scaled_sb, 1)
                    dve.wait_ge(scaled_sb, t + 1)
                    nc.vector.tensor_tensor(z[:, t, :], scaled[:, t % 2, :], x_tok[:, t, :], ALU.add).then_inc(z_sb, 1)
                    if t % 2:
                        if t >= 2:
                            norm.normalise(dve, t // 2 - 1)
                        dve.wait_ge(z_sb, t + 1)
                        norm.statistics(dve, t // 2)

                dve.wait_ge(scales, 16 * (2 * NHT + 1))
                for ch in range(NCH):
                    for n, (h0, hw) in enumerate(HT):
                        x = ch * NHT + n
                        dve.wait_ge(gate_sb, x + 1)
                        if x >= 2:
                            dve.wait_ge(lo_sb, x - 1)
                        nc.vector.scalar_tensor_tensor(hid[0:hw, x % 2, :], bank[0:hw, 2 * (x % 2) + 1, :],
                                                       s_up[0:hw, n:n + 1], gate[0:hw, x % 2, :], ALU.mult,
                                                       ALU.mult).then_inc(hid_sb, 1)
                        if ch and 0 <= n - FIRST_DOWN < CT:
                            sum_of((ch - 1) * CT + n - FIRST_DOWN)
                for t in range(NT - CT, NT):
                    sum_of(t)
                norm.normalise(dve, NT // 2 - 1)


def program(nc, x, xT_in, wqkvT, wprojT, bproj, routerT, rbias, gate, up, down, wqT, wq, wkva, wkvbT, wo, kvscale,
            gateT, s_gate, upT, s_up, downT, s_down, table, out):
    x_rows = nc.dram_tensor("x_rows", (T, C), F32).ap()
    wqk_rows = nc.dram_tensor("wqk_rows", (PAIRS, P, KC, 2 * P), F32).ap()
    sums = [nc.dram_tensor(f"sums{s}", (FAR + P, C), F32).ap() for s in range(2)]
    with Memory(nc, "all") as m:
        bank = m.ps("bank", [P, 8, WIDE])
        at, width = const_columns()
        cst_tile = m.sb("cst", [P, width])
        cst = {n: cst_tile[:, a:z] for n, (a, z) in at.items()}
        bft = m.sb("bf", [P, 6, P], BF16)
        bf = {n: bft[:, i, :] for i, n in enumerate(("ident", "ones", "late_q", "late_k"))}
        bf["late_cols"] = bft[:, 4:6, :].rearrange("p a m -> p (a m)")
        power = m.sb("power", [P, NT])
        x_tok = m.sb("x_tok", [P, NT, C])
        xT = m.sb("xT", [P, KC, T])
        vo = m.sb("vo", [P, 2, PAIRS, C], F32R)
        wqk_stored = m.sem("wqk_stored")
        with Memory(nc, "early") as me:
            z = me.sb("z", [P, NT, C])
            weights_loaded = me.sem("weights_loaded")
            zero = me.sb("zero", [P, C])
            router_w = me.sb("router_w", [P, KC, E])
            router_b = me.sb("router_b", [P, E])
            router_loaded, zeroed, rows_stored = (me.sem(n) for n in ("router_loaded", "zeroed", "rows_stored"))
            w_gu = me.sb("w_gu", [P, E * KC * 2 * I])
            logit_ps = bank[:, 5, 0:NT * E].rearrange("p (t e) -> p t e", e=E)
            phase_linear_attention(nc, bank, cst_tile, table, cst, bf, x_tok, xT, z, x, xT_in, wqkvT, wprojT, bproj,
                                   w_gu, weights_loaded, logit_ps, gate, up, zero, sums, power, x_rows, router_w, router_b,
                                   router_loaded, routerT, rbias, zeroed, rows_stored)
            slot_row = me.sb("slot_row", [P, SLOT_TILES], I32)
            slot_far = me.sb("slot_far", [P, SLOT_TILES], I32)
            slot_w = me.sb("slot_w", [P, SLOT_TILES])
            tile_expert = me.sb("tile_expert", [1, SLOT_TILES], I32)
            w_down = me.sb("w_down", [IH, E * 2 * C])
            phase_route(nc, bank, cst, xT, logit_ps, router_b, router_loaded, slot_row, slot_far, slot_w, tile_expert,
                        z[:].rearrange("p (k t) c -> p k (t c)", k=KC), x_tok, wqk_rows, vo, wqk_stored, wqT, wq, wkvbT, wo,
                        w_down, weights_loaded, down)
            phase_experts(nc, bank, cst, w_gu, w_down, weights_loaded, 16 * (2 * E + 1), zeroed, rows_stored, x_rows,
                          sums, slot_row, slot_far, slot_w, tile_expert)
        with Memory(nc, "late") as ml:
            oT = ml.sb("oT", [P, PAIRS, S])
            last_den = ml.sb("last_den", [P, WIDE])
            with Memory(nc, "sequence") as ms:
                x_hl = ms.sb("x_hl", [P, 2, KC, S], F32R)
                k_hl = ms.sb("k_hl", [P, 2, S], F32R)
                v_hl = ms.sb("v_hl", [P, 2, QT, P], F32R)
                w_raw = ms.sb("w_raw", [P, KC, 2 * P])
                w_hl = ms.sb("w_hl", [P, 2, KC, 2 * P], F32R)
                first_loaded = ms.sem("first_loaded")
                latent_of = lambda m, b: Latent(nc, m, bank, cst, power, xT, x_hl, k_hl, v_hl, w_raw, w_hl, first_loaded, wkva,
                                                kvscale, wqk_rows, wqk_stored, b)
                with Memory(nc, "middle") as mm:
                    phase_collect(nc, bank, cst, power, sums, mm.sb("z", [P, NT, C]), x_tok, xT, latent_of)
                for b in range(B):
                    phase_attention(nc, f"att{b}", bank, cst, bf, x_hl, wqk_rows, w_raw, w_hl, k_hl, v_hl, oT, last_den)
                    if b < B - 1:
                        phase_output(nc, f"out{b}", bank, cst, power, x_tok, oT, last_den, vo, b, latent_of)
            x_hl = ml.sb("x_hl", [P, 2, KC, T], F32R)
            quantised = QuantisedWeights(ml, xT, gateT, upT, downT, s_gate, s_up, s_down)
            phase_output(nc, f"out{B - 1}", bank, cst, power, x_tok, oT, last_den, vo, B - 1, None, x_hl, quantised)
            phase_feed_forward(nc, bank, x_hl, x_tok, power, quantised, out)


def kernel(**a):
    import concourse.bacc as bacc
    from concourse.bass_utils import run_bass_kernel_spmd

    x = np.asarray(a["L0_attn_x"]).reshape(T, C)
    turned = lambda n: np.asarray(a[n]).T
    ins = {
        "x": x, "xT": x.T, "wqkvT": turned("L0_attn_w_qkv"), "wprojT": turned("L0_attn_w_proj"), "bproj": a["L0_attn_b_proj"],
        "routerT": turned("L0_ffn_router_w"), "rbias": a["L0_ffn_expert_bias"], "gate": a["L0_ffn_gate_proj"],
        "up": a["L0_ffn_up_proj"], "down": a["L0_ffn_down_proj"], "wqT": turned("L1_attn_wq"), "wq": a["L1_attn_wq"],
        "wkva": a["L1_attn_wkv_a"], "wkvbT": turned("L1_attn_wkv_b"), "wo": a["L1_attn_wo"],
        "kvscale": a["L1_attn_kv_norm_scale"], "gateT": turned("L1_ffn_wq_gate"), "s_gate": a["L1_ffn_s_gate"],
        "upT": turned("L1_ffn_wq_up"), "s_up": a["L1_ffn_s_up"], "downT": turned("L1_ffn_wq_down"),
        "s_down": a["L1_ffn_s_down"], "table": const_table(),
    }
    nc = bacc.Bacc("TRN2", target_bir_lowering=False, num_devices=1)
    arrays, aps = {}, []
    for name, v in ins.items():
        v = np.ascontiguousarray(v)
        arrays[f"in_{name}"] = v
        aps.append(nc.dram_tensor(f"in_{name}", v.shape, mybir.dt.from_np(v.dtype), kind="ExternalInput").ap())
    out = nc.dram_tensor("out_x", (T, C), F32, kind="ExternalOutput").ap()
    program(nc, *aps, out)
    r = run_bass_kernel_spmd(nc, [arrays], core_ids=[0])
    return r.results[0]["out_x"].reshape(B, S, C)
```
